# Optimizing a Trainium2 kernel written in Bass

```python
import numpy as np
import jax
import jax.numpy as jnp

def _softmax(x, axis=-1):
    return jax.nn.softmax(x, axis=axis)

def _gelu(x):
    return jax.nn.gelu(x, approximate=True)

def _silu(x):
    return jax.nn.silu(x)

def _sigmoid(x):
    return jax.nn.sigmoid(x)

def _layernorm(x, axis=-1, eps=1e-05):
    m = jnp.mean(x, axis=axis, keepdims=True)
    v = jnp.var(x, axis=axis, keepdims=True)
    return (x - m) / jnp.sqrt(v + eps)

def _scatter_add(tgt, idx, src, axis=0):
    return tgt.at[idx].add(src)

def _segment_sum(src, seg, n):
    return jax.ops.segment_sum(src, seg, n)
kernel_name = 'mk_gnn_resnorm_d2_gnn_r32_b1bfe8'

def setup_inputs(seed: int=0):
    np.random.seed(seed)
    _w = jnp.asarray

    def _rec_inputs():
        import jax
        import jax.numpy as jnp
        _gk = jax.random.key(seed)
        x = -0.0004402 + 1 * jax.random.normal(jax.random.fold_in(_gk, 1), (3125, 16), jnp.float32)
        src = jax.random.randint(jax.random.fold_in(_gk, 2), (100000,), 0, 3125, jnp.int32)
        dst = jnp.minimum((3125 * jax.random.uniform(jax.random.fold_in(_gk, 3), (100000,)) ** 2.0).astype(jnp.int32), 99999)
        _o = jnp.argsort(dst, stable=True)
        src = src[_o]
        dst = dst[_o]
        edge_attr_16 = -3.57403e-05 + 0.999761 * jax.random.normal(jax.random.fold_in(_gk, 12), (100000, 16), jnp.float32)
        return (x, src, dst, edge_attr_16)
    x, src, dst, edge_attr_16 = _rec_inputs()

    def _L0_gnn_setup():
        import jax, jax.numpy as jnp
        import numpy as np
        N_NODES = 30000
        N_EDGES = 9375
        IN_FEATS = 16
        OUT_FEATS = 16
        EDGE_DIM = 16
        key = jax.random.key(seed)
        ks = jax.random.split(key, 8)
        feat = jax.random.normal(ks[0], (N_NODES, IN_FEATS), dtype=jnp.float32)
        efeat = jax.random.normal(ks[1], (N_EDGES, EDGE_DIM), dtype=jnp.float32)
        W_msg = jax.random.normal(ks[2], (EDGE_DIM, IN_FEATS * OUT_FEATS), dtype=jnp.float32) * 0.1
        b_msg = jnp.zeros((IN_FEATS * OUT_FEATS,), dtype=jnp.float32)
        W_attn = jax.random.normal(ks[3], (EDGE_DIM, IN_FEATS * OUT_FEATS), dtype=jnp.float32) * 0.1
        b_attn = jnp.zeros((IN_FEATS * OUT_FEATS,), dtype=jnp.float32)
        src = jax.random.randint(ks[4], (N_EDGES,), 0, N_NODES, dtype=jnp.int32)
        dst = jax.random.randint(ks[5], (N_EDGES,), 0, N_NODES, dtype=jnp.int32)
        return {'feat': feat, 'efeat': efeat, 'W_msg': W_msg, 'b_msg': b_msg, 'W_attn': W_attn, 'b_attn': b_attn, 'src': src, 'dst': dst}
    _L0_gnn_all = _L0_gnn_setup()
    _L0_gnn_in = {k: v for k, v in _L0_gnn_all.items() if k in ('W_msg', 'b_msg', 'W_attn', 'b_attn')}
    del _L0_gnn_all

    def _L1_gnn_setup():
        import jax, jax.numpy as jnp
        import numpy as np
        N_NODES = 6250
        N_EDGES = 100000
        F_IN = 16
        N_CLASSES = 16

        def _gin_conv(x, src, dst, eps, wa, ba, wb, bb, n_nodes):
            agg = jax.ops.segment_sum(x[src], dst, num_segments=n_nodes)
            h = (1.0 + eps) * x + agg
            h = jax.nn.relu(h @ wa + ba) @ wb + bb
            return h
        key = jax.random.key(seed)
        ks = jax.random.split(key, 8)
        s = 1.0 / np.sqrt(F_IN)
        return {'x': jax.random.normal(ks[0], (N_NODES, F_IN), dtype=jnp.float32), 'edge_index': jax.random.randint(ks[1], (2, N_EDGES), 0, N_NODES, dtype=jnp.int32), 'eps1': jnp.zeros((), dtype=jnp.float32), 'w1a': jax.random.normal(ks[2], (F_IN, 16), dtype=jnp.float32) * s, 'b1a': jnp.zeros((16,), dtype=jnp.float32), 'w1b': jax.random.normal(ks[3], (16, 16), dtype=jnp.float32) * 0.25, 'b1b': jnp.zeros((16,), dtype=jnp.float32), 'eps2': jnp.zeros((), dtype=jnp.float32), 'w2a': jax.random.normal(ks[4], (16, N_CLASSES), dtype=jnp.float32) * 0.25, 'b2a': jnp.zeros((N_CLASSES,), dtype=jnp.float32), 'w2b': jax.random.normal(ks[5], (N_CLASSES, N_CLASSES), dtype=jnp.float32) * 0.25, 'b2b': jnp.zeros((N_CLASSES,), dtype=jnp.float32)}
    _L1_gnn_all = _L1_gnn_setup()
    _L1_gnn_in = {k: v for k, v in _L1_gnn_all.items() if k in ('eps1', 'w1a', 'b1a', 'w1b', 'b1b', 'eps2', 'w2a', 'b2a', 'w2b', 'b2b')}
    del _L1_gnn_all
    return {'x': x, 'src': src, 'dst': dst, 'edge_attr_16': edge_attr_16, 'L0_gnn_W_msg': _L0_gnn_in['W_msg'], 'L0_gnn_b_msg': _L0_gnn_in['b_msg'], 'L0_gnn_W_attn': _L0_gnn_in['W_attn'], 'L0_gnn_b_attn': _L0_gnn_in['b_attn'], 'L1_gnn_eps1': _L1_gnn_in['eps1'], 'L1_gnn_w1a': _L1_gnn_in['w1a'], 'L1_gnn_b1a': _L1_gnn_in['b1a'], 'L1_gnn_w1b': _L1_gnn_in['w1b'], 'L1_gnn_b1b': _L1_gnn_in['b1b'], 'L1_gnn_eps2': _L1_gnn_in['eps2'], 'L1_gnn_w2a': _L1_gnn_in['w2a'], 'L1_gnn_b2a': _L1_gnn_in['b2a'], 'L1_gnn_w2b': _L1_gnn_in['w2b'], 'L1_gnn_b2b': _L1_gnn_in['b2b']}

def reference(x, src, dst, edge_attr_16, L0_gnn_W_msg, L0_gnn_b_msg, L0_gnn_W_attn, L0_gnn_b_attn, L1_gnn_eps1, L1_gnn_w1a, L1_gnn_b1a, L1_gnn_w1b, L1_gnn_b1b, L1_gnn_eps2, L1_gnn_w2a, L1_gnn_b2a, L1_gnn_w2b, L1_gnn_b2b):
    import jax
    import jax.numpy as jnp

    def _L0_gnn_ref(feat, efeat, W_msg, b_msg, W_attn, b_attn, src, dst):
        import jax, jax.numpy as jnp
        import numpy as np
        N_NODES = 30000
        N_EDGES = 9375
        IN_FEATS = 16
        OUT_FEATS = 16
        EDGE_DIM = 16
        N, in_f = feat.shape
        E = efeat.shape[0]
        w_m = (efeat @ W_msg + b_msg).reshape(E, in_f, -1)
        w_a = (efeat @ W_attn + b_attn).reshape(E, in_f, -1)
        h_src = feat[src][:, :, None]
        e1 = w_m * h_src
        e2 = w_a * h_src
        seg_max = jax.ops.segment_max(e2, dst, num_segments=N)
        ex = jnp.exp(e2 - seg_max[dst])
        denom = jax.ops.segment_sum(ex, dst, num_segments=N)
        attn = ex / denom[dst]
        ft = jax.ops.segment_sum(e1 * attn, dst, num_segments=N)
        return ft.sum(axis=1)

    def _L1_gnn_ref(x, edge_index, eps1, w1a, b1a, w1b, b1b, eps2, w2a, b2a, w2b, b2b):
        import jax, jax.numpy as jnp
        import numpy as np
        N_NODES = 6250
        N_EDGES = 100000
        F_IN = 16
        N_CLASSES = 16

        def _gin_conv(x, src, dst, eps, wa, ba, wb, bb, n_nodes):
            agg = jax.ops.segment_sum(x[src], dst, num_segments=n_nodes)
            h = (1.0 + eps) * x + agg
            h = jax.nn.relu(h @ wa + ba) @ wb + bb
            return h
        src, dst = (edge_index[0], edge_index[1])
        n = x.shape[0]
        h = jax.nn.relu(_gin_conv(x, src, dst, eps1, w1a, b1a, w1b, b1b, n))
        h = _gin_conv(h, src, dst, eps2, w2a, b2a, w2b, b2b, n)
        return jax.nn.log_softmax(h, axis=1)
    edge_index = jnp.stack([src, dst])
    x = _layernorm(x + _L0_gnn_ref(x, edge_attr_16, L0_gnn_W_msg, L0_gnn_b_msg, L0_gnn_W_attn, L0_gnn_b_attn, src, dst), axis=-1)
    x = _layernorm(x + _L1_gnn_ref(x, edge_index, L1_gnn_eps1, L1_gnn_w1a, L1_gnn_b1a, L1_gnn_w1b, L1_gnn_b1b, L1_gnn_eps2, L1_gnn_w2a, L1_gnn_b2a, L1_gnn_w2b, L1_gnn_b2b), axis=-1)
    return x

_drawn_inputs = setup_inputs


def setup_inputs(seed=0):
    import zlib

    import numpy as np

    out = dict(_drawn_inputs(seed))
    spreads = {'L0_gnn_b_msg': (0.0, 0.1),
     'L0_gnn_b_attn': (0.0, 0.1),
     'L1_gnn_b1a': (0.0, 0.8),
     'L1_gnn_b1b': (0.0, 0.549),
     'L1_gnn_b2a': (0.0, 2.0),
     'L1_gnn_b2b': (0.0, 2.0)}
    factors = {}
    for name, (base, spread) in spreads.items():
        noise = np.random.default_rng([zlib.crc32(name.encode()), seed]).standard_normal(out[name].shape)
        drawn = base * np.exp(spread * noise) if base else spread * noise
        out[name] = jnp.asarray(drawn.astype(out[name].dtype))
    for name, factor in factors.items():
        out[name] = (out[name] * factor).astype(out[name].dtype)
    return out
```

```python
from contextlib import ExitStack

import concourse.bass as bass
from concourse import mybir

F32 = mybir.dt.float32
BF16 = mybir.dt.bfloat16
FP16 = mybir.dt.float16
I32 = mybir.dt.int32
ALU = mybir.AluOpType
ACT = mybir.ActivationFunctionType
AX = mybir.AxisListType

P = 128
N = 3125
E = 100000
F = 16
C = F * F
NT = -(-N // P)
NP = NT * P
G = 8
GROUPS = (E + N * (G - 1)) // G
T = -(-GROUPS // (3 * P)) * 3
S = T * P
ROW = 102
KROWS = 100
SR = 256
SROWS = -(-E // SR)
STEPS = -(-(T + NT) // 3) * 3
WIN = 20
NW = NP // WIN
CW = WIN * NT
ET = -(-E // (2 * P)) * 2
BIG = 1.0e30
FAR = 3.0e38
FLAG = N
PREP = 8
PP = 125
PC = E // PP // PREP
EPS = 1e-5
BLOCKS = [(n0, min(512, NP - n0)) for n0 in range(0, NP, 512)]
NB = len(BLOCKS)
assert GROUPS <= S and PP * PC * PREP == E and NW % 2 == 0 and NW * WIN == NP


def ge(eng, sema, value):
    if not isinstance(value, int) or value > 0:
        eng.wait_ge(sema, value)


def program(nc, x, src, dst, ef, w_msg, b_msg, w_att, b_att, gin, out):
    with ExitStack() as ctx:
        def sem(name):
            return ctx.enter_context(nc.semaphore(name))

        def sb(name, shape, dt, at=ctx):
            return at.enter_context(nc.sbuf_tensor(name, shape, dt))

        def dram(name, shape, dt):
            return nc.dram_tensor(name, shape, dt).ap()

        edge_rows = dram("edge_rows", (E + G, ROW), BF16)
        x_table = dram("x_table", (FLAG + N, F), F32)
        dst_rows = dram("dst_rows", (SROWS, SR), I32)
        start_row_d = dram("start_row_d", (NP + 8,), F32)
        g0_row_d = dram("g0_row_d", (NP,), F32)
        slot_row_d = dram("slot_row_d", (NP,), F32)
        group_table = dram("group_table", (S, 4), F32)
        owner_d = dram("owner_d", (S + 1,), F32)
        fence_d = dram("fence_d", (S + 1,), BF16)
        group_sums = dram("group_sums", (T, P, 3 * C), F32)

        bank = [ctx.enter_context(nc.psum_tensor(f"bank{i}", [P, 512], F32)) for i in range(8)]
        turned = bank[4][:, :].bitcast(BF16)

        identf = sb("identf", [P, P], F32)
        identb = sb("identb", [P, P], BF16)
        iotaf = sb("iotaf", [P, P], F32)
        iota_key = sb("iota_key", [P, CW], FP16)
        iota_lo = sb("iota_lo", [P, P], FP16)
        ones_row = sb("ones_row", [1, P], F32)
        w500 = sb("w500", [P, NW], F32)
        wst = sb("wst", [KROWS, 2 * C], BF16)
        own_t = sb("own_t", [P, T], F32)
        est_i = sb("est_i", [P, T + 1], I32)
        empty = sb("empty", [P, T * G], I32)
        step_tile = sb("step_tile", [1, STEPS], I32)
        step_win = sb("step_win", [1, STEPS], I32)
        step_w128 = sb("step_w128", [P, STEPS], F32)
        win_pair = sb("win_pair", [1, NW + 1], I32)
        kb = sb("kb", [P, ET], F32)
        lo = sb("lo", [P, ET], BF16)

        setup = ExitStack()
        r_a = sb("r_a", [1, NP + 8], F32, setup)
        r_b = sb("r_b", [1, NP], F32, setup)
        r_c = sb("r_c", [1, NP], F32, setup)
        r_g = sb("r_g", [1, NP], F32, setup)
        r_i = sb("r_i", [1, NP], I32, setup)
        ef_in = sb("ef_in", [PP, 2, PC, F], F32, setup)
        resid = sb("resid", [PP, PC, F], F32, setup)
        rows = sb("rows", [PP, 2, PC, ROW], BF16, setup)
        src_i = sb("src_i", [PP, PREP, PC], I32, setup)
        node_id = sb("node_id", [P, NT], F32, setup)
        pads = sb("pads", [P, 512], F32, setup)
        ones_t = sb("ones_t", [PP, N * F // PP], F32, setup)
        pad_end = sb("pad_end", [1, 8], F32, setup)
        pads_i = sb("pads_i", [1, SR], I32, setup)
        found_r = sb("found_r", [P, NT], F32, setup)
        found_i = sb("found_i", [P, NT], I32, setup)
        start_nm = sb("start_nm", [P, NT], F32, setup)
        start_t = sb("start_t", [NT, P], F32, setup)
        search = ExitStack()
        rl_i = sb("rl_i", [1, SROWS], I32, search)
        rl_f = sb("rl_f", [1, SROWS], F32, search)
        rl_b = sb("rl_b", [P, SROWS], F32, search)
        less = sb("less", [P, NT, SROWS], BF16, search)
        srow = sb("srow", [P, NT, SR], I32, search)
        search.close()
        tables = ExitStack()
        nm4 = sb("nm4", [NT, 4, P], F32, tables)
        slot_i = sb("slot_i", [P, NT], I32, tables)
        pay = sb("pay", [P, NT, 4], F32, tables)
        gt = sb("gt", [T, P, 4], F32, tables)
        gs = sb("gs", [T, 4, P], F32, tables)
        carry = sb("carry", [T, 4], F32, tables)
        carry_r = sb("carry_r", [4, T + 1], F32, tables)
        carry_b = sb("carry_b", [T, 4], F32, tables)
        own_p = sb("own_p", [T, P], F32, tables)
        fence_r = sb("fence_r", [T, P], BF16, tables)
        fence_end = sb("fence_end", [1, 2], BF16, tables)
        minus_1 = sb("minus_1", [1, 2], F32, tables)
        gm = sb("gm", [P, 4, T], F32, tables)
        gid = sb("gid", [P, T], F32, tables)
        estf = sb("estf", [P, T], F32, tables)
        eslot = sb("eslot", [P, T, G], F32, tables)
        wf = sb("wf", [F + 1, 2 * C], F32, tables)
        wh = sb("wh", [F + 1, 3, 2 * C], BF16, tables)
        wflag = sb("wflag", [1, 2 * C], BF16, tables)
        kst = sb("kst", [1, STEPS], F32, tables)
        kcmp = sb("kcmp", [1, STEPS, NT], F32, tables)
        kwin = sb("kwin", [1, STEPS], F32, tables)
        kt_i = sb("kt_i", [1, NT], I32, tables)
        kt_f = sb("kt_f", [1, NT], F32, tables)
        er = sb("er", [P, 2, 7, P], I32, tables)
        eh = sb("eh", [P, 7, P], I32, tables)
        erf = sb("erf", [P, 2, 7, P], F32, tables)
        tables.close()
        setup.close()
        levels = ExitStack()
        mt = sb("mt", [P, 2, S], F32, levels)
        level1 = ExitStack()
        blk = sb("blk", [P, 3, G, ROW], BF16, level1)
        eft = sb("eft", [KROWS, 3, G, P], BF16, level1)
        hb = sb("hb", [P, 3, G, F], F32, level1)
        em = sb("em", [P, 3, G, 2, C], F32, level1)
        mx = sb("mx", [P, 2, C], F32, level1)
        spb = sb("spb", [P, 3, 3 * C], F32, level1)
        estc = sb("estc", [P, 3], I32, level1)
        idxi = sb("idxi", [P, 3, G], I32, level1)
        level1.close()
        scans = ExitStack()
        fence = sb("fence", [P, S + 1], BF16, scans)
        scans.close()
        level2 = ExitStack()
        acc = sb("acc", [P, NT + 1, 2 * C], F32, level2)
        md = sb("md", [P, 3, 3 * C], F32, level2)
        mc = sb("mc", [P, 3, 2, P], F32, level2)
        own_hot = sb("own_hot", [P, 3, P], F32, level2)
        x1 = sb("x1", [P, NT, F], F32, level2)
        hn = sb("hn", [P, NT, F], F32, level2)
        hn2 = sb("hn2", [P, NT, F], F32, level2)
        st1 = sb("st1", [P, NT], F32, level2)
        st2 = sb("st2", [P, NT], F32, level2)
        level2.close()
        levels.close()
        levelx = ExitStack()
        x_sb = sb("x_sb", [P, NT, F], F32, levelx)
        levelx.close()
        ginx = ExitStack()
        cnt = sb("cnt", [P, NT, NP], BF16, ginx)
        hot_lo = sb("hot_lo", [P, 2, P], BF16, ginx)
        hot_key = sb("hot_key", [P, 2, CW], BF16, ginx)
        zero_b = sb("zero_b", [P, CW], BF16, ginx)
        xs = sb("xs", [P, NT, 3, F], BF16, ginx)
        xr = sb("xr", [P, NT, F], F32, ginx)
        xt = sb("xt", [F, 512], F32, ginx)
        agg = sb("agg", [3 * F, 512], F32, ginx)
        ut = sb("ut", [F, 512], F32, ginx)
        gw = sb("gw", [3 * F, 2, F], F32, ginx)
        gwe = sb("gwe", [F, 2, F], F32, ginx)
        gb = sb("gb", [F, 2, F], F32, ginx)
        gba = sb("gba", [F, 2], F32, ginx)
        gbb = sb("gbb", [1, 2, F], F32, ginx)
        geps = sb("geps", [F, 2], F32, ginx)
        ginx.close()

        (const_ready, pool_step, dve_step, in_x, in_last, in_src, pad_out, last_ready, last_bcast, rows_found, search_in,
         start_ready, start_turned, start_kept, start_out, row_in, row_ready, row_out, nm_in, nm_turned, scatter_ready,
         scattered, table_in, carry_ready, carry_turned, carry_scanned, carry_back, owner_ready, owner_out, owner_in,
         fence_ready, fence_out, owners_turned, tables_ready, w_in, w_split, w_out, wk_ready, wk_bcast, er_in, er_ready,
         er_turned, fill_ready, rows_high, rows_resid, rows_mid, rows_done, x_out, pre_fill, flag_done, tr_done, eft_done,
         mm_done, p1, p2, p3, exp_done, p5, sum_done, mtr_done, mev_done, sev_done, fence_in, scan_done, mc_done,
         mtb_done, sub_done, wexp_done, wmul_done, own_done, node_ps, node_add, ln_var, ln_sd, x1_ready, hot_ready,
         hot_used, win_ps, win_ev, gin_in, xs_ready, conv_ps, conv_ev, xt_ps, xt_ev, hid_ps, hid_ev, map2, lsm_e, lsm_s,
         lsm_l, y_ready, out_done, zero_ready, x_zero) = [sem(n) for n in (
             "const_ready pool_step dve_step in_x in_last in_src pad_out last_ready last_bcast rows_found search_in "
             "start_ready start_turned start_kept start_out row_in row_ready row_out nm_in nm_turned scatter_ready "
             "scattered table_in carry_ready carry_turned carry_scanned carry_back owner_ready owner_out owner_in "
             "fence_ready fence_out owners_turned tables_ready w_in w_split w_out wk_ready wk_bcast er_in er_ready "
             "er_turned fill_ready rows_high rows_resid rows_mid rows_done x_out pre_fill flag_done tr_done eft_done "
             "mm_done p1 p2 p3 exp_done p5 sum_done mtr_done mev_done sev_done fence_in scan_done mc_done "
             "mtb_done sub_done wexp_done wmul_done own_done node_ps node_add ln_var ln_sd x1_ready hot_ready "
             "hot_used win_ps win_ev gin_in xs_ready conv_ps conv_ev xt_ps xt_ev hid_ps hid_ev map2 lsm_e lsm_s "
             "lsm_l y_ready out_done zero_ready x_zero").split()]
        ef_ld = [sem(f"ef_ld{i}") for i in range(2)]
        rows_out = [sem(f"rows_out{i}") for i in range(2)]
        blk_in = [sem(f"blk_in{i}") for i in range(3)]
        h_in = [sem(f"h_in{i}") for i in range(3)]
        spill_out = [sem(f"spill_out{i}") for i in range(3)]
        md_in = [sem(f"md_in{i}") for i in range(3)]
        block = ctx.enter_context(nc.Block())

        @block.sync
        def _(sp):
            sp.wait_ge(const_ready, 4)
            with nc.allow_non_contiguous_dma(reason="the last destination of each search row"):
                sp.dma_start(rl_i[0:1, 0:SROWS - 1],
                             dst[0:(SROWS - 1) * SR].rearrange("(a r c) -> a r c", a=1, c=SR)[:, :, SR - 1]).then_inc(in_last, 16)
            last = E - (SROWS - 1) * SR
            sp.dma_start(dst_rows[0:SROWS - 1, :], dst[0:(SROWS - 1) * SR].rearrange("(r c) -> r c", c=SR)).then_inc(pad_out, 16)
            sp.dma_start(dst_rows[SROWS - 1:SROWS, 0:last], dst[(SROWS - 1) * SR:E].rearrange("(a c) -> a c", a=1)).then_inc(pad_out, 16)
            sp.dma_start(dst_rows[SROWS - 1:SROWS, last:SR], pads_i[0:1, 0:SR - last]).then_inc(pad_out, 16)
            sp.dma_start(x_table[0:N, :], x).then_inc(x_out, 16)
            sp.dma_start(x_table[FLAG:FLAG + N, :].rearrange("(p r) f -> p (r f)", p=PP), ones_t[:, :]).then_inc(x_out, 16)
            sp.dma_start(group_table.rearrange("(t p) k -> t (p k)", p=P), pads[0:T, 0:4 * P]).then_inc(x_out, 16)
            sp.dma_start(edge_rows[E:E + G, :].rearrange("(a e) r -> a (e r)", a=1),
                         pads[0:1, 0:G * ROW // 2].bitcast(BF16)).then_inc(x_out, 16)
            sp.wait_ge(start_kept, 1)
            sp.dma_start(start_row_d[0:NP].rearrange("(t p) -> t p", p=P), start_t[:, :]).then_inc(start_out, 16)
            sp.dma_start(start_row_d[NP:NP + 8].rearrange("(a p) -> a p", a=1), pad_end[0:1, :]).then_inc(start_out, 16)
            sp.wait_ge(start_out, 32)
            sp.dma_start(r_a[0:1, :], start_row_d.rearrange("(a p) -> a p", a=1)).then_inc(row_in, 16)
            sp.dma_start(r_b[0:1, :], start_row_d[1:NP + 1].rearrange("(a p) -> a p", a=1)).then_inc(row_in, 16)
            sp.wait_ge(row_ready, 1)
            sp.dma_start(g0_row_d.rearrange("(a p) -> a p", a=1), r_g[0:1, :]).then_inc(row_out, 16)
            sp.dma_start(slot_row_d.rearrange("(a p) -> a p", a=1), r_c[0:1, :]).then_inc(row_out, 16)
            sp.wait_ge(row_out, 32)
            sp.dma_start(nm4[:, 0, :], g0_row_d.rearrange("(t p) -> t p", p=P)).then_inc(nm_in, 16)
            sp.dma_start(nm4[:, 1, :], slot_row_d.rearrange("(t p) -> t p", p=P)).then_inc(nm_in, 16)
            sp.dma_start(nm4[:, 2, :], start_row_d[1:NP + 1].rearrange("(t p) -> t p", p=P)).then_inc(nm_in, 16)
            sp.dma_start(nm4[:, 3, :], start_row_d[0:NP].rearrange("(t p) -> t p", p=P)).then_inc(nm_in, 16)
            sp.wait_ge(scattered, 16 * NT)
            sp.dma_start(gt[:, :, :], group_table.rearrange("(t p) k -> t p k", p=P)).then_inc(table_in, 16)
            sp.wait_ge(owner_ready, 1)
            sp.dma_start(owner_d[1:S + 1].rearrange("(t p) -> t p", p=P), gs[:, 0, :]).then_inc(owner_out, 16)
            sp.dma_start(owner_d[0:1].rearrange("(a p) -> a p", a=1), minus_1[0:1, 0:1]).then_inc(owner_out, 16)
            sp.wait_ge(owner_out, 32)
            sp.dma_start(own_p[:, :], owner_d[0:S].rearrange("(t p) -> t p", p=P)).then_inc(owner_in, 16)
            sp.wait_ge(fence_ready, 1)
            sp.dma_start(fence_d[0:S].rearrange("(t p) -> t p", p=P), fence_r[:, :]).then_inc(fence_out, 16)
            sp.dma_start(fence_d[S:S + 1].rearrange("(a p) -> a p", a=1), fence_end[0:1, 0:1]).then_inc(fence_out, 16)

            def spill(t, b):
                sp.wait_ge(sev_done, t + 1)
                sp.dma_start(group_sums[bass.ds(t, 1)].rearrange("a p c -> p (a c)"), spb[:, b, :]).then_inc(spill_out[b], 16)

            for t in range(3):
                spill(t, t)
            with sp.Fori(1, T // 3) as i:
                for b in range(3):
                    spill(3 * i + b, b)

            for b in range(3):
                sp.wait_ge(spill_out[b], 16 * (T // 3))
            sp.wait_ge(fence_out, 32)
            sp.dma_start(fence[:, :], fence_d.rearrange("(a p) -> a p", a=1).to_broadcast([P, S + 1])).then_inc(fence_in, 16)
            sp.wait_ge(scan_done, 4)

            def load(k, b):
                ge(sp, node_ps, k - 2)
                sp.nop(nofuse=True)
                tile = sp.value_load(step_tile[0:1, bass.ds(k, 1)], min_val=0, max_val=T - 1)
                sp.dma_start(md[:, b, :], group_sums[bass.ds(tile, 1)].rearrange("a p c -> p (a c)")).then_inc(md_in[b], 16)

            for k in range(3):
                load(k, k)
            with sp.Fori(1, STEPS // 3) as i:
                for b in range(3):
                    load(3 * i + b, b)
            sp.wait_ge(x_zero, 1)
            sp.dma_start(x_sb[:, 0:NT - 1, :], x[0:(NT - 1) * P, :].rearrange("(t p) f -> p t f", p=P)).then_inc(in_x, 16)
            sp.dma_start(x_sb[0:N - (NT - 1) * P, NT - 1, :], x[(NT - 1) * P:N, :]).then_inc(in_x, 16)

            sp.wait_ge(x1_ready, 1)
            for c in range(2):
                wa, ba, wb, bb, eps = gin[c]
                for k in range(3):
                    sp.dma_start(gw[k * F:(k + 1) * F, c, :], wa).then_inc(gin_in, 16)
                sp.dma_start(gwe[:, c, :], wa).then_inc(gin_in, 16)
                sp.dma_start(gb[:, c, :], wb).then_inc(gin_in, 16)
                with nc.allow_non_contiguous_dma(reason="a bias of 16, one on each partition"):
                    sp.dma_start(gba[:, c:c + 1], ba.rearrange("(f a) -> f a", a=1)).then_inc(gin_in, 16)
                sp.dma_start(gbb[0:1, c, :], bb.rearrange("(a f) -> a f", a=1)).then_inc(gin_in, 16)
                sp.dma_start(geps[:, c:c + 1], eps.rearrange("(a f) -> a f", a=1).to_broadcast([F, 1])).then_inc(gin_in, 16)
            sp.wait_ge(y_ready, 1)
            sp.dma_start(out[0:(NT - 1) * P, :].rearrange("(t p) f -> p t f", p=P), hn[:, 0:NT - 1, :]).then_inc(out_done, 16)
            sp.dma_start(out[(NT - 1) * P:N, :], hn[0:N - (NT - 1) * P, NT - 1, :]).then_inc(out_done, 16)
            sp.wait_ge(out_done, 32)

        @block.gpsimd
        def _(pool):
            done = [0]

            def link(ins):
                done[0] += 1
                ins.then_inc(pool_step, 1)
                pool.wait_ge(pool_step, done[0])

            def iota(t, pattern, channel=0):
                link(pool.iota(t, pattern, base=0, channel_multiplier=channel, allow_small_or_imprecise_dtypes=True))

            link(pool.memset(pads[:, :], 0.0))
            link(pool.memset(pad_end[:, :], float(E)))
            link(pool.memset(pads_i[:, :], 2 * NP))
            link(pool.memset(rl_i[:, :], 2 * NP))
            link(pool.memset(ones_row[:, :], 1.0))
            link(pool.memset(ones_t[:, :], 1.0))
            iota(iotaf[:, :], [[1, P]])
            iota(iota_key[:, :], [[1, CW]])
            iota(iota_lo[:, :], [[1, P]])
            iota(node_id[:, :], [[P, NT]], 1)
            iota(w500[:, :], [[CW, NW]])
            for m in (identf, identb):
                link(pool.memset(m[:, :], 0.0))
                link(pool.affine_select(out=m[:, :], in_=m[:, :], compare_op=ALU.not_equal, fill=1.0, base=0,
                                        pattern=[[-1, P]], channel_multiplier=1))
            pool.sem_inc(const_ready, 4)
            pool.memset(rows[:, :, :, 96:99], 1.0).then_inc(pre_fill, 1)
            pool.memset(rows[:, :, :, 99:100], 0.0).then_inc(pre_fill, 1)
            pool.wait_ge(rows_found, 1)
            pool.wait_ge(pad_out, 48)
            for t in range(NT):
                pool.indirect_dma_start(srow[:, t, :], None, dst_rows,
                                        bass.IndirectOffsetOnAxis(ap=found_i[:, t:t + 1], axis=0)).then_inc(search_in, 16)
            pool.wait_ge(row_ready, 1)
            iota(gid[:, :], [[P, T]], 1)
            iota(eslot[:, :, :], [[0, T], [1, G]])
            iota(kst[:, :], [[1, STEPS]])
            link(pool.memset(wflag[:, 0:C], -BIG / FLAG))
            link(pool.memset(wflag[:, C:2 * C], 0.0))
            link(pool.memset(fence_end[:, :], -BIG))
            link(pool.memset(minus_1[:, :], -1.0))
            link(pool.memset(er[:, 0, :, :], 0))
            link(pool.memset(er[:, 1, :, :], -4 * NP))
            pool.sem_inc(fill_ready, 3)
            pool.wait_ge(scatter_ready, 1)
            pool.wait_ge(x_out, 64)
            for t in range(NT):
                pool.indirect_dma_start(group_table, bass.IndirectOffsetOnAxis(ap=slot_i[:, t:t + 1], axis=0),
                                        pay[:, t, :], None, bounds_check=S - 1, oob_is_err=False).then_inc(scattered, 16)

            pool.wait_ge(tables_ready, 1)
            base = done[0]

            def fetch(t, b):
                ge(pool, tr_done, t - 2)
                pool.nop(nofuse=True)
                pool.tensor_copy(estc[:, b:b + 1], est_i[:, bass.ds(t, 1)]).then_inc(pool_step, 1)
                pool.wait_ge(pool_step, base + 1 if isinstance(t, int) and t == 0 else base + 2 * t)
                pool.nop(nofuse=True)
                pool.indirect_dma_start(blk[:, b, :, :].rearrange("p g r -> p (g r)"), None, edge_rows,
                                        bass.IndirectOffsetOnAxis(ap=estc[:, b:b + 1], axis=0)).then_inc(blk_in[b], 16)

            def gather(t, b, i):
                pool.wait_ge(blk_in[b], 16 * (i + 1))
                ge(pool, h_in[b], 16 * G * i)
                ge(pool, p1, G * (t - 2))
                pool.nop(nofuse=True)
                srcs = blk[:, b, :, :].rearrange("p g r -> p (g r)").bitcast(I32)\
                    .rearrange("p (g r) -> p g r", g=G)[:, :, KROWS // 2]
                pool.tensor_tensor(idxi[:, b, :], srcs, empty[:, bass.ds(t * G, G)], ALU.add).then_inc(pool_step, 1)
                pool.wait_ge(pool_step, base + 2 * t + 3)
                pool.nop(nofuse=True)
                for j in range(G):
                    pool.indirect_dma_start(hb[:, b, j, :], None, x_table,
                                            bass.IndirectOffsetOnAxis(ap=idxi[:, b, j:j + 1], axis=0)).then_inc(h_in[b], 16)

            fetch(0, 0)
            for t in range(3):
                fetch(t + 1, (t + 1) % 3)
                gather(t, t, 0)
            with pool.Fori(1, T // 3) as i:
                for b in range(3):
                    fetch(3 * i + b + 1, (b + 1) % 3)
                    gather(3 * i + b, b, i)
            pool.wait_ge(blk_in[0], 16 * (T // 3 + 1))
            pool.wait_ge(mc_done, STEPS)
            pool.memset(x_sb[:, :, :], 0.0).then_inc(x_zero, 1)

        @block.tensor
        def _(pe):
            pe.wait_ge(const_ready, 4)
            pe.wait_ge(last_ready, 1)
            pe.matmul(bank[0][:, 0:SROWS], ones_row[0:1, :], rl_f[0:1, :], start=True, stop=True).then_inc(last_bcast, 1)
            pe.wait_ge(start_ready, 1)
            pe.transpose(bank[1][0:NT, 0:P], start_nm[:, :], identf[:, :]).then_inc(start_turned, 1)
            pe.wait_ge(nm_in, 64)
            for k in range(4):
                mm = pe.transpose(bank[2][:, k * NT:(k + 1) * NT], nm4[:, k, :], identf[0:NT, 0:NT])
            mm.then_inc(nm_turned, 1)
            pe.wait_ge(wk_ready, 1)
            pe.matmul(bank[6][:, 0:STEPS], ones_row[0:1, :], kwin[0:1, :], start=True, stop=True).then_inc(wk_bcast, 1)
            pe.wait_ge(carry_ready, 1)
            pe.transpose(bank[3][0:4, 0:T], carry[:, :], identf[0:T, 0:T]).then_inc(carry_turned, 1)
            pe.wait_ge(carry_scanned, 1)
            pe.transpose(bank[4][0:T, 0:4], carry_r[:, 0:T], identf[0:4, 0:4]).then_inc(carry_back, 1)
            pe.wait_ge(owner_ready, 1)
            for k in range(4):
                mm = pe.transpose(bank[5][:, k * T:(k + 1) * T], gs[:, k, :], identf[0:T, 0:T])
            mm.then_inc(owners_turned, 1)
            pe.wait_ge(er_ready, 1)
            for k in range(2):
                for c in range(7):
                    n = min(P, ET - c * P)
                    mm = pe.transpose(bank[(0, 1, 7, 3)[2 * k + c // 4]][:, (c % 4) * P:(c % 4) * P + n], erf[0:n, k, c, :],
                                      identf[0:n, 0:n])
            mm.then_inc(er_turned, 1)
            pe.wait_ge(tables_ready, 1)

            def turn(t, b):
                pe.wait_ge(flag_done, t + 1)
                ge(pe, eft_done, t)
                for j in range(G):
                    mm = pe.transpose(turned[0:KROWS, j * P:(j + 1) * P], blk[:, b, j, 0:KROWS], identb[:, :])
                mm.then_inc(tr_done, 1)

            def message(t, b, j):
                if j == 0:
                    pe.wait_ge(eft_done, t + 1)
                ge(pe, p1, G * t + j - 3)
                pe.matmul(bank[j % 4][:, :], eft[:, b, j, :], wst[:, :], start=True, stop=True).then_inc(mm_done, 1)

            def total(t, b, j):
                if j == 0:
                    ge(pe, sev_done, t)
                if j % 4 == 0:
                    pe.wait_ge(p5, 2 * t + j // 4 + 1)
                mm = pe.matmul(bank[5][:, :], identf[:, :], em[:, b, j, :, :].rearrange("p a c -> p (a c)"),
                               start=(j == 0), stop=(j == G - 1))
                if j == G - 1:
                    mm.then_inc(sum_done, 1)

            def turn_max(t, b):
                pe.wait_ge(p2, 4 * t + 4)
                ge(pe, mev_done, t)
                for h in range(2):
                    mm = pe.transpose(bank[6][:, h * P:(h + 1) * P], spb[:, b, h * P:(h + 1) * P], identf[:, :])
                mm.then_inc(mtr_done, 1)

            def step(t, b, before=3, left=3):
                def totals(*slots):
                    for j in slots:
                        if before >= 2:
                            total(t - 2, (b + 1) % 3, j)

                totals(0, 1, 2)
                if before >= 1:
                    turn_max(t - 1, (b + 2) % 3)
                totals(3)
                for j in (4, 5):
                    message(t, b, j)
                totals(4)
                for j in (6, 7):
                    message(t, b, j)
                totals(5)
                if left >= 2:
                    turn(t + 2, (b + 2) % 3)
                totals(6)
                for j in range(4):
                    if left >= 1:
                        message(t + 1, (b + 1) % 3, j)
                totals(7)

            for t in range(2):
                turn(t, t)
            for j in range(G // 2):
                message(0, 0, j)
            for t in range(3):
                step(t, t, t)
            with pe.Fori(1, T // 3 - 1) as i:
                for b in range(3):
                    step(3 * i + b, b)
            for b in range(3):
                step(T - 3 + b, b, 3, 2 - b)
            turn_max(T - 1, 2)
            for t in (T - 2, T - 1):
                for j in range(G):
                    total(t, t % 3, j)

            def turn_back(k, b):
                pe.wait_ge(mc_done, k + 1)
                ge(pe, sub_done, k - 2)
                for h in range(2):
                    mm = pe.transpose(bank[b][:, h * P:(h + 1) * P], mc[:, b, h, :], identf[:, :])
                mm.then_inc(mtb_done, 1)

            def to_nodes(k, b):
                pe.wait_ge(wmul_done, k + 1)
                ge(pe, node_add, k - 2)
                pe.matmul(bank[3 + b][:, :], own_hot[:, b, :], md[:, b, C:3 * C], start=True, stop=True).then_inc(node_ps, 1)

            def join(k, b):
                turn_back(k, b)
                if not isinstance(k, int) or k > 0:
                    to_nodes(k - 1, (b + 2) % 3)

            for k in range(3):
                join(k, k)
            with pe.Fori(1, STEPS // 3) as i:
                for b in range(3):
                    join(3 * i + b, b)
            to_nodes(STEPS - 1, 2)

            pe.wait_ge(zero_ready, 1)

            def window(w, b):
                ge(pe, win_ev, w - 1)
                pe.nop(nofuse=True)
                first = pe.value_load(win_pair[0:1, bass.ds(w, 1)], min_val=0, max_val=ET // 2 - 1)
                last = pe.value_load(win_pair[0:1, bass.ds(w + 1, 1)], min_val=0, max_val=ET // 2 - 1)
                pe.matmul(bank[b][:, 0:CW], zero_b[:, 0:P], zero_b[:, :], start=True, stop=False)
                with pe.Fori(first, last + 1) as i:
                    for q in range(2):
                        pe.wait_ge(hot_ready, 2 * (i + w) + q + 1)
                        pe.matmul(bank[b][:, 0:CW], hot_lo[:, q, :], hot_key[:, q, :], start=False, stop=False).then_inc(hot_used, 1)
                pe.matmul(bank[b][:, 0:CW], zero_b[:, 0:P], zero_b[:, :], start=False, stop=True).then_inc(win_ps, 1)

            for w in range(2):
                window(w, w)
            with pe.Fori(1, NW // 2) as v:
                for b in range(2):
                    window(2 * v + b, b)

            pe.wait_ge(win_ev, NW)
            pe.wait_ge(gin_in, 16 * 16)
            for c in range(2):
                pe.wait_ge(xs_ready, c + 1)
                feat = (x1, hn)[c]
                for q, (n0, n) in enumerate(BLOCKS):
                    k = c * NB + q
                    ge(pe, xt_ev, k)
                    for t in range(n0 // P, (n0 + n) // P):
                        mm = pe.transpose(bank[4][0:F, t * P - n0:t * P - n0 + P], feat[:, t, :], identf[:, :])
                    mm.then_inc(xt_ps, 1)
                    ge(pe, conv_ev, k)
                    for h in range(NT):
                        mm = pe.matmul(bank[5][0:3 * F, 0:n], xs[:, h, :, :].rearrange("p a f -> p (a f)"), cnt[:, h, n0:n0 + n],
                                       start=(h == 0), stop=(h == NT - 1))
                    mm.then_inc(conv_ps, 1)
                    pe.wait_ge(conv_ev, k + 1)
                    pe.wait_ge(xt_ev, k + 1)
                    ge(pe, hid_ev, k)
                    pe.matmul(bank[6][0:F, 0:n], gw[:, c, :], agg[:, 0:n], start=True, stop=False)
                    pe.matmul(bank[6][0:F, 0:n], gwe[:, c, :], xt[:, 0:n], start=False, stop=True).then_inc(hid_ps, 1)
                    pe.wait_ge(hid_ev, k + 1)
                    for t in range(n0 // P, (n0 + n) // P):
                        pe.matmul(bank[7][:, t * F:(t + 1) * F], ut[:, t * P - n0:(t + 1) * P - n0], gb[:, c, :], start=True, stop=False)
                        mm = pe.matmul(bank[7][:, t * F:(t + 1) * F], ones_row[0:1, :], gbb[0:1, c, :], start=False, stop=True)
                    mm.then_inc(map2, 1)

        @block.scalar
        def _(act):
            ef_v = ef.rearrange("(p c e) f -> p c (e f)", p=PP, c=PREP)
            rows_v = edge_rows[0:E, :].rearrange("(p c e) r -> p c (e r)", p=PP, c=PREP)
            act.dma_start(src_i[:, :, :], src.rearrange("(p c e) -> p c e", p=PP, c=PREP)).then_inc(in_src, 16)
            for c in range(2):
                act.dma_start(ef_in[:, c, :, :].rearrange("p e f -> p (e f)"), ef_v[:, c]).then_inc(ef_ld[c], 16)
            act.wait_ge(pre_fill, 2)
            for c in range(PREP):
                b = c % 2
                act.wait_ge(ef_ld[b], 16 * (c // 2 + 1))
                ge(act, rows_out[b], 16 * (c // 2))
                act.activation(rows[:, b, :, 0:3 * F].rearrange("p e (k f) -> p e k f", k=3),
                               ef_in[:, b, :, :].unsqueeze(2).to_broadcast([PP, PC, 3, F]), ACT.Copy).then_inc(rows_high, 1)
                act.wait_ge(rows_resid, c + 1)
                act.activation(rows[:, b, :, 3 * F:5 * F].rearrange("p e (k f) -> p e k f", k=2),
                               resid[:, :, :].unsqueeze(2).to_broadcast([PP, PC, 2, F]), ACT.Copy).then_inc(rows_mid, 1)
                if c + 2 < PREP:
                    act.wait_ge(rows_high, c + 1)
                    act.dma_start(ef_in[:, b, :, :].rearrange("p e f -> p (e f)"), ef_v[:, c + 2]).then_inc(ef_ld[b], 16)
                act.wait_ge(rows_done, 2 * (c + 1))
                act.dma_start(rows_v[:, c], rows[:, b, :, :].rearrange("p e r -> p (e r)")).then_inc(rows_out[b], 16)
            act.wait_ge(fill_ready, 3)
            act.dma_start(wf[0:F, 0:C], w_att).then_inc(w_in, 16)
            act.dma_start(wf[0:F, C:2 * C], w_msg).then_inc(w_in, 16)
            act.dma_start(wf[F:F + 1, 0:C], b_att.rearrange("(a c) -> a c", a=1)).then_inc(w_in, 16)
            act.dma_start(wf[F:F + 1, C:2 * C], b_msg.rearrange("(a c) -> a c", a=1)).then_inc(w_in, 16)
            full = E // P
            for k, a in enumerate((src, dst)):
                act.dma_start(er[:, k, 0:6, :], a[0:6 * P * P].rearrange("(c r p) -> r c p", p=P, r=P)).then_inc(er_in, 16)
                act.dma_start(er[0:full - 6 * P, k, 6, :], a[6 * P * P:full * P].rearrange("(r p) -> r p", p=P)).then_inc(er_in, 16)
                act.dma_start(er[full - 6 * P:full - 6 * P + 1, k, 6, 0:E - full * P],
                              a[full * P:E].rearrange("(a p) -> a p", a=1)).then_inc(er_in, 16)
            act.wait_ge(w_split, 1)
            for k, part in enumerate((0, 1, 2, 0, 1, 0)):
                act.dma_start(wst[k * F:(k + 1) * F, :], wh[0:F, part, :]).then_inc(w_out, 16)
            for part in range(3):
                act.dma_start(wst[6 * F + part:6 * F + part + 1, :], wh[F:F + 1, part, :]).then_inc(w_out, 16)
            act.dma_start(wst[KROWS - 1:KROWS, :], wflag[0:1, :]).then_inc(w_out, 16)
            act.wait_ge(tables_ready, 1)

            def flags(t, b, i):
                act.wait_ge(blk_in[b], 16 * (i + 1))
                act.nop(nofuse=True)
                act.activation(blk[:, b, :, KROWS - 1], empty[:, bass.ds(t * G, G)], ACT.Copy).then_inc(flag_done, 1)

            def keep_turned(t, b):
                act.wait_ge(tr_done, t + 1)
                ge(act, mm_done, G * (t - 2))
                act.activation(eft[:, b, :, :].rearrange("p g e -> p (g e)"), turned[0:KROWS, :], ACT.Copy).then_inc(eft_done, 1)

            def exps(t, b):
                for q in range(2):
                    act.wait_ge(p3, 2 * t + q + 1)
                    act.activation(em[:, b, 4 * q:4 * q + 4, 0, :], em[:, b, 4 * q:4 * q + 4, 0, :], ACT.Exp).then_inc(exp_done, 1)

            def keep_max(t, b):
                act.wait_ge(mtr_done, t + 1)
                act.nop(nofuse=True)
                act.activation(mt[:, :, bass.ds(t * P, P)], bank[6][:, 0:2 * P].rearrange("p (h g) -> p h g", h=2),
                               ACT.Copy).then_inc(mev_done, 1)

            def keep_sums(t, b, i):
                act.wait_ge(sum_done, t + 1)
                ge(act, spill_out[b], 16 * i)
                act.activation(spb[:, b, C:3 * C], bank[5][:, :], ACT.Copy).then_inc(sev_done, 1)

            def step(t, b, i, before=3, left=3):
                if left >= 2:
                    keep_turned(t + 2, (b + 2) % 3)
                if before >= 1:
                    keep_max(t - 1, (b + 2) % 3)
                if before >= 2:
                    keep_sums(t - 2, (b + 1) % 3, i - 1 if b < 2 else i)
                exps(t, b)
                if left >= 3:
                    flags(t + 3, b, i + 1)

            for t in range(3):
                flags(t, t, 0)
                if t < 2:
                    keep_turned(t, t)
            for t in range(6):
                step(t, t % 3, t // 3, t)
            with act.Fori(2, T // 3 - 1) as i:
                for b in range(3):
                    step(3 * i + b, b, i)
            for b in range(3):
                step(T - 3 + b, b, T // 3 - 1, 3, 2 - b)
            keep_max(T - 1, 2)
            keep_sums(T - 2, 1, T // 3 - 1)
            keep_sums(T - 1, 2, T // 3 - 1)

            act.wait_ge(scan_done, 4)

            def maxima(k, b):
                ge(act, mtb_done, k - 2)
                act.nop(nofuse=True)
                tile = act.value_load(step_tile[0:1, bass.ds(k, 1)], min_val=0, max_val=T - 1)
                act.nop(nofuse=True)
                act.activation(mc[:, b, :, :], mt[:, :, bass.ds(tile * P, P)], ACT.Copy).then_inc(mc_done, 1)

            def factors(k, b):
                act.wait_ge(sub_done, k + 1)
                act.activation(md[:, b, 0:C], md[:, b, 0:C], ACT.Exp).then_inc(wexp_done, 1)

            for k in range(2):
                maxima(k, k)
            for k in range(3):
                maxima(k + 2, (k + 2) % 3)
                factors(k, k)
            with act.Fori(1, STEPS // 3 - 1) as i:
                for b in range(3):
                    maxima(3 * i + b + 2, (b + 2) % 3)
                    factors(3 * i + b, b)
            maxima(STEPS - 1, 2)
            for b in range(3):
                factors(STEPS - 3 + b, b)
            act.wait_ge(ln_var, 1)
            act.activation(st2[:, :], st1[:, :], ACT.Sqrt).then_inc(ln_sd, 1)

            with act.Fori(0, NW // 2) as v:
                for b in range(2):
                    act.wait_ge(win_ps, 2 * v + b + 1)
                    act.nop(nofuse=True)
                    act.activation(cnt[:, :, bass.ds((2 * v + b) * WIN, WIN)],
                                   bank[b][:, 0:CW].rearrange("p (n h) -> p h n", h=NT), ACT.Copy).then_inc(win_ev, 1)

            for c in range(2):
                for q, (n0, n) in enumerate(BLOCKS):
                    k = c * NB + q
                    act.wait_ge(xt_ps, k + 1)
                    ge(act, hid_ps, k)
                    act.activation(xt[:, 0:n], bank[4][0:F, 0:n], ACT.Copy).then_inc(xt_ev, 1)
                    act.wait_ge(conv_ps, k + 1)
                    act.activation(agg[:, 0:n], bank[5][0:3 * F, 0:n], ACT.Copy).then_inc(conv_ev, 1)
                    act.wait_ge(hid_ps, k + 1)
                    ge(act, map2, k)
                    act.activation(ut[:, 0:n], bank[6][0:F, 0:n], ACT.Relu, bias=gba[:, c:c + 1]).then_inc(hid_ev, 1)
            act.wait_ge(lsm_e, 1)
            act.activation(hn[:, :, :], hn2[:, :, :], ACT.Exp).then_inc(lsm_s, 1)
            act.wait_ge(lsm_e, 2)
            act.activation(st2[:, :], st1[:, :], ACT.Ln).then_inc(lsm_l, 1)
            act.wait_ge(ln_var, 2)
            act.activation(st2[:, :], st1[:, :], ACT.Sqrt).then_inc(ln_sd, 1)

        @block.vector
        def _(dve):
            done = [0]

            def link(ins):
                done[0] += 1
                ins.then_inc(dve_step, 1)
                dve.wait_ge(dve_step, done[0])

            dve.wait_ge(const_ready, 4)
            dve.wait_ge(in_last, 16)
            dve.tensor_copy(rl_f[:, :], rl_i[:, :]).then_inc(last_ready, 1)
            dve.wait_ge(last_bcast, 1)
            link(dve.tensor_copy(rl_b[:, :], bank[0][:, 0:SROWS]))
            link(dve.tensor_tensor(less[:, :, :], rl_b[:, :].unsqueeze(1).to_broadcast([P, NT, SROWS]),
                                   node_id[:, :].unsqueeze(2).to_broadcast([P, NT, SROWS]), ALU.is_lt))
            link(dve.tensor_reduce(found_r[:, :], less[:, :, :], AX.X, ALU.add))
            dve.tensor_copy(found_i[:, :], found_r[:, :]).then_inc(rows_found, 1)
            dve.wait_ge(in_src, 16)

            def split_rows(c):
                b = c % 2
                dve.wait_ge(rows_high, c + 1)
                ge(dve, rows_mid, c)
                ge(dve, rows_done, 2 * c)
                dve.tensor_tensor(resid[:, :, :], ef_in[:, b, :, :], rows[:, b, :, 0:F], ALU.subtract).then_inc(rows_resid, 1)
                dve.tensor_copy(rows[:, b, :, :].rearrange("p e r -> p (e r)").bitcast(I32)
                                .rearrange("p (e r) -> p e r", e=PC)[:, :, KROWS // 2], src_i[:, c, :]).then_inc(rows_done, 1)
                dve.wait_ge(rows_mid, c + 1)
                dve.tensor_tensor(rows[:, b, :, 5 * F:6 * F], resid[:, :, :], rows[:, b, :, 3 * F:4 * F],
                                  ALU.subtract).then_inc(rows_done, 1)

            for c in range(3):
                split_rows(c)
            dve.wait_ge(search_in, 16 * NT)
            link(dve.tensor_tensor(less[:, :, 0:SR], srow[:, :, :],
                                   node_id[:, :].unsqueeze(2).to_broadcast([P, NT, SR]), ALU.is_lt))
            link(dve.tensor_reduce(start_nm[:, :], less[:, :, 0:SR], AX.X, ALU.add))
            dve.scalar_tensor_tensor(out=start_nm[:, :], in0=found_r[:, :], scalar=float(SR), in1=start_nm[:, :],
                                     op0=ALU.mult, op1=ALU.add).then_inc(start_ready, 1)
            dve.wait_ge(start_turned, 1)
            dve.tensor_copy(start_t[:, :], bank[1][0:NT, 0:P]).then_inc(start_kept, 1)
            for c in range(3, 6):
                split_rows(c)
            dve.wait_ge(row_in, 32)
            link(dve.tensor_tensor(r_c[:, :], r_b[:, :], r_a[:, 0:NP], ALU.subtract))
            link(dve.tensor_scalar(r_i[:, :], r_c[:, :], float(G - 1), None, ALU.add))
            link(dve.tensor_scalar(r_i[:, :], r_i[:, :], 3, None, ALU.arith_shift_right))
            link(dve.tensor_copy(r_b[:, :], r_i[:, :]))
            link(dve.tensor_scalar(r_c[:, :], r_c[:, :], 0.0, float(2 * S), ALU.is_equal, ALU.mult))
            link(dve.tensor_tensor_scan(r_g[:, :], r_b[:, :], r_b[:, :], 0.0, ALU.add, ALU.max))
            link(dve.tensor_copy(r_i[0:1, 0:NT], r_g[0:1, P - 1:NP:P]))
            link(dve.tensor_scalar(r_i[0:1, 0:NT], r_i[0:1, 0:NT], 7, None, ALU.arith_shift_right))
            link(dve.tensor_copy(win_pair[:, :], r_a[0:1, 0:NP + 1:WIN]))
            link(dve.tensor_scalar(win_pair[:, :], win_pair[:, :], 8, None, ALU.arith_shift_right))
            link(dve.tensor_tensor(r_g[:, :], r_g[:, :], r_b[:, :], ALU.subtract))
            dve.tensor_tensor(r_c[:, :], r_c[:, :], r_g[:, :], ALU.add).then_inc(row_ready, 1)
            for c in range(6, PREP):
                split_rows(c)
            dve.wait_ge(fill_ready, 3)
            link(dve.tensor_copy(kt_f[:, :], r_i[0:1, 0:NT]))
            link(dve.tensor_tensor(kt_f[:, :], kt_f[:, :], kst[:, 0:NT], ALU.add))
            link(dve.tensor_tensor(kcmp[:, :, :], kt_f[:, :].unsqueeze(1).to_broadcast([1, STEPS, NT]),
                                   kst[:, :].unsqueeze(2).to_broadcast([1, STEPS, NT]), ALU.is_lt))
            link(dve.tensor_reduce(kwin[:, :], kcmp[:, :, :], AX.X, ALU.add))
            link(dve.tensor_copy(step_win[:, :], kwin[:, :]))
            link(dve.tensor_tensor(kst[:, :], kst[:, :], kwin[:, :], ALU.subtract))
            link(dve.tensor_scalar(step_tile[:, :], kst[:, :], float(T - 1), None, ALU.min))
            dve.tensor_scalar(kwin[:, :], kwin[:, :], float(P), None, ALU.mult).then_inc(wk_ready, 1)
            dve.wait_ge(nm_turned, 1)
            nmv = bank[2][:, 0:4 * NT].rearrange("p (k t) -> p k t", k=4)
            link(dve.tensor_copy(pay[:, :, 0], node_id[:, :]))
            link(dve.tensor_copy(pay[:, :, 1], nmv[:, 3, :]))
            link(dve.tensor_copy(pay[:, :, 2], nmv[:, 2, :]))
            link(dve.tensor_copy(pay[:, :, 3], nmv[:, 0, :]))
            dve.tensor_copy(slot_i[:, :], nmv[:, 1, :]).then_inc(scatter_ready, 1)
            dve.wait_ge(w_in, 64)
            link(dve.tensor_copy(wh[:, 0, :], wf[:, :]))
            link(dve.tensor_tensor(wf[:, :], wf[:, :], wh[:, 0, :], ALU.subtract))
            link(dve.tensor_copy(wh[:, 1, :], wf[:, :]))
            dve.tensor_tensor(wh[:, 2, :], wf[:, :], wh[:, 1, :], ALU.subtract).then_inc(w_split, 1)
            dve.wait_ge(er_in, 96)
            link(dve.tensor_scalar(eh[:, :, :], er[:, 0, :, :], 7, None, ALU.arith_shift_right))
            link(dve.tensor_scalar(erf[:, 0, :, :], er[:, 1, :, :], float(NT), None, ALU.mult))
            link(dve.tensor_tensor(erf[:, 0, :, :], erf[:, 0, :, :], eh[:, :, :], ALU.add))
            link(dve.tensor_scalar(eh[:, :, :], er[:, 0, :, :], P - 1, None, ALU.bitwise_and))
            dve.tensor_copy(erf[:, 1, :, :], eh[:, :, :]).then_inc(er_ready, 1)
            dve.wait_ge(table_in, 16)
            for k in range(4):
                link(dve.tensor_tensor_scan(gs[:, k, :], gt[:, :, k], gt[:, :, k], 0.0, ALU.max, ALU.max))
            dve.tensor_copy(carry[:, :], gs[:, :, P - 1]).then_inc(carry_ready, 1)
            link(dve.memset(carry_r[:, 0:1], 0.0))
            dve.wait_ge(carry_turned, 1)
            link(dve.tensor_copy(carry_r[:, 1:T + 1], bank[3][0:4, 0:T]))
            dve.tensor_tensor_scan(carry_r[:, :], carry_r[:, :], carry_r[:, :], 0.0, ALU.max, ALU.max).then_inc(carry_scanned, 1)
            dve.wait_ge(carry_back, 1)
            link(dve.tensor_copy(carry_b[:, :], bank[4][0:T, 0:4]))
            for k in range(3):
                link(dve.tensor_scalar(gs[:, k, :], gs[:, k, :], carry_b[:, k:k + 1], None, ALU.max))
            dve.tensor_scalar(gs[:, 3, :], gs[:, 3, :], carry_b[:, 3:4], None, ALU.max).then_inc(owner_ready, 1)
            dve.wait_ge(owner_in, 16)
            link(dve.tensor_tensor(own_p[:, :], own_p[:, :], gs[:, 0, :], ALU.not_equal))
            dve.tensor_scalar(fence_r[:, :], own_p[:, :], -FAR, None, ALU.mult).then_inc(fence_ready, 1)
            dve.wait_ge(owners_turned, 1)
            link(dve.tensor_copy(gm[:, :, :], bank[5][:, 0:4 * T].rearrange("p (k t) -> p k t", k=4)))
            link(dve.tensor_copy(own_t[:, :], gm[:, 0, :]))
            link(dve.tensor_tensor(gid[:, :], gid[:, :], gm[:, 3, :], ALU.subtract))
            link(dve.scalar_tensor_tensor(out=estf[:, :], in0=gid[:, :], scalar=float(G), in1=gm[:, 1, :], op0=ALU.mult, op1=ALU.add))
            link(dve.memset(est_i[:, T:T + 1], 0))
            link(dve.tensor_scalar(est_i[:, 0:T], estf[:, :], float(E), None, ALU.min))
            link(dve.tensor_tensor(eslot[:, :, :], eslot[:, :, :], estf[:, :].unsqueeze(2).to_broadcast([P, T, G]), ALU.add))
            link(dve.tensor_tensor(eslot[:, :, :], eslot[:, :, :], gm[:, 2, :].unsqueeze(2).to_broadcast([P, T, G]), ALU.is_ge))
            link(dve.tensor_scalar(empty[:, :], eslot[:, :, :].rearrange("p t g -> p (t g)"), float(FLAG), None, ALU.mult))
            dve.wait_ge(wk_bcast, 1)
            link(dve.tensor_copy(step_w128[:, :], bank[6][:, 0:STEPS]))
            dve.wait_ge(er_turned, 1)
            link(dve.tensor_copy(kb[:, 0:512], bank[0][:, :]))
            link(dve.tensor_copy(kb[:, 512:ET], bank[1][:, 0:ET - 512]))
            link(dve.tensor_copy(lo[:, 0:512], bank[7][:, :]))
            link(dve.tensor_copy(lo[:, 512:ET], bank[3][:, 0:ET - 512]))
            dve.wait_ge(w_out, 16 * 10)
            dve.wait_ge(fence_out, 32)
            for c in range(2):
                dve.wait_ge(rows_out[c], 16 * PREP // 2)
            dve.sem_inc(tables_ready, 1)

            def scores(t, b, i):
                dve.wait_ge(h_in[b], 16 * G * (i + 1))
                ge(dve, sum_done, t - 2)
                for j in range(G):
                    dve.wait_ge(mm_done, G * t + j + 1)
                    dve.tensor_tensor(em[:, b, j, :, :].rearrange("p a (i o) -> p a i o", i=F),
                                      bank[j % 4][:, :].rearrange("p (a i o) -> p a i o", a=2, i=F),
                                      hb[:, b, j, :].unsqueeze(1).unsqueeze(3).to_broadcast([P, 2, F, F]),
                                      ALU.mult).then_inc(p1, 1)

            def weigh(t, b, q):
                dve.wait_ge(exp_done, 2 * t + q + 1)
                dve.tensor_tensor(em[:, b, 4 * q:4 * q + 4, 1, :], em[:, b, 4 * q:4 * q + 4, 1, :],
                                  em[:, b, 4 * q:4 * q + 4, 0, :], ALU.mult).then_inc(p5, 1)

            def step(t, b, i, before=3):
                scores(t, b, i)
                dve.wait_ge(p1, G * t + G)
                dve.tensor_tensor(mx[:, :, :], em[:, b, 0:2, 0, :], em[:, b, 2:4, 0, :], ALU.max).then_inc(p2, 1)
                for q in range(2):
                    if before >= 1:
                        weigh(t - 1, (b + 2) % 3, q)
                    dve.wait_ge(p2, 4 * t + q + 1)
                    dve.tensor_tensor(mx[:, :, :], mx[:, :, :], em[:, b, 4 + 2 * q:6 + 2 * q, 0, :], ALU.max).then_inc(p2, 1)
                dve.wait_ge(p2, 4 * t + 3)
                ge(dve, mtr_done, t - 2)
                ge(dve, spill_out[b], 16 * i)
                dve.tensor_tensor(spb[:, b, 0:C], mx[:, 0, :], mx[:, 1, :], ALU.max).then_inc(p2, 1)
                dve.wait_ge(p2, 4 * t + 4)
                for q in range(2):
                    dve.tensor_tensor(em[:, b, 4 * q:4 * q + 4, 0, :], em[:, b, 4 * q:4 * q + 4, 0, :],
                                      spb[:, b, 0:C].unsqueeze(1).to_broadcast([P, 4, C]), ALU.subtract).then_inc(p3, 1)

            for t in range(3):
                step(t, t, 0, t)
            with dve.Fori(1, T // 3) as i:
                for b in range(3):
                    step(3 * i + b, b, i)
            for q in range(2):
                weigh(T - 1, 2, q)

            dve.wait_ge(fence_in, 16)
            dve.wait_ge(mev_done, T)
            for h in range(2):
                dve.tensor_tensor_scan(mt[:, h, :], fence[:, 0:S], mt[:, h, :], 0.0, ALU.add, ALU.max).then_inc(scan_done, 1)
            for h in range(2):
                dve.wait_ge(scan_done, h + 1)
                dve.tensor_tensor_scan(mt[:, h, ::-1], fence[:, S:0:-1], mt[:, h, ::-1], 0.0, ALU.add, ALU.max).then_inc(scan_done, 1)
            dve.wait_ge(scan_done, 4)
            link(dve.memset(acc[:, :, :], 0.0))

            def tile_factors(k, b, i):
                tile = dve.value_load(step_tile[0:1, bass.ds(k, 1)], min_val=0, max_val=T - 1)
                ge(dve, node_ps, k - 2)
                dve.nop(nofuse=True)
                dve.tensor_scalar(own_hot[:, b, :], iotaf[:, :], step_w128[:, bass.ds(k, 1)], own_t[:, bass.ds(tile, 1)],
                                  ALU.add, ALU.is_equal).then_inc(own_done, 1)
                dve.wait_ge(md_in[b], 16 * (i + 1))
                dve.wait_ge(mtb_done, k + 1)
                dve.tensor_tensor(md[:, b, 0:C], md[:, b, 0:C], bank[b][:, 0:C], ALU.subtract).then_inc(sub_done, 1)

            def scale(k, b):
                dve.wait_ge(wexp_done, k + 1)
                dve.wait_ge(own_done, k + 1)
                sums = md[:, b, C:3 * C].rearrange("p (a c) -> p a c", a=2)
                dve.tensor_tensor(sums, sums, md[:, b, 0:C].unsqueeze(1).to_broadcast([P, 2, C]), ALU.mult).then_inc(wmul_done, 1)

            def add_nodes(k, b):
                win = dve.value_load(step_win[0:1, bass.ds(k, 1)], min_val=0, max_val=NT)
                dve.wait_ge(node_ps, k + 1)
                ge(dve, node_add, k)
                dve.nop(nofuse=True)
                node = acc[:, bass.ds(win, 1), :].rearrange("p a c -> p (a c)")
                dve.tensor_tensor(node, node, bank[3 + b][:, :], ALU.add).then_inc(node_add, 1)

            def join(k, b, i):
                tile_factors(k, b, i)
                if not isinstance(k, int) or k >= 1:
                    scale(k - 1, (b + 2) % 3)
                if not isinstance(k, int) or k >= 2:
                    add_nodes(k - 2, (b + 1) % 3)

            for k in range(3):
                join(k, k, 0)
            with dve.Fori(1, STEPS // 3) as i:
                for b in range(3):
                    join(3 * i + b, b, i)
            scale(STEPS - 1, 2)
            for b in (1, 2):
                add_nodes(STEPS - 3 + b, b)
            dve.wait_ge(node_add, STEPS)
            den = acc[:, 0:NT, 0:C]
            num = acc[:, 0:NT, C:2 * C]
            link(dve.tensor_scalar(den, den, 0.5, None, ALU.max))
            link(dve.reciprocal(den, den))
            link(dve.tensor_tensor(num, num, den, ALU.mult))
            link(dve.tensor_reduce(hn2[:, :, :], num.rearrange("p t (i o) -> p t o i", i=F), AX.X, ALU.add))
            dve.wait_ge(in_x, 32)
            link(dve.tensor_tensor(hn2[:, :, :], hn2[:, :, :], x_sb[:, :, :], ALU.add))

            def layernorm(result, n, ready):
                link(dve.tensor_reduce(st1[:, :], hn2[:, :, :], AX.X, ALU.add))
                link(dve.tensor_scalar(st1[:, :], st1[:, :], 1.0 / F, None, ALU.mult))
                link(dve.tensor_tensor(hn2[:, :, :], hn2[:, :, :], st1[:, :].unsqueeze(2).to_broadcast([P, NT, F]), ALU.subtract))
                link(dve.tensor_tensor(hn[:, :, :], hn2[:, :, :], hn2[:, :, :], ALU.mult))
                link(dve.tensor_reduce(st1[:, :], hn[:, :, :], AX.X, ALU.add))
                link(dve.tensor_scalar(st1[:, :], st1[:, :], 1.0 / F, EPS, ALU.mult, ALU.add))
                dve.sem_inc(ln_var, 1)
                dve.wait_ge(ln_sd, n)
                link(dve.reciprocal(st2[:, :], st2[:, :]))
                link(dve.tensor_tensor(result[:, :, :], hn2[:, :, :], st2[:, :].unsqueeze(2).to_broadcast([P, NT, F]), ALU.mult))
                dve.sem_inc(ready, 1)

            layernorm(x1, 1, x1_ready)

            dve.memset(zero_b[:, :], 0.0).then_inc(zero_ready, 1)
            dve.memset(hot_lo[:, :, :], 0.0).then_inc(hot_used, 2)
            with dve.Fori(0, NW) as w:
                first = dve.value_load(win_pair[0:1, bass.ds(w, 1)], min_val=0, max_val=ET // 2 - 1)
                last = dve.value_load(win_pair[0:1, bass.ds(w + 1, 1)], min_val=0, max_val=ET // 2 - 1)
                with dve.Fori(first, last + 1) as i:
                    for q in range(2):
                        dve.wait_ge(hot_used, 2 * (i + w) + q + 1)
                        dve.nop(nofuse=True)
                        dve.tensor_scalar(hot_lo[:, q, :], iota_lo[:, :], lo[:, bass.ds(2 * i + q, 1)], None, ALU.is_equal)
                        dve.tensor_scalar(hot_key[:, q, :], iota_key[:, :], w500[:, bass.ds(w, 1)], kb[:, bass.ds(2 * i + q, 1)],
                                          ALU.add, ALU.is_equal).then_inc(hot_ready, 1)

            dve.wait_ge(win_ev, NW)
            dve.wait_ge(gin_in, 16 * 16)
            link(dve.tensor_scalar(geps[:, :], geps[:, :], 1.0, None, ALU.add))
            for c in range(2):
                link(dve.tensor_scalar(gwe[:, c, :], gwe[:, c, :], geps[:, c:c + 1], None, ALU.mult))
            hps = bank[7][:, 0:NT * F].rearrange("p (t f) -> p t f", f=F)
            for c, feat in enumerate((x1, hn)):
                link(dve.tensor_copy(xs[:, :, 0, :], feat[:, :, :]))
                link(dve.tensor_tensor(xr[:, :, :], feat[:, :, :], xs[:, :, 0, :], ALU.subtract))
                link(dve.tensor_copy(xs[:, :, 1, :], xr[:, :, :]))
                dve.tensor_tensor(xs[:, :, 2, :], xr[:, :, :], xs[:, :, 1, :], ALU.subtract).then_inc(xs_ready, 1)
                dve.wait_ge(map2, (c + 1) * NB)
                if c == 0:
                    link(dve.tensor_scalar(hn[:, :, :], hps, 0.0, None, ALU.max))
            link(dve.tensor_copy(hn2[:, :, :], hps))
            link(dve.tensor_reduce(st1[:, :], hn2[:, :, :], AX.X, ALU.max))
            dve.tensor_tensor(hn2[:, :, :], hn2[:, :, :], st1[:, :].unsqueeze(2).to_broadcast([P, NT, F]),
                              ALU.subtract).then_inc(lsm_e, 1)
            dve.wait_ge(lsm_s, 1)
            dve.tensor_reduce(st1[:, :], hn[:, :, :], AX.X, ALU.add).then_inc(lsm_e, 1)
            dve.wait_ge(lsm_l, 1)
            link(dve.tensor_tensor(hn2[:, :, :], hn2[:, :, :], st2[:, :].unsqueeze(2).to_broadcast([P, NT, F]), ALU.subtract))
            link(dve.tensor_tensor(hn2[:, :, :], hn2[:, :, :], x1[:, :, :], ALU.add))
            layernorm(hn, 2, y_ready)


def kernel(**inputs):
    import numpy as np
    import concourse.bacc as bacc
    from concourse.bass_utils import run_bass_kernel_spmd

    nc = bacc.Bacc("TRN2", target_bir_lowering=False, num_devices=1)
    arrays, a = {}, {}
    for name, value in inputs.items():
        v = np.ascontiguousarray(value)
        if v.ndim == 0:
            v = v.reshape(1)
        arrays[f"in_{name}"] = v
        a[name] = nc.dram_tensor(f"in_{name}", v.shape, mybir.dt.from_np(v.dtype), kind="ExternalInput").ap()
    out = nc.dram_tensor("out_0", (N, F), F32, kind="ExternalOutput").ap()
    gin = [tuple(a[f"L1_gnn_{k}"] for k in (f"w{c}a", f"b{c}a", f"w{c}b", f"b{c}b", f"eps{c}")) for c in (1, 2)]
    program(nc, a["x"], a["src"], a["dst"], a["edge_attr_16"], a["L0_gnn_W_msg"], a["L0_gnn_b_msg"],
            a["L0_gnn_W_attn"], a["L0_gnn_b_attn"], gin, out)
    r = run_bass_kernel_spmd(nc, [arrays], core_ids=[0])
    return r.results[0]["out_0"]
```

```python
from contextlib import ExitStack

import concourse.bass as bass
from concourse import mybir

F32 = mybir.dt.float32
BF16 = mybir.dt.bfloat16
FP16 = mybir.dt.float16
I32 = mybir.dt.int32
ALU = mybir.AluOpType
ACT = mybir.ActivationFunctionType
AX = mybir.AxisListType

P = 128
N = 3125
E = 100000
F = 16
C = F * F
NT = -(-N // P)
NP = NT * P
G = 8
GROUPS = (E + N * (G - 1)) // G
T = -(-GROUPS // (3 * P)) * 3
S = T * P
ROW = 102
KROWS = 100
SR = 256
SROWS = -(-E // SR)
STEPS = -(-(T + NT) // 3) * 3
WIN = 20
NW = NP // WIN
WG = 8
CW = WIN * NT
EU = 3
UNITS = -(-E // (EU * P))
ET = UNITS * EU
BIG = 1.0e30
FAR = 3.0e38
FLAG = N
PREP = 8
PP = 125
PC = E // PP // PREP
EPS = 1e-5
BLOCKS = [(n0, min(512, NP - n0)) for n0 in range(0, NP, 512)]
NB = len(BLOCKS)
assert GROUPS <= S and PP * PC * PREP == E and NW % WG == 0 and NW * WIN == NP


def ge(eng, sema, value):
    if not isinstance(value, int) or value > 0:
        eng.wait_ge(sema, value)


def program(nc, x, src, dst, ef, w_msg, b_msg, w_att, b_att, gin, out):
    with ExitStack() as ctx:
        def sem(name):
            return ctx.enter_context(nc.semaphore(name))

        def sb(name, shape, dt, at=ctx):
            return at.enter_context(nc.sbuf_tensor(name, shape, dt))

        def dram(name, shape, dt):
            return nc.dram_tensor(name, shape, dt).ap()

        edge_rows = dram("edge_rows", (E + G, ROW), BF16)
        x_table = dram("x_table", (FLAG + N, F), F32)
        dst_rows = dram("dst_rows", (SROWS, SR), I32)
        start_row_d = dram("start_row_d", (NP + 8,), F32)
        g0_row_d = dram("g0_row_d", (NP,), F32)
        slot_row_d = dram("slot_row_d", (NP,), F32)
        group_table = dram("group_table", (S, 4), F32)
        owner_d = dram("owner_d", (S + 1,), F32)
        fence_d = dram("fence_d", (S + 1,), BF16)
        group_sums = dram("group_sums", (T, P, 3 * C), F32)

        bank = [ctx.enter_context(nc.psum_tensor(f"bank{i}", [P, 512], F32)) for i in range(8)]
        turned = bank[4][:, :].bitcast(BF16)

        identf = sb("identf", [P, P], F32)
        identb = sb("identb", [P, P], BF16)
        iotaf = sb("iotaf", [P, P], F32)
        iota_key = sb("iota_key", [P, CW], FP16)
        iota_lo = sb("iota_lo", [P, P], FP16)
        ones_row = sb("ones_row", [1, P], F32)
        w500 = sb("w500", [P, NW], F32)
        wst = sb("wst", [KROWS, 2 * C], BF16)
        own_t = sb("own_t", [P, T], F32)
        est_i = sb("est_i", [P, T + 1], I32)
        empty = sb("empty", [P, T * G], I32)
        step_tile = sb("step_tile", [1, STEPS], I32)
        step_win = sb("step_win", [1, STEPS], I32)
        step_w128 = sb("step_w128", [P, STEPS], F32)
        win_unit = sb("win_unit", [1, NW + 1], I32)
        kb = sb("kb", [P, ET], F32)
        lo = sb("lo", [P, ET], BF16)

        setup = ExitStack()
        r_a = sb("r_a", [1, NP + 8], F32, setup)
        r_b = sb("r_b", [1, NP], F32, setup)
        r_c = sb("r_c", [1, NP], F32, setup)
        r_g = sb("r_g", [1, NP], F32, setup)
        r_i = sb("r_i", [1, NP], I32, setup)
        ef_in = sb("ef_in", [PP, 2, PC, F], F32, setup)
        resid = sb("resid", [PP, PC, F], F32, setup)
        rows = sb("rows", [PP, 2, PC, ROW], BF16, setup)
        src_i = sb("src_i", [PP, PREP, PC], I32, setup)
        node_id = sb("node_id", [P, NT], F32, setup)
        pads = sb("pads", [P, 512], F32, setup)
        ones_t = sb("ones_t", [PP, N * F // PP], F32, setup)
        pad_end = sb("pad_end", [1, 8], F32, setup)
        pads_i = sb("pads_i", [1, SR], I32, setup)
        found_r = sb("found_r", [P, NT], F32, setup)
        found_i = sb("found_i", [P, NT], I32, setup)
        start_nm = sb("start_nm", [P, NT], F32, setup)
        start_t = sb("start_t", [NT, P], F32, setup)
        search = ExitStack()
        rl_i = sb("rl_i", [1, SROWS], I32, search)
        rl_f = sb("rl_f", [1, max(SROWS, 3 * (NW + 1))], F32, search)
        rl_b = sb("rl_b", [P, SROWS], F32, search)
        less = sb("less", [P, NT, SROWS], BF16, search)
        srow = sb("srow", [P, NT, SR], I32, search)
        search.close()
        tables = ExitStack()
        nm4 = sb("nm4", [NT, 4, P], F32, tables)
        slot_i = sb("slot_i", [P, NT], I32, tables)
        pay = sb("pay", [P, NT, 4], F32, tables)
        gt = sb("gt", [T, P, 4], F32, tables)
        gs = sb("gs", [T, 4, P], F32, tables)
        carry = sb("carry", [T, 4], F32, tables)
        carry_r = sb("carry_r", [4, T + 1], F32, tables)
        carry_b = sb("carry_b", [T, 4], F32, tables)
        own_p = sb("own_p", [T, P], F32, tables)
        fence_r = sb("fence_r", [T, P], BF16, tables)
        fence_end = sb("fence_end", [1, 2], BF16, tables)
        minus_1 = sb("minus_1", [1, 2], F32, tables)
        gm = sb("gm", [P, 4, T], F32, tables)
        gid = sb("gid", [P, T], F32, tables)
        estf = sb("estf", [P, T], F32, tables)
        eslot = sb("eslot", [P, T, G], F32, tables)
        wf = sb("wf", [F + 1, 2 * C], F32, tables)
        wh = sb("wh", [F + 1, 3, 2 * C], BF16, tables)
        wflag = sb("wflag", [1, 2 * C], BF16, tables)
        kst = sb("kst", [1, STEPS], F32, tables)
        kcmp = sb("kcmp", [1, STEPS, NT], F32, tables)
        kwin = sb("kwin", [1, STEPS], F32, tables)
        kt_i = sb("kt_i", [1, NT], I32, tables)
        kt_f = sb("kt_f", [1, NT], F32, tables)
        er = sb("er", [P, 2, 7, P], I32, tables)
        eh = sb("eh", [P, 7, P], I32, tables)
        erf = sb("erf", [P, 2, 7, P], F32, tables)
        tables.close()
        setup.close()
        levels = ExitStack()
        mt = sb("mt", [P, 2, S], F32, levels)
        level1 = ExitStack()
        blk = sb("blk", [P, 3, G, ROW], BF16, level1)
        eft = sb("eft", [KROWS, 3, G, P], BF16, level1)
        hb = sb("hb", [P, 3, G, F], F32, level1)
        em = sb("em", [P, 3, G, 2, C], F32, level1)
        mx = sb("mx", [P, 2, C], F32, level1)
        spb = sb("spb", [P, 3, 3 * C], F32, level1)
        estc = sb("estc", [P, 3], I32, level1)
        idxi = sb("idxi", [P, 3, G], I32, level1)
        level1.close()
        scans = ExitStack()
        fence = sb("fence", [P, S + 1], BF16, scans)
        scans.close()
        level2 = ExitStack()
        acc = sb("acc", [P, NT + 1, 2 * C], F32, level2)
        md = sb("md", [P, 3, 3 * C], F32, level2)
        mc = sb("mc", [P, 3, 2, P], F32, level2)
        own_hot = sb("own_hot", [P, 3, P], F32, level2)
        x1 = sb("x1", [P, NT, F], F32, level2)
        hn = sb("hn", [P, NT, F], F32, level2)
        hn2 = sb("hn2", [P, NT, F], F32, level2)
        st1 = sb("st1", [P, NT], F32, level2)
        st2 = sb("st2", [P, NT], F32, level2)
        level2.close()
        levels.close()
        levelx = ExitStack()
        x_sb = sb("x_sb", [P, NT, F], F32, levelx)
        levelx.close()
        ginx = ExitStack()
        cnt = sb("cnt", [P, NT, NP], BF16, ginx)
        hot_lo = sb("hot_lo", [P, EU, P], BF16, ginx)
        hot_sq = sb("hot_sq", [P, EU - 1, P], BF16, ginx)
        minus_lo = sb("minus_lo", [P, ET], F32, ginx)
        hot_key = sb("hot_key", [P, EU, CW], BF16, ginx)
        one_col = sb("one_col", [P, 1], F32, ginx)
        zero_b = sb("zero_b", [P, CW], BF16, ginx)
        xs = sb("xs", [P, NT, 3, F], BF16, ginx)
        xr = sb("xr", [P, NT, F], F32, ginx)
        xt = sb("xt", [F, 2, 512], F32, ginx)
        agg = sb("agg", [3 * F, 2, 512], F32, ginx)
        ut = sb("ut", [F, 2, 512], F32, ginx)
        gw = sb("gw", [3 * F, 2, F], F32, ginx)
        gwe = sb("gwe", [F, 2, F], F32, ginx)
        gb = sb("gb", [F, 2, F], F32, ginx)
        gba = sb("gba", [F, 2], F32, ginx)
        gbb = sb("gbb", [1, 2, F], F32, ginx)
        geps = sb("geps", [F, 2], F32, ginx)
        ginx.close()

        (const_ready, pool_step, dve_step, in_x, in_last, in_src, pad_out, last_ready, last_bcast, rows_found, search_in,
         start_ready, start_turned, start_kept, start_out, row_in, row_ready, row_out, nm_in, nm_turned, scatter_ready,
         scattered, table_in, carry_ready, carry_turned, carry_scanned, carry_back, owner_ready, owner_out, owner_in,
         fence_ready, fence_out, owners_turned, tables_ready, w_in, w_split, w_out, wk_ready, wk_bcast, er_in, er_ready,
         er_turned, fill_ready, rows_high, rows_resid, rows_mid, rows_done, x_out, pre_fill, flag_done, tr_done, eft_done,
         mm_done, p1, p2, p3, exp_done, p5, sum_done, mtr_done, mev_done, sev_done, fence_in, scan_done, mc_done,
         mtb_done, sub_done, wexp_done, wmul_done, own_done, node_ps, node_add, ln_var, ln_sd, x1_ready, hot_ready,
         hot_used, win_ps, win_ev, gin_in, xs_ready, conv_ps, conv_ev, xt_ps, xt_ev, hid_ps, hid_ev, map2, lsm_e, lsm_s,
         lsm_l, y_ready, out_done, zero_ready, x_zero, lo_ready, sq_done) = [sem(n) for n in (
             "const_ready pool_step dve_step in_x in_last in_src pad_out last_ready last_bcast rows_found search_in "
             "start_ready start_turned start_kept start_out row_in row_ready row_out nm_in nm_turned scatter_ready "
             "scattered table_in carry_ready carry_turned carry_scanned carry_back owner_ready owner_out owner_in "
             "fence_ready fence_out owners_turned tables_ready w_in w_split w_out wk_ready wk_bcast er_in er_ready "
             "er_turned fill_ready rows_high rows_resid rows_mid rows_done x_out pre_fill flag_done tr_done eft_done "
             "mm_done p1 p2 p3 exp_done p5 sum_done mtr_done mev_done sev_done fence_in scan_done mc_done "
             "mtb_done sub_done wexp_done wmul_done own_done node_ps node_add ln_var ln_sd x1_ready hot_ready "
             "hot_used win_ps win_ev gin_in xs_ready conv_ps conv_ev xt_ps xt_ev hid_ps hid_ev map2 lsm_e lsm_s "
             "lsm_l y_ready out_done zero_ready x_zero lo_ready sq_done").split()]
        ef_ld = [sem(f"ef_ld{i}") for i in range(2)]
        rows_out = [sem(f"rows_out{i}") for i in range(2)]
        blk_in = [sem(f"blk_in{i}") for i in range(3)]
        h_in = [sem(f"h_in{i}") for i in range(3)]
        spill_out = [sem(f"spill_out{i}") for i in range(3)]
        md_in = [sem(f"md_in{i}") for i in range(3)]

        def window_units(engine, v):
            return nc.values_load_multi_w_load_instructions(win_unit[0:1, bass.ds(WG * v, WG + 1)], [engine], min_val=0,
                                                            max_val=UNITS - 1)[1]

        block = ctx.enter_context(nc.Block())

        @block.sync
        def _(sp):
            sp.wait_ge(const_ready, 4)
            with nc.allow_non_contiguous_dma(reason="the last destination of each search row"):
                sp.dma_start(rl_i[0:1, 0:SROWS - 1],
                             dst[0:(SROWS - 1) * SR].rearrange("(a r c) -> a r c", a=1, c=SR)[:, :, SR - 1]).then_inc(in_last, 16)
            last = E - (SROWS - 1) * SR
            sp.dma_start(dst_rows[0:SROWS - 1, :], dst[0:(SROWS - 1) * SR].rearrange("(r c) -> r c", c=SR)).then_inc(pad_out, 16)
            sp.dma_start(dst_rows[SROWS - 1:SROWS, 0:last], dst[(SROWS - 1) * SR:E].rearrange("(a c) -> a c", a=1)).then_inc(pad_out, 16)
            sp.dma_start(dst_rows[SROWS - 1:SROWS, last:SR], pads_i[0:1, 0:SR - last]).then_inc(pad_out, 16)
            sp.dma_start(x_table[0:N, :], x).then_inc(x_out, 16)
            sp.dma_start(x_table[FLAG:FLAG + N, :].rearrange("(p r) f -> p (r f)", p=PP), ones_t[:, :]).then_inc(x_out, 16)
            sp.dma_start(group_table.rearrange("(t p) k -> t (p k)", p=P), pads[0:T, 0:4 * P]).then_inc(x_out, 16)
            sp.dma_start(edge_rows[E:E + G, :].rearrange("(a e) r -> a (e r)", a=1),
                         pads[0:1, 0:G * ROW // 2].bitcast(BF16)).then_inc(x_out, 16)
            sp.wait_ge(start_kept, 1)
            sp.dma_start(start_row_d[0:NP].rearrange("(t p) -> t p", p=P), start_t[:, :]).then_inc(start_out, 16)
            sp.dma_start(start_row_d[NP:NP + 8].rearrange("(a p) -> a p", a=1), pad_end[0:1, :]).then_inc(start_out, 16)
            sp.wait_ge(start_out, 32)
            sp.dma_start(r_a[0:1, :], start_row_d.rearrange("(a p) -> a p", a=1)).then_inc(row_in, 16)
            sp.dma_start(r_b[0:1, :], start_row_d[1:NP + 1].rearrange("(a p) -> a p", a=1)).then_inc(row_in, 16)
            sp.wait_ge(row_ready, 1)
            sp.dma_start(g0_row_d.rearrange("(a p) -> a p", a=1), r_g[0:1, :]).then_inc(row_out, 16)
            sp.dma_start(slot_row_d.rearrange("(a p) -> a p", a=1), r_c[0:1, :]).then_inc(row_out, 16)
            sp.wait_ge(row_out, 32)
            sp.dma_start(nm4[:, 0, :], g0_row_d.rearrange("(t p) -> t p", p=P)).then_inc(nm_in, 16)
            sp.dma_start(nm4[:, 1, :], slot_row_d.rearrange("(t p) -> t p", p=P)).then_inc(nm_in, 16)
            sp.dma_start(nm4[:, 2, :], start_row_d[1:NP + 1].rearrange("(t p) -> t p", p=P)).then_inc(nm_in, 16)
            sp.dma_start(nm4[:, 3, :], start_row_d[0:NP].rearrange("(t p) -> t p", p=P)).then_inc(nm_in, 16)
            sp.wait_ge(scattered, 16 * NT)
            sp.dma_start(gt[:, :, :], group_table.rearrange("(t p) k -> t p k", p=P)).then_inc(table_in, 16)
            sp.wait_ge(owner_ready, 1)
            sp.dma_start(owner_d[1:S + 1].rearrange("(t p) -> t p", p=P), gs[:, 0, :]).then_inc(owner_out, 16)
            sp.dma_start(owner_d[0:1].rearrange("(a p) -> a p", a=1), minus_1[0:1, 0:1]).then_inc(owner_out, 16)
            sp.wait_ge(owner_out, 32)
            sp.dma_start(own_p[:, :], owner_d[0:S].rearrange("(t p) -> t p", p=P)).then_inc(owner_in, 16)
            sp.wait_ge(fence_ready, 1)
            sp.dma_start(fence_d[0:S].rearrange("(t p) -> t p", p=P), fence_r[:, :]).then_inc(fence_out, 16)
            sp.dma_start(fence_d[S:S + 1].rearrange("(a p) -> a p", a=1), fence_end[0:1, 0:1]).then_inc(fence_out, 16)

            def spill(t, b):
                sp.wait_ge(sev_done, t + 1)
                sp.dma_start(group_sums[bass.ds(t, 1)].rearrange("a p c -> p (a c)"), spb[:, b, :]).then_inc(spill_out[b], 16)

            for t in range(3):
                spill(t, t)
            with sp.Fori(1, T // 3) as i:
                for b in range(3):
                    spill(3 * i + b, b)

            for b in range(3):
                sp.wait_ge(spill_out[b], 16 * (T // 3))
            sp.wait_ge(fence_out, 32)
            sp.dma_start(fence[:, :], fence_d.rearrange("(a p) -> a p", a=1).to_broadcast([P, S + 1])).then_inc(fence_in, 16)
            sp.wait_ge(scan_done, 4)

            def load(k, b):
                ge(sp, node_ps, k - 2)
                sp.nop(nofuse=True)
                tile = sp.value_load(step_tile[0:1, bass.ds(k, 1)], min_val=0, max_val=T - 1)
                sp.dma_start(md[:, b, :], group_sums[bass.ds(tile, 1)].rearrange("a p c -> p (a c)")).then_inc(md_in[b], 16)

            for k in range(3):
                load(k, k)
            with sp.Fori(1, STEPS // 3) as i:
                for b in range(3):
                    load(3 * i + b, b)
            sp.wait_ge(x_zero, 1)
            sp.dma_start(x_sb[:, 0:NT - 1, :], x[0:(NT - 1) * P, :].rearrange("(t p) f -> p t f", p=P)).then_inc(in_x, 16)
            sp.dma_start(x_sb[0:N - (NT - 1) * P, NT - 1, :], x[(NT - 1) * P:N, :]).then_inc(in_x, 16)

            sp.wait_ge(x1_ready, 1)
            for c in range(2):
                wa, ba, wb, bb, eps = gin[c]
                for k in range(3):
                    sp.dma_start(gw[k * F:(k + 1) * F, c, :], wa).then_inc(gin_in, 16)
                sp.dma_start(gwe[:, c, :], wa).then_inc(gin_in, 16)
                sp.dma_start(gb[:, c, :], wb).then_inc(gin_in, 16)
                with nc.allow_non_contiguous_dma(reason="a bias of 16, one on each partition"):
                    sp.dma_start(gba[:, c:c + 1], ba.rearrange("(f a) -> f a", a=1)).then_inc(gin_in, 16)
                sp.dma_start(gbb[0:1, c, :], bb.rearrange("(a f) -> a f", a=1)).then_inc(gin_in, 16)
                sp.dma_start(geps[:, c:c + 1], eps.rearrange("(a f) -> a f", a=1).to_broadcast([F, 1])).then_inc(gin_in, 16)
            sp.wait_ge(y_ready, 1)
            sp.dma_start(out[0:(NT - 1) * P, :].rearrange("(t p) f -> p t f", p=P), hn[:, 0:NT - 1, :]).then_inc(out_done, 16)
            sp.dma_start(out[(NT - 1) * P:N, :], hn[0:N - (NT - 1) * P, NT - 1, :]).then_inc(out_done, 16)
            sp.wait_ge(out_done, 32)

        @block.gpsimd
        def _(pool):
            done = [0]

            def link(ins):
                done[0] += 1
                ins.then_inc(pool_step, 1)
                pool.wait_ge(pool_step, done[0])

            def iota(t, pattern, channel=0):
                link(pool.iota(t, pattern, base=0, channel_multiplier=channel, allow_small_or_imprecise_dtypes=True))

            link(pool.memset(pads[:, :], 0.0))
            link(pool.memset(pad_end[:, :], float(E)))
            link(pool.memset(pads_i[:, :], 2 * NP))
            link(pool.memset(rl_i[:, :], 2 * NP))
            link(pool.memset(ones_row[:, :], 1.0))
            link(pool.memset(ones_t[:, :], 1.0))
            iota(iotaf[:, :], [[1, P]])
            iota(iota_key[:, :], [[1, CW]])
            iota(iota_lo[:, :], [[1, P]])
            iota(node_id[:, :], [[P, NT]], 1)
            iota(w500[:, :], [[CW, NW]])
            for m in (identf, identb):
                link(pool.memset(m[:, :], 0.0))
                link(pool.affine_select(out=m[:, :], in_=m[:, :], compare_op=ALU.not_equal, fill=1.0, base=0,
                                        pattern=[[-1, P]], channel_multiplier=1))
            pool.sem_inc(const_ready, 4)
            pool.memset(rows[:, :, :, 96:99], 1.0).then_inc(pre_fill, 1)
            pool.memset(rows[:, :, :, 99:100], 0.0).then_inc(pre_fill, 1)
            pool.wait_ge(rows_found, 1)
            pool.wait_ge(pad_out, 48)
            for t in range(NT):
                pool.indirect_dma_start(srow[:, t, :], None, dst_rows,
                                        bass.IndirectOffsetOnAxis(ap=found_i[:, t:t + 1], axis=0)).then_inc(search_in, 16)
            pool.wait_ge(row_ready, 1)
            iota(gid[:, :], [[P, T]], 1)
            iota(eslot[:, :, :], [[0, T], [1, G]])
            iota(kst[:, :], [[1, STEPS]])
            link(pool.memset(wflag[:, 0:C], -BIG / FLAG))
            link(pool.memset(wflag[:, C:2 * C], 0.0))
            link(pool.memset(fence_end[:, :], -BIG))
            link(pool.memset(minus_1[:, :], -1.0))
            link(pool.memset(er[:, 0, :, :], 0))
            link(pool.memset(er[:, 1, :, :], -4 * NP))
            pool.sem_inc(fill_ready, 3)
            pool.wait_ge(scatter_ready, 1)
            pool.wait_ge(x_out, 64)
            for t in range(NT):
                pool.indirect_dma_start(group_table, bass.IndirectOffsetOnAxis(ap=slot_i[:, t:t + 1], axis=0),
                                        pay[:, t, :], None, bounds_check=S - 1, oob_is_err=False).then_inc(scattered, 16)

            pool.wait_ge(tables_ready, 1)
            base = done[0]

            def fetch(t, b):
                ge(pool, tr_done, t - 2)
                pool.nop(nofuse=True)
                pool.tensor_copy(estc[:, b:b + 1], est_i[:, bass.ds(t, 1)]).then_inc(pool_step, 1)
                pool.wait_ge(pool_step, base + 1 if isinstance(t, int) and t == 0 else base + 2 * t)
                pool.nop(nofuse=True)
                pool.indirect_dma_start(blk[:, b, :, :].rearrange("p g r -> p (g r)"), None, edge_rows,
                                        bass.IndirectOffsetOnAxis(ap=estc[:, b:b + 1], axis=0)).then_inc(blk_in[b], 16)

            def gather(t, b, i):
                pool.wait_ge(blk_in[b], 16 * (i + 1))
                ge(pool, h_in[b], 16 * G * i)
                ge(pool, p1, G * (t - 2))
                pool.nop(nofuse=True)
                srcs = blk[:, b, :, :].rearrange("p g r -> p (g r)").bitcast(I32)\
                    .rearrange("p (g r) -> p g r", g=G)[:, :, KROWS // 2]
                pool.tensor_tensor(idxi[:, b, :], srcs, empty[:, bass.ds(t * G, G)], ALU.add).then_inc(pool_step, 1)
                pool.wait_ge(pool_step, base + 2 * t + 3)
                pool.nop(nofuse=True)
                for j in range(G):
                    pool.indirect_dma_start(hb[:, b, j, :], None, x_table,
                                            bass.IndirectOffsetOnAxis(ap=idxi[:, b, j:j + 1], axis=0)).then_inc(h_in[b], 16)

            fetch(0, 0)
            for t in range(3):
                fetch(t + 1, (t + 1) % 3)
                gather(t, t, 0)
            with pool.Fori(1, T // 3) as i:
                for b in range(3):
                    fetch(3 * i + b + 1, (b + 1) % 3)
                    gather(3 * i + b, b, i)
            pool.wait_ge(blk_in[0], 16 * (T // 3 + 1))
            pool.wait_ge(mc_done, STEPS)
            pool.memset(x_sb[:, :, :], 0.0).then_inc(x_zero, 1)

        @block.tensor
        def _(pe):
            pe.wait_ge(const_ready, 4)
            pe.wait_ge(last_ready, 1)
            pe.matmul(bank[0][:, 0:SROWS], ones_row[0:1, :], rl_f[0:1, 0:SROWS], start=True, stop=True).then_inc(last_bcast, 1)
            pe.wait_ge(start_ready, 1)
            pe.transpose(bank[1][0:NT, 0:P], start_nm[:, :], identf[:, :]).then_inc(start_turned, 1)
            pe.wait_ge(nm_in, 64)
            for k in range(4):
                mm = pe.transpose(bank[2][:, k * NT:(k + 1) * NT], nm4[:, k, :], identf[0:NT, 0:NT])
            mm.then_inc(nm_turned, 1)
            pe.wait_ge(wk_ready, 1)
            pe.matmul(bank[6][:, 0:STEPS], ones_row[0:1, :], kwin[0:1, :], start=True, stop=True).then_inc(wk_bcast, 1)
            pe.wait_ge(carry_ready, 1)
            pe.transpose(bank[3][0:4, 0:T], carry[:, :], identf[0:T, 0:T]).then_inc(carry_turned, 1)
            pe.wait_ge(carry_scanned, 1)
            pe.transpose(bank[4][0:T, 0:4], carry_r[:, 0:T], identf[0:4, 0:4]).then_inc(carry_back, 1)
            pe.wait_ge(owner_ready, 1)
            for k in range(4):
                mm = pe.transpose(bank[5][:, k * T:(k + 1) * T], gs[:, k, :], identf[0:T, 0:T])
            mm.then_inc(owners_turned, 1)
            pe.wait_ge(er_ready, 1)
            for k in range(2):
                for c in range(7):
                    n = min(P, ET - c * P)
                    mm = pe.transpose(bank[(0, 1, 7, 3)[2 * k + c // 4]][:, (c % 4) * P:(c % 4) * P + n], erf[0:n, k, c, :],
                                      identf[0:n, 0:n])
            mm.then_inc(er_turned, 1)
            pe.wait_ge(tables_ready, 1)

            def turn(t, b):
                pe.wait_ge(flag_done, t + 1)
                ge(pe, eft_done, t)
                for j in range(G):
                    mm = pe.transpose(turned[0:KROWS, j * P:(j + 1) * P], blk[:, b, j, 0:KROWS], identb[:, :])
                mm.then_inc(tr_done, 1)

            def message(t, b, j):
                if j == 0:
                    pe.wait_ge(eft_done, t + 1)
                ge(pe, p1, G * t + j - 3)
                pe.matmul(bank[j % 4][:, :], eft[:, b, j, :], wst[:, :], start=True, stop=True).then_inc(mm_done, 1)

            def total(t, b, j):
                if j == 0:
                    ge(pe, sev_done, t)
                if j % 4 == 0:
                    pe.wait_ge(p5, 2 * t + j // 4 + 1)
                mm = pe.matmul(bank[5][:, :], identf[:, :], em[:, b, j, :, :].rearrange("p a c -> p (a c)"),
                               start=(j == 0), stop=(j == G - 1))
                if j == G - 1:
                    mm.then_inc(sum_done, 1)

            def turn_max(t, b):
                pe.wait_ge(p2, 4 * t + 4)
                ge(pe, mev_done, t)
                for h in range(2):
                    mm = pe.transpose(bank[6][:, h * P:(h + 1) * P], spb[:, b, h * P:(h + 1) * P], identf[:, :])
                mm.then_inc(mtr_done, 1)

            def step(t, b, before=3, left=3):
                def totals(*slots):
                    for j in slots:
                        if before >= 2:
                            total(t - 2, (b + 1) % 3, j)

                totals(0, 1, 2)
                if before >= 1:
                    turn_max(t - 1, (b + 2) % 3)
                totals(3)
                for j in (4, 5):
                    message(t, b, j)
                totals(4)
                for j in (6, 7):
                    message(t, b, j)
                totals(5)
                if left >= 2:
                    turn(t + 2, (b + 2) % 3)
                totals(6)
                for j in range(4):
                    if left >= 1:
                        message(t + 1, (b + 1) % 3, j)
                totals(7)

            for t in range(2):
                turn(t, t)
            for j in range(G // 2):
                message(0, 0, j)
            for t in range(3):
                step(t, t, t)
            with pe.Fori(1, T // 3 - 1) as i:
                for b in range(3):
                    step(3 * i + b, b)
            for b in range(3):
                step(T - 3 + b, b, 3, 2 - b)
            turn_max(T - 1, 2)
            for t in (T - 2, T - 1):
                for j in range(G):
                    total(t, t % 3, j)

            def turn_back(k, b):
                pe.wait_ge(mc_done, k + 1)
                ge(pe, sub_done, k - 2)
                for h in range(2):
                    mm = pe.transpose(bank[b][:, h * P:(h + 1) * P], mc[:, b, h, :], identf[:, :])
                mm.then_inc(mtb_done, 1)

            def to_nodes(k, b):
                pe.wait_ge(wmul_done, k + 1)
                ge(pe, node_add, k - 2)
                pe.matmul(bank[3 + b][:, :], own_hot[:, b, :], md[:, b, C:3 * C], start=True, stop=True).then_inc(node_ps, 1)

            def join(k, b, more=True):
                if more:
                    turn_back(k + 2, (b + 2) % 3)
                to_nodes(k, b)

            for k in range(2):
                turn_back(k, k)
            for k in range(3):
                join(k, k)
            with pe.Fori(1, STEPS // 3 - 1) as i:
                for b in range(3):
                    join(3 * i + b, b)
            for b in range(3):
                join(STEPS - 3 + b, b, b < 1)

            pe.wait_ge(zero_ready, 1)

            def windows(v):
                units = window_units(mybir.EngineType.PE, v)
                for b in range(WG):
                    w = WG * v + b
                    ge(pe, win_ev, w - 3)
                    pe.nop(nofuse=True)
                    pe.matmul(bank[b % 4][:, 0:CW], zero_b[:, 0:P], zero_b[:, :], start=True, stop=False)
                    with pe.Fori(units[b], units[b + 1] + 1) as i:
                        for q in range(EU):
                            if q == 1:
                                pe.wait_ge(lo_ready, i + w + 2)
                            pe.wait_ge(hot_ready, EU * (i + w) + q + 1)
                            pe.matmul(bank[b % 4][:, 0:CW], hot_lo[:, q, :], hot_key[:, q, :], start=False, stop=False).then_inc(hot_used, 1)
                    pe.matmul(bank[b % 4][:, 0:CW], zero_b[:, 0:P], zero_b[:, :], start=False, stop=True).then_inc(win_ps, 1)

            windows(0)
            with pe.Fori(1, NW // WG) as v:
                windows(v)

            pe.wait_ge(win_ev, NW)
            pe.wait_ge(gin_in, 16 * 16)

            def neighbours(c, q):
                k, (n0, n) = c * NB + q, BLOCKS[q]
                ge(pe, xt_ev, k - 1)
                for t in range(n0 // P, (n0 + n) // P):
                    mm = pe.transpose(bank[k % 2][0:F, t * P - n0:t * P - n0 + P], (x1, hn)[c][:, t, :], identf[:, :])
                mm.then_inc(xt_ps, 1)
                ge(pe, conv_ev, k - 1)
                for h in range(NT):
                    mm = pe.matmul(bank[2 + k % 2][0:3 * F, 0:n], xs[:, h, :, :].rearrange("p a f -> p (a f)"), cnt[:, h, n0:n0 + n],
                                   start=(h == 0), stop=(h == NT - 1))
                mm.then_inc(conv_ps, 1)

            def map_first(c, q):
                k, (n0, n) = c * NB + q, BLOCKS[q]
                pe.wait_ge(conv_ev, k + 1)
                pe.wait_ge(xt_ev, k + 1)
                ge(pe, hid_ev, k - 1)
                pe.matmul(bank[4 + k % 2][0:F, 0:n], gw[:, c, :], agg[:, k % 2, 0:n], start=True, stop=False)
                pe.matmul(bank[4 + k % 2][0:F, 0:n], gwe[:, c, :], xt[:, k % 2, 0:n], start=False, stop=True).then_inc(hid_ps, 1)

            def map_second(c, q):
                k, (n0, n) = c * NB + q, BLOCKS[q]
                pe.wait_ge(hid_ev, k + 1)
                for t in range(n0 // P, (n0 + n) // P):
                    pe.matmul(bank[7][:, t * F:(t + 1) * F], ut[:, k % 2, t * P - n0:(t + 1) * P - n0], gb[:, c, :], start=True, stop=False)
                    mm = pe.matmul(bank[7][:, t * F:(t + 1) * F], ones_row[0:1, :], gbb[0:1, c, :], start=False, stop=True)
                mm.then_inc(map2, 1)

            for c in range(2):
                pe.wait_ge(xs_ready, c + 1)
                for q in range(NB + 2):
                    if q < NB:
                        neighbours(c, q)
                    if q >= 2:
                        map_second(c, q - 2)
                    if 1 <= q <= NB:
                        map_first(c, q - 1)

        @block.scalar
        def _(act):
            ef_v = ef.rearrange("(p c e) f -> p c (e f)", p=PP, c=PREP)
            rows_v = edge_rows[0:E, :].rearrange("(p c e) r -> p c (e r)", p=PP, c=PREP)
            act.dma_start(src_i[:, :, :], src.rearrange("(p c e) -> p c e", p=PP, c=PREP)).then_inc(in_src, 16)
            for c in range(2):
                act.dma_start(ef_in[:, c, :, :].rearrange("p e f -> p (e f)"), ef_v[:, c]).then_inc(ef_ld[c], 16)
            act.wait_ge(pre_fill, 2)

            def raise_rows(c):
                b = c % 2
                act.wait_ge(ef_ld[b], 16 * (c // 2 + 1))
                ge(act, rows_out[b], 16 * (c // 2))
                act.activation(rows[:, b, :, 0:3 * F].rearrange("p e (k f) -> p e k f", k=3),
                               ef_in[:, b, :, :].unsqueeze(2).to_broadcast([PP, PC, 3, F]), ACT.Copy).then_inc(rows_high, 1)
                act.wait_ge(rows_resid, c + 1)
                act.activation(rows[:, b, :, 3 * F:5 * F].rearrange("p e (k f) -> p e k f", k=2),
                               resid[:, :, :].unsqueeze(2).to_broadcast([PP, PC, 2, F]), ACT.Copy).then_inc(rows_mid, 1)
                if c + 2 < PREP:
                    act.wait_ge(rows_high, c + 1)
                    act.dma_start(ef_in[:, b, :, :].rearrange("p e f -> p (e f)"), ef_v[:, c + 2]).then_inc(ef_ld[b], 16)
                act.wait_ge(rows_done, 2 * (c + 1))
                act.dma_start(rows_v[:, c], rows[:, b, :, :].rearrange("p e r -> p (e r)")).then_inc(rows_out[b], 16)

            for c in range(5):
                raise_rows(c)
            act.wait_ge(fill_ready, 3)
            act.dma_start(wf[0:F, 0:C], w_att).then_inc(w_in, 16)
            act.dma_start(wf[0:F, C:2 * C], w_msg).then_inc(w_in, 16)
            act.dma_start(wf[F:F + 1, 0:C], b_att.rearrange("(a c) -> a c", a=1)).then_inc(w_in, 16)
            act.dma_start(wf[F:F + 1, C:2 * C], b_msg.rearrange("(a c) -> a c", a=1)).then_inc(w_in, 16)
            full = E // P
            for k, a in enumerate((src, dst)):
                act.dma_start(er[:, k, 0:6, :], a[0:6 * P * P].rearrange("(c r p) -> r c p", p=P, r=P)).then_inc(er_in, 16)
                act.dma_start(er[0:full - 6 * P, k, 6, :], a[6 * P * P:full * P].rearrange("(r p) -> r p", p=P)).then_inc(er_in, 16)
                act.dma_start(er[full - 6 * P:full - 6 * P + 1, k, 6, 0:E - full * P],
                              a[full * P:E].rearrange("(a p) -> a p", a=1)).then_inc(er_in, 16)
            for c in range(5, PREP):
                raise_rows(c)
            act.wait_ge(w_split, 1)
            for k, part in enumerate((0, 1, 2, 0, 1, 0)):
                act.dma_start(wst[k * F:(k + 1) * F, :], wh[0:F, part, :]).then_inc(w_out, 16)
            for part in range(3):
                act.dma_start(wst[6 * F + part:6 * F + part + 1, :], wh[F:F + 1, part, :]).then_inc(w_out, 16)
            act.dma_start(wst[KROWS - 1:KROWS, :], wflag[0:1, :]).then_inc(w_out, 16)
            act.wait_ge(tables_ready, 1)

            def flags(t, b, i):
                act.wait_ge(blk_in[b], 16 * (i + 1))
                act.nop(nofuse=True)
                act.activation(blk[:, b, :, KROWS - 1], empty[:, bass.ds(t * G, G)], ACT.Copy).then_inc(flag_done, 1)

            def keep_turned(t, b):
                act.wait_ge(tr_done, t + 1)
                ge(act, mm_done, G * (t - 2))
                act.activation(eft[:, b, :, :].rearrange("p g e -> p (g e)"), turned[0:KROWS, :], ACT.Copy).then_inc(eft_done, 1)

            def exps(t, b):
                for q in range(2):
                    act.wait_ge(p3, 2 * t + q + 1)
                    act.activation(em[:, b, 4 * q:4 * q + 4, 0, :], em[:, b, 4 * q:4 * q + 4, 0, :], ACT.Exp).then_inc(exp_done, 1)

            def keep_max(t, b):
                act.wait_ge(mtr_done, t + 1)
                act.nop(nofuse=True)
                act.activation(mt[:, :, bass.ds(t * P, P)], bank[6][:, 0:2 * P].rearrange("p (h g) -> p h g", h=2),
                               ACT.Copy).then_inc(mev_done, 1)

            def keep_sums(t, b, i):
                act.wait_ge(sum_done, t + 1)
                ge(act, spill_out[b], 16 * i)
                act.activation(spb[:, b, C:3 * C], bank[5][:, :], ACT.Copy).then_inc(sev_done, 1)

            def step(t, b, i, before=3, left=3):
                if left >= 2:
                    keep_turned(t + 2, (b + 2) % 3)
                if before >= 1:
                    keep_max(t - 1, (b + 2) % 3)
                if before >= 2:
                    keep_sums(t - 2, (b + 1) % 3, i - 1 if b < 2 else i)
                exps(t, b)
                if left >= 3:
                    flags(t + 3, b, i + 1)

            for t in range(3):
                flags(t, t, 0)
                if t < 2:
                    keep_turned(t, t)
            for t in range(6):
                step(t, t % 3, t // 3, t)
            with act.Fori(2, T // 3 - 1) as i:
                for b in range(3):
                    step(3 * i + b, b, i)
            for b in range(3):
                step(T - 3 + b, b, T // 3 - 1, 3, 2 - b)
            keep_max(T - 1, 2)
            keep_sums(T - 2, 1, T // 3 - 1)
            keep_sums(T - 1, 2, T // 3 - 1)

            act.wait_ge(scan_done, 4)

            def maxima(k, b):
                ge(act, mtb_done, k - 2)
                act.nop(nofuse=True)
                tile = act.value_load(step_tile[0:1, bass.ds(k, 1)], min_val=0, max_val=T - 1)
                act.nop(nofuse=True)
                act.activation(mc[:, b, :, :], mt[:, :, bass.ds(tile * P, P)], ACT.Copy).then_inc(mc_done, 1)

            def factors(k, b):
                act.wait_ge(sub_done, k + 1)
                act.activation(md[:, b, 0:C], md[:, b, 0:C], ACT.Exp).then_inc(wexp_done, 1)

            for k in range(3):
                maxima(k, k)
            for k in range(3):
                maxima(k + 3, k)
                factors(k, k)
            with act.Fori(1, STEPS // 3 - 1) as i:
                for b in range(3):
                    maxima(3 * i + b + 3, b)
                    factors(3 * i + b, b)
            for b in range(3):
                factors(STEPS - 3 + b, b)
            act.wait_ge(ln_var, 1)
            act.activation(st2[:, :], st1[:, :], ACT.Sqrt).then_inc(ln_sd, 1)

            act.wait_ge(zero_ready, 1)
            act.sem_inc(lo_ready, 1)

            def keep_counts(w, b):
                act.wait_ge(win_ps, w + 1)
                act.nop(nofuse=True)
                act.activation(cnt[:, :, bass.ds(w * WIN, WIN)],
                               bank[b][:, 0:CW].rearrange("p (n h) -> p h n", h=NT), ACT.Copy).then_inc(win_ev, 1)

            def windows(v, first=False):
                units = window_units(mybir.EngineType.Activation, v)
                for b in range(WG):
                    w = WG * v + b
                    with act.Fori(units[b], units[b + 1] + 1) as i:
                        act.wait_ge(lo_ready, i + w + 1)
                        act.nop(nofuse=True)
                        for q in range(1, EU):
                            act.activation(hot_sq[:, q - 1, :], iota_lo[:, :], ACT.Square,
                                           bias=minus_lo[:, bass.ds(EU * i + q, 1)]).then_inc(sq_done, 1)
                        act.wait_ge(sq_done, (EU - 1) * (i + w + 1))
                        act.wait_ge(hot_used, EU * (i + w + 1))
                        act.activation(hot_lo[:, 1:EU, :], hot_sq[:, :, :], ACT.Relu, bias=one_col[:, :], scale=-1.0).then_inc(lo_ready, 1)
                    if b >= 1 or not first:
                        keep_counts(w - 1, (b + 3) % 4)

            windows(0, True)
            with act.Fori(1, NW // WG) as v:
                windows(v)
            keep_counts(NW - 1, 3)

            for c in range(2):
                for q in range(NB + 1):
                    if q < NB:
                        k, n = c * NB + q, BLOCKS[q][1]
                        act.wait_ge(xt_ps, k + 1)
                        ge(act, hid_ps, k - 1)
                        act.activation(xt[:, k % 2, 0:n], bank[k % 2][0:F, 0:n], ACT.Copy).then_inc(xt_ev, 1)
                        act.wait_ge(conv_ps, k + 1)
                        act.activation(agg[:, k % 2, 0:n], bank[2 + k % 2][0:3 * F, 0:n], ACT.Copy).then_inc(conv_ev, 1)
                    if q >= 1:
                        k, n = c * NB + q - 1, BLOCKS[q - 1][1]
                        act.wait_ge(hid_ps, k + 1)
                        ge(act, map2, k - 1)
                        act.activation(ut[:, k % 2, 0:n], bank[4 + k % 2][0:F, 0:n], ACT.Relu, bias=gba[:, c:c + 1]).then_inc(hid_ev, 1)
            act.wait_ge(lsm_e, 1)
            act.activation(hn[:, :, :], hn2[:, :, :], ACT.Exp).then_inc(lsm_s, 1)
            act.wait_ge(lsm_e, 2)
            act.activation(st2[:, :], st1[:, :], ACT.Ln).then_inc(lsm_l, 1)
            act.wait_ge(ln_var, 2)
            act.activation(st2[:, :], st1[:, :], ACT.Sqrt).then_inc(ln_sd, 1)

        @block.vector
        def _(dve):
            done = [0]

            def link(ins):
                done[0] += 1
                ins.then_inc(dve_step, 1)
                dve.wait_ge(dve_step, done[0])

            dve.wait_ge(const_ready, 4)
            dve.wait_ge(in_last, 16)
            dve.tensor_copy(rl_f[:, 0:SROWS], rl_i[:, :]).then_inc(last_ready, 1)
            dve.wait_ge(last_bcast, 1)
            link(dve.tensor_copy(rl_b[:, :], bank[0][:, 0:SROWS]))
            link(dve.tensor_tensor(less[:, :, :], rl_b[:, :].unsqueeze(1).to_broadcast([P, NT, SROWS]),
                                   node_id[:, :].unsqueeze(2).to_broadcast([P, NT, SROWS]), ALU.is_lt))
            link(dve.tensor_reduce(found_r[:, :], less[:, :, :], AX.X, ALU.add))
            dve.tensor_copy(found_i[:, :], found_r[:, :]).then_inc(rows_found, 1)
            dve.wait_ge(in_src, 16)

            def split_rows(c):
                b = c % 2
                dve.wait_ge(rows_high, c + 1)
                ge(dve, rows_mid, c)
                ge(dve, rows_done, 2 * c)
                dve.tensor_tensor(resid[:, :, :], ef_in[:, b, :, :], rows[:, b, :, 0:F], ALU.subtract).then_inc(rows_resid, 1)
                dve.tensor_copy(rows[:, b, :, :].rearrange("p e r -> p (e r)").bitcast(I32)
                                .rearrange("p (e r) -> p e r", e=PC)[:, :, KROWS // 2], src_i[:, c, :]).then_inc(rows_done, 1)
                dve.wait_ge(rows_mid, c + 1)
                dve.tensor_tensor(rows[:, b, :, 5 * F:6 * F], resid[:, :, :], rows[:, b, :, 3 * F:4 * F],
                                  ALU.subtract).then_inc(rows_done, 1)

            for c in range(3):
                split_rows(c)
            dve.wait_ge(search_in, 16 * NT)
            link(dve.tensor_tensor(less[:, :, 0:SR], srow[:, :, :],
                                   node_id[:, :].unsqueeze(2).to_broadcast([P, NT, SR]), ALU.is_lt))
            link(dve.tensor_reduce(start_nm[:, :], less[:, :, 0:SR], AX.X, ALU.add))
            dve.scalar_tensor_tensor(out=start_nm[:, :], in0=found_r[:, :], scalar=float(SR), in1=start_nm[:, :],
                                     op0=ALU.mult, op1=ALU.add).then_inc(start_ready, 1)
            dve.wait_ge(start_turned, 1)
            dve.tensor_copy(start_t[:, :], bank[1][0:NT, 0:P]).then_inc(start_kept, 1)
            split_rows(3)
            dve.wait_ge(row_in, 32)
            link(dve.tensor_tensor(r_c[:, :], r_b[:, :], r_a[:, 0:NP], ALU.subtract))
            link(dve.tensor_scalar(r_i[:, :], r_c[:, :], float(G - 1), None, ALU.add))
            link(dve.tensor_scalar(r_i[:, :], r_i[:, :], 3, None, ALU.arith_shift_right))
            link(dve.tensor_copy(r_b[:, :], r_i[:, :]))
            link(dve.tensor_scalar(r_c[:, :], r_c[:, :], 0.0, float(2 * S), ALU.is_equal, ALU.mult))
            link(dve.tensor_tensor_scan(r_g[:, :], r_b[:, :], r_b[:, :], 0.0, ALU.add, ALU.max))
            link(dve.tensor_copy(r_i[0:1, 0:NT], r_g[0:1, P - 1:NP:P]))
            link(dve.tensor_scalar(r_i[0:1, 0:NT], r_i[0:1, 0:NT], 7, None, ALU.arith_shift_right))
            wstart, wq, wt = (rl_f[:, k * (NW + 1):(k + 1) * (NW + 1)] for k in range(3))
            link(dve.tensor_copy(wstart, r_a[0:1, 0:NP + 1:WIN]))
            link(dve.tensor_scalar(win_unit[:, :], wstart, 1.0 / (EU * P), None, ALU.mult))
            link(dve.tensor_copy(wq, win_unit[:, :]))
            link(dve.scalar_tensor_tensor(out=wt, in0=wq, scalar=float(EU * P), in1=wstart, op0=ALU.mult, op1=ALU.is_gt))
            link(dve.tensor_tensor(win_unit[:, :], wq, wt, ALU.subtract))
            link(dve.tensor_tensor(r_g[:, :], r_g[:, :], r_b[:, :], ALU.subtract))
            dve.tensor_tensor(r_c[:, :], r_c[:, :], r_g[:, :], ALU.add).then_inc(row_ready, 1)
            split_rows(4)
            dve.wait_ge(fill_ready, 3)
            link(dve.tensor_copy(kt_f[:, :], r_i[0:1, 0:NT]))
            link(dve.tensor_tensor(kt_f[:, :], kt_f[:, :], kst[:, 0:NT], ALU.add))
            link(dve.tensor_tensor(kcmp[:, :, :], kt_f[:, :].unsqueeze(1).to_broadcast([1, STEPS, NT]),
                                   kst[:, :].unsqueeze(2).to_broadcast([1, STEPS, NT]), ALU.is_lt))
            link(dve.tensor_reduce(kwin[:, :], kcmp[:, :, :], AX.X, ALU.add))
            link(dve.tensor_copy(step_win[:, :], kwin[:, :]))
            link(dve.tensor_tensor(kst[:, :], kst[:, :], kwin[:, :], ALU.subtract))
            link(dve.tensor_scalar(step_tile[:, :], kst[:, :], float(T - 1), None, ALU.min))
            dve.tensor_scalar(kwin[:, :], kwin[:, :], float(P), None, ALU.mult).then_inc(wk_ready, 1)
            dve.wait_ge(nm_turned, 1)
            nmv = bank[2][:, 0:4 * NT].rearrange("p (k t) -> p k t", k=4)
            link(dve.tensor_copy(pay[:, :, 0], node_id[:, :]))
            link(dve.tensor_copy(pay[:, :, 1], nmv[:, 3, :]))
            link(dve.tensor_copy(pay[:, :, 2], nmv[:, 2, :]))
            link(dve.tensor_copy(pay[:, :, 3], nmv[:, 0, :]))
            dve.tensor_copy(slot_i[:, :], nmv[:, 1, :]).then_inc(scatter_ready, 1)
            dve.wait_ge(w_in, 64)
            link(dve.tensor_copy(wh[:, 0, :], wf[:, :]))
            link(dve.tensor_tensor(wf[:, :], wf[:, :], wh[:, 0, :], ALU.subtract))
            link(dve.tensor_copy(wh[:, 1, :], wf[:, :]))
            dve.tensor_tensor(wh[:, 2, :], wf[:, :], wh[:, 1, :], ALU.subtract).then_inc(w_split, 1)
            dve.wait_ge(er_in, 96)
            link(dve.tensor_scalar(eh[:, :, :], er[:, 0, :, :], 7, None, ALU.arith_shift_right))
            link(dve.tensor_scalar(erf[:, 0, :, :], er[:, 1, :, :], float(NT), None, ALU.mult))
            link(dve.tensor_tensor(erf[:, 0, :, :], erf[:, 0, :, :], eh[:, :, :], ALU.add))
            link(dve.tensor_scalar(eh[:, :, :], er[:, 0, :, :], P - 1, None, ALU.bitwise_and))
            dve.tensor_copy(erf[:, 1, :, :], eh[:, :, :]).then_inc(er_ready, 1)
            for c in range(5, PREP):
                split_rows(c)
            dve.wait_ge(table_in, 16)
            for k in range(4):
                link(dve.tensor_tensor_scan(gs[:, k, :], gt[:, :, k], gt[:, :, k], 0.0, ALU.max, ALU.max))
            dve.tensor_copy(carry[:, :], gs[:, :, P - 1]).then_inc(carry_ready, 1)
            link(dve.memset(carry_r[:, 0:1], 0.0))
            dve.wait_ge(carry_turned, 1)
            link(dve.tensor_copy(carry_r[:, 1:T + 1], bank[3][0:4, 0:T]))
            dve.tensor_tensor_scan(carry_r[:, :], carry_r[:, :], carry_r[:, :], 0.0, ALU.max, ALU.max).then_inc(carry_scanned, 1)
            dve.wait_ge(carry_back, 1)
            link(dve.tensor_copy(carry_b[:, :], bank[4][0:T, 0:4]))
            for k in range(3):
                link(dve.tensor_scalar(gs[:, k, :], gs[:, k, :], carry_b[:, k:k + 1], None, ALU.max))
            dve.tensor_scalar(gs[:, 3, :], gs[:, 3, :], carry_b[:, 3:4], None, ALU.max).then_inc(owner_ready, 1)
            dve.wait_ge(owner_in, 16)
            link(dve.tensor_tensor(own_p[:, :], own_p[:, :], gs[:, 0, :], ALU.not_equal))
            dve.tensor_scalar(fence_r[:, :], own_p[:, :], -FAR, None, ALU.mult).then_inc(fence_ready, 1)
            dve.wait_ge(owners_turned, 1)
            link(dve.tensor_copy(gm[:, :, :], bank[5][:, 0:4 * T].rearrange("p (k t) -> p k t", k=4)))
            link(dve.tensor_copy(own_t[:, :], gm[:, 0, :]))
            link(dve.tensor_tensor(gid[:, :], gid[:, :], gm[:, 3, :], ALU.subtract))
            link(dve.scalar_tensor_tensor(out=estf[:, :], in0=gid[:, :], scalar=float(G), in1=gm[:, 1, :], op0=ALU.mult, op1=ALU.add))
            link(dve.memset(est_i[:, T:T + 1], 0))
            link(dve.tensor_scalar(est_i[:, 0:T], estf[:, :], float(E), None, ALU.min))
            link(dve.tensor_tensor(eslot[:, :, :], eslot[:, :, :], estf[:, :].unsqueeze(2).to_broadcast([P, T, G]), ALU.add))
            link(dve.tensor_tensor(eslot[:, :, :], eslot[:, :, :], gm[:, 2, :].unsqueeze(2).to_broadcast([P, T, G]), ALU.is_ge))
            link(dve.tensor_scalar(empty[:, :], eslot[:, :, :].rearrange("p t g -> p (t g)"), float(FLAG), None, ALU.mult))
            dve.wait_ge(wk_bcast, 1)
            link(dve.tensor_copy(step_w128[:, :], bank[6][:, 0:STEPS]))
            dve.wait_ge(er_turned, 1)
            link(dve.tensor_copy(kb[:, 0:512], bank[0][:, :]))
            link(dve.tensor_copy(kb[:, 512:ET], bank[1][:, 0:ET - 512]))
            link(dve.tensor_copy(lo[:, 0:512], bank[7][:, :]))
            link(dve.tensor_copy(lo[:, 512:ET], bank[3][:, 0:ET - 512]))
            dve.wait_ge(w_out, 16 * 10)
            dve.wait_ge(fence_out, 32)
            for c in range(2):
                dve.wait_ge(rows_out[c], 16 * PREP // 2)
            dve.sem_inc(tables_ready, 1)

            def scores(t, b, i):
                dve.wait_ge(h_in[b], 16 * G * (i + 1))
                ge(dve, sum_done, t - 2)
                for j in range(G):
                    dve.wait_ge(mm_done, G * t + j + 1)
                    dve.tensor_tensor(em[:, b, j, :, :].rearrange("p a (i o) -> p a i o", i=F),
                                      bank[j % 4][:, :].rearrange("p (a i o) -> p a i o", a=2, i=F),
                                      hb[:, b, j, :].unsqueeze(1).unsqueeze(3).to_broadcast([P, 2, F, F]),
                                      ALU.mult).then_inc(p1, 1)

            def weigh(t, b, q):
                dve.wait_ge(exp_done, 2 * t + q + 1)
                dve.tensor_tensor(em[:, b, 4 * q:4 * q + 4, 1, :], em[:, b, 4 * q:4 * q + 4, 1, :],
                                  em[:, b, 4 * q:4 * q + 4, 0, :], ALU.mult).then_inc(p5, 1)

            def step(t, b, i, before=3):
                scores(t, b, i)
                dve.wait_ge(p1, G * t + G)
                dve.tensor_tensor(mx[:, :, :], em[:, b, 0:2, 0, :], em[:, b, 2:4, 0, :], ALU.max).then_inc(p2, 1)
                for q in range(2):
                    if before >= 1:
                        weigh(t - 1, (b + 2) % 3, q)
                    dve.wait_ge(p2, 4 * t + q + 1)
                    dve.tensor_tensor(mx[:, :, :], mx[:, :, :], em[:, b, 4 + 2 * q:6 + 2 * q, 0, :], ALU.max).then_inc(p2, 1)
                dve.wait_ge(p2, 4 * t + 3)
                ge(dve, mtr_done, t - 2)
                ge(dve, spill_out[b], 16 * i)
                dve.tensor_tensor(spb[:, b, 0:C], mx[:, 0, :], mx[:, 1, :], ALU.max).then_inc(p2, 1)
                dve.wait_ge(p2, 4 * t + 4)
                for q in range(2):
                    dve.tensor_tensor(em[:, b, 4 * q:4 * q + 4, 0, :], em[:, b, 4 * q:4 * q + 4, 0, :],
                                      spb[:, b, 0:C].unsqueeze(1).to_broadcast([P, 4, C]), ALU.subtract).then_inc(p3, 1)

            for t in range(3):
                step(t, t, 0, t)
            with dve.Fori(1, T // 3) as i:
                for b in range(3):
                    step(3 * i + b, b, i)
            for q in range(2):
                weigh(T - 1, 2, q)

            dve.wait_ge(fence_in, 16)
            dve.wait_ge(mev_done, T)
            for h in range(2):
                dve.tensor_tensor_scan(mt[:, h, :], fence[:, 0:S], mt[:, h, :], 0.0, ALU.add, ALU.max).then_inc(scan_done, 1)
            for h in range(2):
                dve.wait_ge(scan_done, h + 1)
                dve.tensor_tensor_scan(mt[:, h, ::-1], fence[:, S:0:-1], mt[:, h, ::-1], 0.0, ALU.add, ALU.max).then_inc(scan_done, 1)
            dve.wait_ge(scan_done, 4)
            link(dve.memset(acc[:, :, :], 0.0))

            def tile_factors(k, b, i):
                tile = dve.value_load(step_tile[0:1, bass.ds(k, 1)], min_val=0, max_val=T - 1)
                ge(dve, node_ps, k - 2)
                dve.nop(nofuse=True)
                dve.tensor_scalar(own_hot[:, b, :], iotaf[:, :], step_w128[:, bass.ds(k, 1)], own_t[:, bass.ds(tile, 1)],
                                  ALU.add, ALU.is_equal).then_inc(own_done, 1)
                dve.wait_ge(md_in[b], 16 * (i + 1))
                dve.wait_ge(mtb_done, k + 1)
                dve.tensor_tensor(md[:, b, 0:C], md[:, b, 0:C], bank[b][:, 0:C], ALU.subtract).then_inc(sub_done, 1)

            def scale(k, b):
                dve.wait_ge(wexp_done, k + 1)
                dve.wait_ge(own_done, k + 1)
                sums = md[:, b, C:3 * C].rearrange("p (a c) -> p a c", a=2)
                dve.tensor_tensor(sums, sums, md[:, b, 0:C].unsqueeze(1).to_broadcast([P, 2, C]), ALU.mult).then_inc(wmul_done, 1)

            def add_nodes(k, b):
                win = dve.value_load(step_win[0:1, bass.ds(k, 1)], min_val=0, max_val=NT)
                dve.wait_ge(node_ps, k + 1)
                ge(dve, node_add, k)
                dve.nop(nofuse=True)
                node = acc[:, bass.ds(win, 1), :].rearrange("p a c -> p (a c)")
                dve.tensor_tensor(node, node, bank[3 + b][:, :], ALU.add).then_inc(node_add, 1)

            def join(k, b, i):
                tile_factors(k, b, i)
                if not isinstance(k, int) or k >= 1:
                    scale(k - 1, (b + 2) % 3)
                if not isinstance(k, int) or k >= 2:
                    add_nodes(k - 2, (b + 1) % 3)

            for k in range(3):
                join(k, k, 0)
            with dve.Fori(1, STEPS // 3) as i:
                for b in range(3):
                    join(3 * i + b, b, i)
            scale(STEPS - 1, 2)
            for b in (1, 2):
                add_nodes(STEPS - 3 + b, b)
            dve.wait_ge(node_add, STEPS)
            den = acc[:, 0:NT, 0:C]
            num = acc[:, 0:NT, C:2 * C]
            link(dve.tensor_scalar(den, den, 0.5, None, ALU.max))
            link(dve.reciprocal(den, den))
            link(dve.tensor_tensor(num, num, den, ALU.mult))
            link(dve.tensor_reduce(hn2[:, :, :], num.rearrange("p t (i o) -> p t o i", i=F), AX.X, ALU.add))
            dve.wait_ge(in_x, 32)
            link(dve.tensor_tensor(hn2[:, :, :], hn2[:, :, :], x_sb[:, :, :], ALU.add))

            def layernorm(result, n, ready):
                link(dve.tensor_reduce(st1[:, :], hn2[:, :, :], AX.X, ALU.add))
                link(dve.tensor_scalar(st1[:, :], st1[:, :], 1.0 / F, None, ALU.mult))
                link(dve.tensor_tensor(hn2[:, :, :], hn2[:, :, :], st1[:, :].unsqueeze(2).to_broadcast([P, NT, F]), ALU.subtract))
                link(dve.tensor_tensor(hn[:, :, :], hn2[:, :, :], hn2[:, :, :], ALU.mult))
                link(dve.tensor_reduce(st1[:, :], hn[:, :, :], AX.X, ALU.add))
                link(dve.tensor_scalar(st1[:, :], st1[:, :], 1.0 / F, EPS, ALU.mult, ALU.add))
                dve.sem_inc(ln_var, 1)
                dve.wait_ge(ln_sd, n)
                link(dve.reciprocal(st2[:, :], st2[:, :]))
                link(dve.tensor_tensor(result[:, :, :], hn2[:, :, :], st2[:, :].unsqueeze(2).to_broadcast([P, NT, F]), ALU.mult))
                dve.sem_inc(ready, 1)

            layernorm(x1, 1, x1_ready)

            link(dve.memset(one_col[:, :], 1.0))
            link(dve.tensor_scalar(minus_lo[:, :], lo[:, :], -1.0, None, ALU.mult))
            dve.memset(zero_b[:, :], 0.0).then_inc(zero_ready, 1)
            dve.sem_inc(hot_used, EU)
            with dve.Fori(0, NW // WG) as v:
                units = window_units(mybir.EngineType.DVE, v)
                for b in range(WG):
                    w = WG * v + b
                    with dve.Fori(units[b], units[b + 1] + 1) as i:
                        for q in range(EU):
                            dve.wait_ge(hot_used, EU * (i + w) + q + 1)
                            dve.nop(nofuse=True)
                            if q == 0:
                                dve.tensor_scalar(hot_lo[:, 0, :], iota_lo[:, :], minus_lo[:, bass.ds(EU * i, 1)], 0.0,
                                                  ALU.add, ALU.is_equal)
                            dve.tensor_scalar(hot_key[:, q, :], iota_key[:, :], w500[:, bass.ds(w, 1)],
                                              kb[:, bass.ds(EU * i + q, 1)], ALU.add, ALU.is_equal).then_inc(hot_ready, 1)

            dve.wait_ge(win_ev, NW)
            dve.wait_ge(gin_in, 16 * 16)
            link(dve.tensor_scalar(geps[:, :], geps[:, :], 1.0, None, ALU.add))
            for c in range(2):
                link(dve.tensor_scalar(gwe[:, c, :], gwe[:, c, :], geps[:, c:c + 1], None, ALU.mult))
            hps = bank[7][:, 0:NT * F].rearrange("p (t f) -> p t f", f=F)
            for c, feat in enumerate((x1, hn)):
                link(dve.tensor_copy(xs[:, :, 0, :], feat[:, :, :]))
                link(dve.tensor_tensor(xr[:, :, :], feat[:, :, :], xs[:, :, 0, :], ALU.subtract))
                link(dve.tensor_copy(xs[:, :, 1, :], xr[:, :, :]))
                dve.tensor_tensor(xs[:, :, 2, :], xr[:, :, :], xs[:, :, 1, :], ALU.subtract).then_inc(xs_ready, 1)
                dve.wait_ge(map2, (c + 1) * NB)
                if c == 0:
                    link(dve.tensor_scalar(hn[:, :, :], hps, 0.0, None, ALU.max))
            link(dve.tensor_copy(hn2[:, :, :], hps))
            link(dve.tensor_reduce(st1[:, :], hn2[:, :, :], AX.X, ALU.max))
            dve.tensor_tensor(hn2[:, :, :], hn2[:, :, :], st1[:, :].unsqueeze(2).to_broadcast([P, NT, F]),
                              ALU.subtract).then_inc(lsm_e, 1)
            dve.wait_ge(lsm_s, 1)
            dve.tensor_reduce(st1[:, :], hn[:, :, :], AX.X, ALU.add).then_inc(lsm_e, 1)
            dve.wait_ge(lsm_l, 1)
            link(dve.tensor_tensor(hn2[:, :, :], hn2[:, :, :], st2[:, :].unsqueeze(2).to_broadcast([P, NT, F]), ALU.subtract))
            link(dve.tensor_tensor(hn2[:, :, :], hn2[:, :, :], x1[:, :, :], ALU.add))
            layernorm(hn, 2, y_ready)


def kernel(**inputs):
    import numpy as np
    import concourse.bacc as bacc
    from concourse.bass_utils import run_bass_kernel_spmd

    nc = bacc.Bacc("TRN2", target_bir_lowering=False, num_devices=1)
    arrays, a = {}, {}
    for name, value in inputs.items():
        v = np.ascontiguousarray(value)
        if v.ndim == 0:
            v = v.reshape(1)
        arrays[f"in_{name}"] = v
        a[name] = nc.dram_tensor(f"in_{name}", v.shape, mybir.dt.from_np(v.dtype), kind="ExternalInput").ap()
    out = nc.dram_tensor("out_0", (N, F), F32, kind="ExternalOutput").ap()
    gin = [tuple(a[f"L1_gnn_{k}"] for k in (f"w{c}a", f"b{c}a", f"w{c}b", f"b{c}b", f"eps{c}")) for c in (1, 2)]
    program(nc, a["x"], a["src"], a["dst"], a["edge_attr_16"], a["L0_gnn_W_msg"], a["L0_gnn_b_msg"],
            a["L0_gnn_W_attn"], a["L0_gnn_b_attn"], gin, out)
    r = run_bass_kernel_spmd(nc, [arrays], core_ids=[0])
    return r.results[0]["out_0"]
```

```python
from contextlib import ExitStack

import concourse.bass as bass
from concourse import mybir

F32 = mybir.dt.float32
BF16 = mybir.dt.bfloat16
FP16 = mybir.dt.float16
I32 = mybir.dt.int32
ALU = mybir.AluOpType
ACT = mybir.ActivationFunctionType
AX = mybir.AxisListType

P = 128
N = 3125
E = 100000
F = 16
C = F * F
NT = -(-N // P)
NP = NT * P
G = 8
GROUPS = (E + N * (G - 1)) // G
T = -(-GROUPS // (3 * P)) * 3
S = T * P
ROW = 102
KROWS = 100
SR = 256
SROWS = -(-E // SR)
STEPS = -(-(T + NT) // 4) * 4
WIN = 20
NW = NP // WIN
WG = 16
CW = WIN * NT
EU = 3
UNITS = -(-E // (EU * P))
ET = UNITS * EU
LOOPS = ((E // G) // (3 * P) + 1, T // 3)
JOINS = ((E // G // P + NT + 3) // 4, STEPS // 4)
CH = 3 * P
BIG = 1.0e30
FAR = 3.0e38
FLAG = N
PREP = 8
PP = 125
PC = E // PP // PREP
EPS = 1e-5
EXACT = 256
BLOCKS = [(n0, min(512, NP - n0)) for n0 in range(0, NP, 512)]
NB = len(BLOCKS)
assert GROUPS <= S and PP * PC * PREP == E and NW % WG == 0 and NW * WIN == NP


def ge(eng, sema, value):
    if not isinstance(value, int) or value > 0:
        eng.wait_ge(sema, value)


def program(nc, x, src, dst, ef, w_msg, b_msg, w_att, b_att, gin, out):
    with ExitStack() as ctx:
        def sem(name):
            return ctx.enter_context(nc.semaphore(name))

        def sb(name, shape, dt, at=ctx):
            return at.enter_context(nc.sbuf_tensor(name, shape, dt))

        def dram(name, shape, dt):
            return nc.dram_tensor(name, shape, dt).ap()

        edge_rows = dram("edge_rows", (E + G, ROW), BF16)
        x_table = dram("x_table", (FLAG + N, F), F32)
        dst_rows = dram("dst_rows", (SROWS, SR), I32)
        start_row_d = dram("start_row_d", (NP + 8,), F32)
        g0_row_d = dram("g0_row_d", (NP,), F32)
        slot_row_d = dram("slot_row_d", (NP,), F32)
        group_table = dram("group_table", (S, 4), F32)
        owner_d = dram("owner_d", (S + 1,), F32)
        fence_d = dram("fence_d", (S + 1,), BF16)
        left_d = dram("left_d", (NW, P, CW), BF16)
        extra_d = dram("extra_d", (3 * F, NP), F32)
        group_sums = dram("group_sums", (T, P, 3 * C), F32)

        bank = [ctx.enter_context(nc.psum_tensor(f"bank{i}", [P, 512], F32)) for i in range(8)]
        turned = bank[4][:, :].bitcast(BF16)

        identf = sb("identf", [P, P], F32)
        identb = sb("identb", [P, P], BF16)
        iotaf = sb("iotaf", [P, P], F32)
        iota_key = sb("iota_key", [P, CW], FP16)
        iota_lo = sb("iota_lo", [P, P], FP16)
        ones_row = sb("ones_row", [1, P], F32)
        w500 = sb("w500", [P, NW], F32)
        wst = sb("wst", [KROWS, 2 * C], BF16)
        counts = sb("counts", [1, 3], I32)
        step_tile = sb("step_tile", [1, STEPS], I32)
        step_win = sb("step_win", [1, STEPS], I32)
        step_own = sb("step_own", [P, STEPS], F32)
        win_unit = sb("win_unit", [1, NW + 1], I32)
        kb = sb("kb", [P, ET], F32)
        lo = sb("lo", [P, ET], BF16)

        setup = ExitStack()
        r_a = sb("r_a", [1, NP + 8], F32, setup)
        r_b = sb("r_b", [1, NP], F32, setup)
        r_c = sb("r_c", [1, NP], F32, setup)
        r_g = sb("r_g", [1, NP], F32, setup)
        r_i = sb("r_i", [1, NP], I32, setup)
        ef_in = sb("ef_in", [PP, 2, PC, F], F32, setup)
        resid = sb("resid", [PP, PC, F], F32, setup)
        rows = sb("rows", [PP, 2, PC, ROW], BF16, setup)
        src_i = sb("src_i", [PP, PREP, PC], I32, setup)
        node_id = sb("node_id", [P, NT], F32, setup)
        pads = sb("pads", [P, 512], F32, setup)
        ones_t = sb("ones_t", [PP, N * F // PP], F32, setup)
        pad_end = sb("pad_end", [1, 8], F32, setup)
        pads_i = sb("pads_i", [1, SR], I32, setup)
        found_r = sb("found_r", [P, NT], F32, setup)
        found_i = sb("found_i", [P, NT], I32, setup)
        start_nm = sb("start_nm", [P, NT], F32, setup)
        start_t = sb("start_t", [NT, P], F32, setup)
        search = ExitStack()
        rl_i = sb("rl_i", [1, SROWS], I32, search)
        rl_f = sb("rl_f", [1, max(SROWS, 3 * (NW + 1) + 2)], F32, search)
        rl_b = sb("rl_b", [P, SROWS], F32, search)
        less = sb("less", [P, NT, SROWS], BF16, search)
        srow = sb("srow", [P, NT, SR], I32, search)
        search.close()
        tables = ExitStack()
        nm4 = sb("nm4", [NT, 4, P], F32, tables)
        slot_i = sb("slot_i", [P, NT], I32, tables)
        pay = sb("pay", [P, NT, 4], F32, tables)
        gt = sb("gt", [T, P, 4], F32, tables)
        gs = sb("gs", [T, 4, P], F32, tables)
        carry = sb("carry", [T, 4], F32, tables)
        carry_r = sb("carry_r", [4, T + 1], F32, tables)
        carry_b = sb("carry_b", [T, 4], F32, tables)
        own_p = sb("own_p", [T, P], F32, tables)
        fence_r = sb("fence_r", [T, P], BF16, tables)
        fence_end = sb("fence_end", [1, 2], BF16, tables)
        minus_1 = sb("minus_1", [1, 2], F32, tables)
        gm = sb("gm", [P, 4, T], F32, tables)
        gid = sb("gid", [P, T], F32, tables)
        estf = sb("estf", [P, T], F32, tables)
        eslot = sb("eslot", [P, T, G], F32, tables)
        wf = sb("wf", [F + 1, 2 * C], F32, tables)
        wh = sb("wh", [F + 1, 3, 2 * C], BF16, tables)
        wflag = sb("wflag", [1, 2 * C], BF16, tables)
        kst = sb("kst", [1, STEPS], F32, tables)
        kcmp = sb("kcmp", [1, STEPS, NT], F32, tables)
        kwin = sb("kwin", [1, STEPS], F32, tables)
        tile_hot = sb("tile_hot", [T, STEPS], F32, tables)
        kt_i = sb("kt_i", [1, NT], I32, tables)
        kt_f = sb("kt_f", [1, NT], F32, tables)
        last_tile = sb("last_tile", [1, 1], F32, tables)
        er = sb("er", [P, 2, 7, P], I32, tables)
        eh = sb("eh", [P, 7, P], I32, tables)
        erf = sb("erf", [P, 2, 7, P], F32, tables)
        tables.close()
        setup.close()
        levels = ExitStack()
        mt = sb("mt", [P, 2, S], F32, levels)
        level1 = ExitStack()
        blk = sb("blk", [P, 3, G, ROW], BF16, level1)
        eft = sb("eft", [KROWS, 3, G, P], BF16, level1)
        hb = sb("hb", [P, 3, G, F], F32, level1)
        em = sb("em", [P, 3, G, 2, C], F32, level1)
        mx = sb("mx", [P, 2, C], F32, level1)
        spb = sb("spb", [P, 3, 3 * C], F32, level1)
        estc = sb("estc", [P, 3], I32, level1)
        idxi = sb("idxi", [P, 3, G], I32, level1)
        est_i = sb("est_i", [P, T + 1], I32, level1)
        empty = sb("empty", [P, T * G], I32, level1)
        level1.close()
        scans = ExitStack()
        fence = sb("fence", [P, S + 1], BF16, scans)
        scans.close()
        level2 = ExitStack()
        acc = sb("acc", [P, NT + 1, 2 * C], F32, level2)
        md = sb("md", [P, 4, 3 * C], F32, level2)
        mc = sb("mc", [P, 4, 2, P], F32, level2)
        own_hot = sb("own_hot", [P, 4, P], F32, level2)
        x1 = sb("x1", [P, NT, F], F32, level2)
        st1 = sb("st1", [P, NT], F32, level2)
        st2 = sb("st2", [P, NT], F32, level2)
        level2.close()
        levels.close()
        levelx = ExitStack()
        x_sb = sb("x_sb", [P, NT, F], F32, levelx)
        sum0 = sb("sum0", [P, NT, F], F32, levelx)
        square0 = sb("square0", [P, NT, F], F32, levelx)
        levelx.close()
        ginx = ExitStack()
        cnt = sb("cnt", [P, NT, NP], BF16, ginx)
        hot_lo = sb("hot_lo", [P, EU, P], BF16, ginx)
        hot_sq = sb("hot_sq", [P, EU - 1, P], BF16, ginx)
        minus_lo = sb("minus_lo", [P, ET], F32, ginx)
        hot_key = sb("hot_key", [P, EU, CW], BF16, ginx)
        one_col = sb("one_col", [P, 1], F32, ginx)
        zero_b = sb("zero_b", [P, CW], BF16, ginx)
        xs = sb("xs", [P, NT, 3, F], BF16, ginx)
        xr = sb("xr", [P, NT, F], F32, ginx)
        xt = sb("xt", [F, 2, 512], F32, ginx)
        agg = sb("agg", [3 * F, 2, 512], F32, ginx)
        ut = sb("ut", [F + 1, 2, 512], F32, ginx)
        gw = sb("gw", [3 * F, 2, F], F32, ginx)
        gwe = sb("gwe", [F, 2, F], F32, ginx)
        gb = sb("gb", [F + 1, 2, F], F32, ginx)
        gba = sb("gba", [F, 2], F32, ginx)
        geps = sb("geps", [F, 2], F32, ginx)
        left = sb("left", [P, CW], BF16, ginx)
        left_any = sb("left_any", [P, CW], BF16, ginx)
        left_p = sb("left_p", [P, 1], F32, ginx)
        left_1 = sb("left_1", [1, 1], F32, ginx)
        flag = sb("flag", [1, 1], I32, ginx)
        left_sums = sb("left_sums", [3 * F, WIN], F32, ginx)
        extra = sb("extra", [3 * F, 512], F32, ginx)
        hn = sb("hn", [P, NT, F], F32, ginx)
        hn2 = sb("hn2", [P, NT, F], F32, ginx)
        ginx.close()

        (
            const_ready, pool_step, dve_step, in_x, in_last, in_src, pad_out, last_ready, last_bcast,
            rows_found, search_in, start_ready, start_turned, start_kept, start_out, row_in, row_ready,
            row_out, nm_in, nm_turned, scatter_ready, scattered, table_in, carry_ready, carry_turned,
            carry_scanned, carry_back, owner_ready, owner_out, owner_in, fence_ready, fence_out,
            owners_turned, tables_ready, w_in, w_split, w_out, wk_ready, wk_bcast, er_in, er_ready, er_turned,
            fill_ready, rows_high, rows_resid, rows_mid, rows_done, x_out, pre_fill, flag_done, rows_turned,
            eft_done, slot_product, slot_scored, max_taken, shifted, exp_done, weighed, sum_done, max_turned,
            max_kept, sums_kept, fence_in, scan_done, back_done, scans_ready, mc_done, node_max_turned,
            sub_done, wexp_done, wmul_done, own_done, node_ps, node_add, ln_var, ln_sd, x1_ready, hot_ready,
            hot_used, win_ps, win_ev, gin_in, xs_ready, conv_ps, conv_ev, xt_ps, xt_ev, hid_ps, hid_ev, map2,
            lsm_e, lsm_s, lsm_l, y_ready, out_done, zero_ready, x_zero, lo_ready, sq_done, acc_zero,
            tile_hot_ready, step_owners, left_ready, left_or, left_out, left_past, any_ready, any_turned,
            flag_ready, zeros_out, left_in, left_ps, left_kept, sums_out, extra_in, agg_ready
        ) = [sem(n) for n in (
            "const_ready pool_step dve_step in_x in_last in_src pad_out last_ready last_bcast rows_found "
            "search_in start_ready start_turned start_kept start_out row_in row_ready row_out nm_in nm_turned "
            "scatter_ready scattered table_in carry_ready carry_turned carry_scanned carry_back owner_ready "
            "owner_out owner_in fence_ready fence_out owners_turned tables_ready w_in w_split w_out wk_ready "
            "wk_bcast er_in er_ready er_turned fill_ready rows_high rows_resid rows_mid rows_done x_out pre_fill "
            "flag_done rows_turned eft_done slot_product slot_scored max_taken shifted exp_done weighed sum_done "
            "max_turned max_kept sums_kept fence_in scan_done back_done scans_ready mc_done node_max_turned "
            "sub_done wexp_done wmul_done own_done node_ps node_add ln_var ln_sd x1_ready hot_ready hot_used "
            "win_ps win_ev gin_in xs_ready conv_ps conv_ev xt_ps xt_ev hid_ps hid_ev map2 lsm_e lsm_s lsm_l "
            "y_ready out_done zero_ready x_zero lo_ready sq_done acc_zero tile_hot_ready step_owners left_ready "
            "left_or left_out left_past any_ready any_turned flag_ready zeros_out left_in left_ps left_kept "
            "sums_out extra_in agg_ready").split()]
        ef_ld = [sem(f"ef_ld{i}") for i in range(2)]
        rows_out = [sem(f"rows_out{i}") for i in range(2)]
        blk_in = [sem(f"blk_in{i}") for i in range(3)]
        h_in = [sem(f"h_in{i}") for i in range(3)]
        spill_out = [sem(f"spill_out{i}") for i in range(3)]
        md_in = [sem(f"md_in{i}") for i in range(4)]

        def loops(eng):
            return eng.value_load(counts[0:1, 0:1], min_val=LOOPS[0] - 3, max_val=LOOPS[1] - 3) + 3

        def joins(eng):
            return eng.value_load(counts[0:1, 1:2], min_val=JOINS[0] - 3, max_val=JOINS[1] - 3) + 3

        def dense_windows(eng):
            return eng.value_load(counts[0:1, 2:3], min_val=0, max_val=NW - 1) + 1

        def window_units(engine, v):
            return nc.values_load_multi_w_load_instructions(win_unit[0:1, bass.ds(WG * v, WG + 1)], [engine], min_val=0,
                                                            max_val=UNITS - 1)[1]

        block = ctx.enter_context(nc.Block())

        @block.sync
        def _(sp):
            sp.wait_ge(const_ready, 4)
            with nc.allow_non_contiguous_dma(reason="the last destination of each search row"):
                sp.dma_start(rl_i[0:1, 0:SROWS - 1],
                             dst[0:(SROWS - 1) * SR].rearrange("(a r c) -> a r c", a=1, c=SR)[:, :, SR - 1]).then_inc(in_last, 16)
            last = E - (SROWS - 1) * SR
            sp.dma_start(dst_rows[0:SROWS - 1, :], dst[0:(SROWS - 1) * SR].rearrange("(r c) -> r c", c=SR)).then_inc(pad_out, 16)
            sp.dma_start(dst_rows[SROWS - 1:SROWS, 0:last], dst[(SROWS - 1) * SR:E].rearrange("(a c) -> a c", a=1)).then_inc(pad_out, 16)
            sp.dma_start(dst_rows[SROWS - 1:SROWS, last:SR], pads_i[0:1, 0:SR - last]).then_inc(pad_out, 16)
            sp.dma_start(x_table[0:N, :], x).then_inc(x_out, 16)
            sp.dma_start(x_table[FLAG:FLAG + N, :].rearrange("(p r) f -> p (r f)", p=PP), ones_t[:, :]).then_inc(x_out, 16)
            sp.dma_start(group_table.rearrange("(t p) k -> t (p k)", p=P), pads[0:T, 0:4 * P]).then_inc(x_out, 16)
            sp.dma_start(edge_rows[E:E + G, :].rearrange("(a e) r -> a (e r)", a=1),
                         pads[0:1, 0:G * ROW // 2].bitcast(BF16)).then_inc(x_out, 16)
            sp.wait_ge(start_kept, 1)
            sp.dma_start(start_row_d[0:NP].rearrange("(t p) -> t p", p=P), start_t[:, :]).then_inc(start_out, 16)
            sp.dma_start(start_row_d[NP:NP + 8].rearrange("(a p) -> a p", a=1), pad_end[0:1, :]).then_inc(start_out, 16)
            sp.wait_ge(start_out, 32)
            sp.dma_start(r_a[0:1, :], start_row_d.rearrange("(a p) -> a p", a=1)).then_inc(row_in, 16)
            sp.dma_start(r_b[0:1, :], start_row_d[1:NP + 1].rearrange("(a p) -> a p", a=1)).then_inc(row_in, 16)
            sp.wait_ge(row_ready, 1)
            sp.dma_start(g0_row_d.rearrange("(a p) -> a p", a=1), r_g[0:1, :]).then_inc(row_out, 16)
            sp.dma_start(slot_row_d.rearrange("(a p) -> a p", a=1), r_c[0:1, :]).then_inc(row_out, 16)
            sp.wait_ge(row_out, 32)
            sp.dma_start(nm4[:, 0, :], g0_row_d.rearrange("(t p) -> t p", p=P)).then_inc(nm_in, 16)
            sp.dma_start(nm4[:, 1, :], slot_row_d.rearrange("(t p) -> t p", p=P)).then_inc(nm_in, 16)
            sp.dma_start(nm4[:, 2, :], start_row_d[1:NP + 1].rearrange("(t p) -> t p", p=P)).then_inc(nm_in, 16)
            sp.dma_start(nm4[:, 3, :], start_row_d[0:NP].rearrange("(t p) -> t p", p=P)).then_inc(nm_in, 16)
            sp.wait_ge(scattered, 16 * NT)
            sp.dma_start(gt[:, :, :], group_table.rearrange("(t p) k -> t p k", p=P)).then_inc(table_in, 16)
            sp.wait_ge(owner_ready, 1)
            sp.dma_start(owner_d[1:S + 1].rearrange("(t p) -> t p", p=P), gs[:, 0, :]).then_inc(owner_out, 16)
            sp.dma_start(owner_d[0:1].rearrange("(a p) -> a p", a=1), minus_1[0:1, 0:1]).then_inc(owner_out, 16)
            sp.wait_ge(owner_out, 32)
            sp.dma_start(own_p[:, :], owner_d[0:S].rearrange("(t p) -> t p", p=P)).then_inc(owner_in, 16)
            sp.wait_ge(fence_ready, 1)
            sp.dma_start(fence_d[0:S].rearrange("(t p) -> t p", p=P), fence_r[:, :]).then_inc(fence_out, 16)
            sp.dma_start(fence_d[S:S + 1].rearrange("(a p) -> a p", a=1), fence_end[0:1, 0:1]).then_inc(fence_out, 16)

            def spill(t, b):
                sp.wait_ge(sums_kept, t + 1)
                sp.dma_start(group_sums[bass.ds(t, 1)].rearrange("a p c -> p (a c)"), spb[:, b, :]).then_inc(spill_out[b], 16)

            for t in range(3):
                spill(t, t)
            n3 = loops(sp)
            with sp.Fori(1, n3) as i:
                for b in range(3):
                    spill(3 * i + b, b)

            for b in range(3):
                sp.wait_ge(spill_out[b], 16 * n3)
            sp.wait_ge(fence_out, 32)
            sp.dma_start(fence[:, :], fence_d.rearrange("(a p) -> a p", a=1).to_broadcast([P, S + 1])).then_inc(fence_in, 16)
            sp.wait_ge(scans_ready, 1)

            def load(k, b):
                ge(sp, node_ps, k - 3)
                sp.nop(nofuse=True)
                tile = sp.value_load(step_tile[0:1, bass.ds(k, 1)], min_val=0, max_val=T - 1)
                sp.dma_start(md[:, b, :], group_sums[bass.ds(tile, 1)].rearrange("a p c -> p (a c)")).then_inc(md_in[b], 16)

            for k in range(4):
                load(k, k)
            with sp.Fori(1, joins(sp)) as i:
                for b in range(4):
                    load(4 * i + b, b)
            sp.wait_ge(x_zero, 1)
            sp.dma_start(x_sb[:, 0:NT - 1, :], x[0:(NT - 1) * P, :].rearrange("(t p) f -> p t f", p=P)).then_inc(in_x, 16)
            sp.dma_start(x_sb[0:N - (NT - 1) * P, NT - 1, :], x[(NT - 1) * P:N, :]).then_inc(in_x, 16)

            sp.wait_ge(x1_ready, 1)
            for c in range(2):
                wa, ba, wb, bb, eps = gin[c]
                for k in range(3):
                    sp.dma_start(gw[k * F:(k + 1) * F, c, :], wa).then_inc(gin_in, 16)
                sp.dma_start(gwe[:, c, :], wa).then_inc(gin_in, 16)
                sp.dma_start(gb[0:F, c, :], wb).then_inc(gin_in, 16)
                with nc.allow_non_contiguous_dma(reason="a bias of 16, one on each partition"):
                    sp.dma_start(gba[:, c:c + 1], ba.rearrange("(f a) -> f a", a=1)).then_inc(gin_in, 16)
                sp.dma_start(gb[F:F + 1, c, :], bb.rearrange("(a f) -> a f", a=1)).then_inc(gin_in, 16)
                sp.dma_start(geps[:, c:c + 1], eps.rearrange("(a f) -> a f", a=1).to_broadcast([F, 1])).then_inc(gin_in, 16)
            hw = dense_windows(sp)
            with sp.Fori(0, hw) as w:
                sp.wait_ge(left_ready, w + 1)
                sp.nop(nofuse=True)
                sp.dma_start(left_d[bass.ds(w, 1)].rearrange("a p c -> p (a c)"), left[:, :]).then_inc(left_out, 16)
            sp.wait_ge(flag_ready, 1)
            some = sp.value_load(flag[0:1, 0:1], min_val=0, max_val=1)
            with sp.If(some == 1):
                sp.wait_ge(left_out, 16 * hw + 16)
                sp.nop(nofuse=True)
                for k in range(NP // 200):
                    sp.dma_start(extra_d[:, k * 200:(k + 1) * 200], zero_b[0:3 * F, 0:400].bitcast(F32)).then_inc(zeros_out, 16)
                sp.wait_ge(zeros_out, 16 * (NP // 200))
                for c in range(2):
                    with sp.Fori(0, hw) as w:
                        sp.dma_start(left[:, :], left_d[bass.ds(w, 1)].rearrange("a p c -> p (a c)")).then_inc(left_in, 16)
                        sp.wait_ge(left_kept, hw * c + w + 1)
                        sp.nop(nofuse=True)
                        sp.dma_start(extra_d[:, bass.ds(w * WIN, WIN)], left_sums[:, :]).then_inc(sums_out, 16)
                        sp.wait_ge(sums_out, (hw * c + w) * 16 + 16)
                        sp.nop(nofuse=True)
                    for q, (n0, n) in enumerate(BLOCKS):
                        ge(sp, agg_ready, c * NB + q)
                        sp.dma_start(extra[:, 0:n], extra_d[:, n0:n0 + n]).then_inc(extra_in, 16)
            sp.wait_ge(y_ready, 1)
            sp.dma_start(out[0:(NT - 1) * P, :].rearrange("(t p) f -> p t f", p=P), hn[:, 0:NT - 1, :]).then_inc(out_done, 16)
            sp.dma_start(out[(NT - 1) * P:N, :], hn[0:N - (NT - 1) * P, NT - 1, :]).then_inc(out_done, 16)
            sp.wait_ge(out_done, 32)

        @block.gpsimd
        def _(pool):
            done = [0]

            def link(ins):
                done[0] += 1
                ins.then_inc(pool_step, 1)
                pool.wait_ge(pool_step, done[0])

            def iota(t, pattern, channel=0):
                link(pool.iota(t, pattern, base=0, channel_multiplier=channel, allow_small_or_imprecise_dtypes=True))

            link(pool.memset(pads[:, :], 0.0))
            link(pool.memset(pad_end[:, :], float(E)))
            link(pool.memset(pads_i[:, :], 2 * NP))
            link(pool.memset(rl_i[:, :], 2 * NP))
            link(pool.memset(ones_row[:, :], 1.0))
            link(pool.memset(ones_t[:, :], 1.0))
            iota(iotaf[:, :], [[1, P]])
            iota(iota_key[:, :], [[1, CW]])
            iota(iota_lo[:, :], [[1, P]])
            iota(node_id[:, :], [[P, NT]], 1)
            iota(w500[:, :], [[CW, NW]])
            for m in (identf, identb):
                link(pool.memset(m[:, :], 0.0))
                link(pool.affine_select(out=m[:, :], in_=m[:, :], compare_op=ALU.not_equal, fill=1.0, base=0,
                                        pattern=[[-1, P]], channel_multiplier=1))
            pool.sem_inc(const_ready, 4)
            pool.memset(rows[:, :, :, 96:99], 1.0).then_inc(pre_fill, 1)
            pool.memset(rows[:, :, :, 99:100], 0.0).then_inc(pre_fill, 1)
            pool.wait_ge(rows_found, 1)
            pool.wait_ge(pad_out, 48)
            for t in range(NT):
                pool.indirect_dma_start(srow[:, t, :], None, dst_rows,
                                        bass.IndirectOffsetOnAxis(ap=found_i[:, t:t + 1], axis=0)).then_inc(search_in, 16)
            pool.wait_ge(row_ready, 1)
            iota(gid[:, :], [[P, T]], 1)
            iota(eslot[:, :, :], [[0, T], [1, G]])
            iota(kst[:, :], [[1, STEPS]])
            link(pool.memset(wflag[:, 0:C], -BIG / FLAG))
            link(pool.memset(wflag[:, C:2 * C], 0.0))
            link(pool.memset(fence_end[:, :], -BIG))
            link(pool.memset(minus_1[:, :], -1.0))
            link(pool.memset(er[:, 0, :, :], 0))
            link(pool.memset(er[:, 1, :, :], -4 * NP))
            pool.sem_inc(fill_ready, 3)
            pool.wait_ge(scatter_ready, 1)
            pool.wait_ge(x_out, 64)
            for t in range(NT):
                pool.indirect_dma_start(group_table, bass.IndirectOffsetOnAxis(ap=slot_i[:, t:t + 1], axis=0),
                                        pay[:, t, :], None, bounds_check=S - 1, oob_is_err=False).then_inc(scattered, 16)

            pool.wait_ge(tables_ready, 1)
            base = done[0]

            def fetch(t, b):
                ge(pool, rows_turned, t - 2)
                pool.nop(nofuse=True)
                pool.tensor_copy(estc[:, b:b + 1], est_i[:, bass.ds(t, 1)]).then_inc(pool_step, 1)
                pool.wait_ge(pool_step, base + 1 if isinstance(t, int) and t == 0 else base + 2 * t)
                pool.nop(nofuse=True)
                pool.indirect_dma_start(blk[:, b, :, :].rearrange("p g r -> p (g r)"), None, edge_rows,
                                        bass.IndirectOffsetOnAxis(ap=estc[:, b:b + 1], axis=0)).then_inc(blk_in[b], 16)

            def gather(t, b, i):
                pool.wait_ge(blk_in[b], 16 * (i + 1))
                ge(pool, h_in[b], 16 * G * i)
                ge(pool, slot_scored, G * (t - 2))
                pool.nop(nofuse=True)
                srcs = blk[:, b, :, :].rearrange("p g r -> p (g r)").bitcast(I32)\
                    .rearrange("p (g r) -> p g r", g=G)[:, :, KROWS // 2]
                pool.tensor_tensor(idxi[:, b, :], srcs, empty[:, bass.ds(t * G, G)], ALU.add).then_inc(pool_step, 1)
                pool.wait_ge(pool_step, base + 2 * t + 3)
                pool.nop(nofuse=True)
                for j in range(G):
                    pool.indirect_dma_start(hb[:, b, j, :], None, x_table,
                                            bass.IndirectOffsetOnAxis(ap=idxi[:, b, j:j + 1], axis=0)).then_inc(h_in[b], 16)

            n3 = loops(pool)
            n4 = joins(pool)
            fetch(0, 0)
            for t in range(3):
                fetch(t + 1, (t + 1) % 3)
                gather(t, t, 0)
            with pool.Fori(1, n3) as i:
                for b in range(3):
                    fetch(3 * i + b + 1, (b + 1) % 3)
                    gather(3 * i + b, b, i)
            pool.wait_ge(blk_in[0], 16 * n3 + 16)
            pool.nop(nofuse=True)
            pool.wait_ge(fence_in, 16)
            past = -(-(S + 1) * 2 // (8 * C)) + 1
            pool.memset(acc[:, past:NT + 1, :], 0.0).then_inc(acc_zero, 1)
            pool.wait_ge(scans_ready, 1)
            pool.memset(acc[:, 2:past, :], 0.0).then_inc(acc_zero, 1)
            pool.wait_ge(mc_done, 4 * n4)
            pool.nop(nofuse=True)
            pool.memset(x_sb[:, :, :], 0.0).then_inc(x_zero, 1)

        @block.tensor
        def _(pe):
            pe.wait_ge(const_ready, 4)
            pe.wait_ge(last_ready, 1)
            pe.matmul(bank[0][:, 0:SROWS], ones_row[0:1, :], rl_f[0:1, 0:SROWS], start=True, stop=True).then_inc(last_bcast, 1)
            pe.wait_ge(start_ready, 1)
            pe.transpose(bank[1][0:NT, 0:P], start_nm[:, :], identf[:, :]).then_inc(start_turned, 1)
            pe.wait_ge(nm_in, 64)
            for k in range(4):
                mm = pe.transpose(bank[2][:, k * NT:(k + 1) * NT], nm4[:, k, :], identf[0:NT, 0:NT])
            mm.then_inc(nm_turned, 1)
            pe.wait_ge(wk_ready, 1)
            pe.matmul(bank[6][:, 0:STEPS], ones_row[0:1, :], kwin[0:1, :], start=True, stop=True)
            pe.matmul(bank[6][:, STEPS:2 * STEPS], ones_row[0:1, :], kst[0:1, :], start=True, stop=True).then_inc(wk_bcast, 1)
            pe.wait_ge(carry_ready, 1)
            pe.transpose(bank[3][0:4, 0:T], carry[:, :], identf[0:T, 0:T]).then_inc(carry_turned, 1)
            pe.wait_ge(carry_scanned, 1)
            pe.transpose(bank[4][0:T, 0:4], carry_r[:, 0:T], identf[0:4, 0:4]).then_inc(carry_back, 1)
            pe.wait_ge(owner_ready, 1)
            for k in range(4):
                mm = pe.transpose(bank[5][:, k * T:(k + 1) * T], gs[:, k, :], identf[0:T, 0:T])
            mm.then_inc(owners_turned, 1)
            pe.wait_ge(tile_hot_ready, 1)
            pe.matmul(bank[6][:, 2 * STEPS:3 * STEPS], gs[:, 0, :], tile_hot[:, :], start=True, stop=True).then_inc(step_owners, 1)
            pe.wait_ge(er_ready, 1)
            for k in range(2):
                for c in range(7):
                    n = min(P, ET - c * P)
                    mm = pe.transpose(bank[(0, 1, 7, 3)[2 * k + c // 4]][:, (c % 4) * P:(c % 4) * P + n], erf[0:n, k, c, :],
                                      identf[0:n, 0:n])
            mm.then_inc(er_turned, 1)
            pe.wait_ge(tables_ready, 1)

            def turn(t, b):
                pe.wait_ge(flag_done, t + 1)
                ge(pe, eft_done, t)
                for j in range(G):
                    mm = pe.transpose(turned[0:KROWS, j * P:(j + 1) * P], blk[:, b, j, 0:KROWS], identb[:, :])
                mm.then_inc(rows_turned, 1)

            def message(t, b, j):
                if j == 0:
                    pe.wait_ge(eft_done, t + 1)
                ge(pe, slot_scored, G * t + j - 3)
                pe.matmul(bank[j % 4][:, :], eft[:, b, j, :], wst[:, :], start=True, stop=True).then_inc(slot_product, 1)

            def total(t, b, j):
                if j == 0:
                    ge(pe, sums_kept, t)
                if j % 4 == 0:
                    pe.wait_ge(weighed, 2 * t + j // 4 + 1)
                mm = pe.matmul(bank[5][:, :], identf[:, :], em[:, b, j, :, :].rearrange("p a c -> p (a c)"),
                               start=(j == 0), stop=(j == G - 1))
                if j == G - 1:
                    mm.then_inc(sum_done, 1)

            def turn_max(t, b):
                pe.wait_ge(max_taken, 4 * t + 4)
                ge(pe, max_kept, t)
                for h in range(2):
                    mm = pe.transpose(bank[6][:, h * P:(h + 1) * P], spb[:, b, h * P:(h + 1) * P], identf[:, :])
                mm.then_inc(max_turned, 1)

            def step(t, b, before=3, left=3):
                def totals(*slots):
                    for j in slots:
                        if before >= 2:
                            total(t - 2, (b + 1) % 3, j)

                totals(0, 1, 2)
                if before >= 1:
                    turn_max(t - 1, (b + 2) % 3)
                totals(3)
                for j in (4, 5):
                    message(t, b, j)
                totals(4)
                for j in (6, 7):
                    message(t, b, j)
                totals(5)
                if left >= 2:
                    turn(t + 2, (b + 2) % 3)
                totals(6)
                for j in range(4):
                    if left >= 1:
                        message(t + 1, (b + 1) % 3, j)
                totals(7)

            for t in range(2):
                turn(t, t)
            for j in range(G // 2):
                message(0, 0, j)
            for t in range(3):
                step(t, t, t)
            n3 = loops(pe)
            n4 = joins(pe)
            with pe.Fori(1, n3 - 1) as i:
                for b in range(3):
                    step(3 * i + b, b)
            for b in range(3):
                step(3 * n3 - 3 + b, b, 3, 2 - b)
            turn_max(3 * n3 - 1, 2)
            for b in (1, 2):
                for j in range(G):
                    total(3 * n3 - 3 + b, b, j)

            def turn_back(k, b):
                pe.wait_ge(mc_done, k + 1)
                ge(pe, sub_done, k - 3)
                for h in range(2):
                    mm = pe.transpose(bank[b][:, h * P:(h + 1) * P], mc[:, b, h, :], identf[:, :])
                mm.then_inc(node_max_turned, 1)

            def to_nodes(k, b):
                pe.wait_ge(wmul_done, k + 1)
                ge(pe, node_add, k - 3)
                pe.matmul(bank[4 + b][:, :], own_hot[:, b, :], md[:, b, C:3 * C], start=True, stop=True).then_inc(node_ps, 1)

            def join(k, b, more=True):
                if more:
                    turn_back(k + 2, (b + 2) % 4)
                to_nodes(k, b)

            for k in range(2):
                turn_back(k, k)
            for k in range(4):
                join(k, k)
            with pe.Fori(1, n4 - 1) as i:
                for b in range(4):
                    join(4 * i + b, b)
            for b in range(4):
                join(4 * n4 - 4 + b, b, b < 2)

            pe.wait_ge(zero_ready, 1)

            def windows(v):
                units = window_units(mybir.EngineType.PE, v)
                for b in range(WG):
                    w = WG * v + b
                    ge(pe, win_ev, w - 3)
                    ge(pe, left_past, w - 3)
                    pe.nop(nofuse=True)
                    pe.matmul(bank[b % 4][:, 0:CW], zero_b[:, 0:P], zero_b[:, :], start=True, stop=False)
                    with pe.Fori(units[b], units[b + 1] + 1) as i:
                        for q in range(EU):
                            if q == 1:
                                pe.wait_ge(lo_ready, i + w + 2)
                            pe.wait_ge(hot_ready, EU * (i + w) + q + 1)
                            pe.matmul(bank[b % 4][:, 0:CW], hot_lo[:, q, :], hot_key[:, q, :], start=False, stop=False).then_inc(hot_used, 1)
                    pe.matmul(bank[b % 4][:, 0:CW], zero_b[:, 0:P], zero_b[:, :], start=False, stop=True).then_inc(win_ps, 1)

            windows(0)
            with pe.Fori(1, NW // WG) as v:
                windows(v)

            pe.wait_ge(any_ready, 1)
            pe.transpose(bank[6][0:1, 0:P], left_p[:, :], identf[:, :]).then_inc(any_turned, 1)
            pe.wait_ge(flag_ready, 1)
            some = pe.value_load(flag[0:1, 0:1], min_val=0, max_val=1)

            def left_products(c):
                with pe.If(some == 1):
                    hw = dense_windows(pe)
                    with pe.Fori(0, hw) as w:
                        pe.wait_ge(left_in, (hw * c + w) * 16 + 16)
                        for h in range(NT):
                            mm = pe.matmul(bank[6][0:3 * F, 0:WIN], xs[:, h, :, :].rearrange("p a f -> p (a f)"),
                                           left[:, :].rearrange("p (n h) -> p h n", h=NT)[:, h, :], start=(h == 0), stop=(h == NT - 1))
                        mm.then_inc(left_ps, 1)

            pe.wait_ge(win_ev, NW)
            pe.wait_ge(gin_in, 16 * 16)

            def neighbours(c, q):
                k, (n0, n) = c * NB + q, BLOCKS[q]
                ge(pe, xt_ev, k - 1)
                for t in range(n0 // P, (n0 + n) // P):
                    mm = pe.transpose(bank[k % 2][0:F, t * P - n0:t * P - n0 + P], (x1, hn)[c][:, t, :], identf[:, :])
                mm.then_inc(xt_ps, 1)
                ge(pe, conv_ev, k - 1)
                for h in range(NT):
                    mm = pe.matmul(bank[2 + k % 2][0:3 * F, 0:n], xs[:, h, :, :].rearrange("p a f -> p (a f)"), cnt[:, h, n0:n0 + n],
                                   start=(h == 0), stop=(h == NT - 1))
                mm.then_inc(conv_ps, 1)

            def map_first(c, q):
                k, (n0, n) = c * NB + q, BLOCKS[q]
                pe.wait_ge(conv_ev, k + 1)
                pe.wait_ge(agg_ready, k + 1)
                pe.wait_ge(xt_ev, k + 1)
                ge(pe, hid_ev, k - 1)
                pe.matmul(bank[4 + k % 2][0:F, 0:n], gw[:, c, :], agg[:, k % 2, 0:n], start=True, stop=False)
                pe.matmul(bank[4 + k % 2][0:F, 0:n], gwe[:, c, :], xt[:, k % 2, 0:n], start=False, stop=True).then_inc(hid_ps, 1)

            def map_second(c, q):
                k, (n0, n) = c * NB + q, BLOCKS[q]
                pe.wait_ge(hid_ev, k + 1)
                for t in range(n0 // P, (n0 + n) // P):
                    mm = pe.matmul(bank[7][:, t * F:(t + 1) * F], ut[:, k % 2, t * P - n0:(t + 1) * P - n0], gb[:, c, :],
                                   start=True, stop=True)
                mm.then_inc(map2, 1)

            for c in range(2):
                pe.wait_ge(xs_ready, c + 1)
                left_products(c)
                for q in range(NB + 2):
                    if q < NB:
                        neighbours(c, q)
                    if q >= 2:
                        map_second(c, q - 2)
                    if 1 <= q <= NB:
                        map_first(c, q - 1)

        @block.scalar
        def _(act):
            ef_v = ef.rearrange("(p c e) f -> p c (e f)", p=PP, c=PREP)
            rows_v = edge_rows[0:E, :].rearrange("(p c e) r -> p c (e r)", p=PP, c=PREP)
            act.dma_start(src_i[:, :, :], src.rearrange("(p c e) -> p c e", p=PP, c=PREP)).then_inc(in_src, 16)
            for c in range(2):
                act.dma_start(ef_in[:, c, :, :].rearrange("p e f -> p (e f)"), ef_v[:, c]).then_inc(ef_ld[c], 16)
            act.wait_ge(pre_fill, 2)

            def raise_rows(c):
                b = c % 2
                act.wait_ge(ef_ld[b], 16 * (c // 2 + 1))
                ge(act, rows_out[b], 16 * (c // 2))
                act.activation(rows[:, b, :, 0:3 * F].rearrange("p e (k f) -> p e k f", k=3),
                               ef_in[:, b, :, :].unsqueeze(2).to_broadcast([PP, PC, 3, F]), ACT.Copy).then_inc(rows_high, 1)
                act.wait_ge(rows_resid, c + 1)
                act.activation(rows[:, b, :, 3 * F:5 * F].rearrange("p e (k f) -> p e k f", k=2),
                               resid[:, :, :].unsqueeze(2).to_broadcast([PP, PC, 2, F]), ACT.Copy).then_inc(rows_mid, 1)
                if c + 2 < PREP:
                    act.wait_ge(rows_high, c + 1)
                    act.dma_start(ef_in[:, b, :, :].rearrange("p e f -> p (e f)"), ef_v[:, c + 2]).then_inc(ef_ld[b], 16)
                act.wait_ge(rows_done, 2 * (c + 1))
                act.dma_start(rows_v[:, c], rows[:, b, :, :].rearrange("p e r -> p (e r)")).then_inc(rows_out[b], 16)

            for c in range(5):
                raise_rows(c)
            act.wait_ge(fill_ready, 3)
            act.dma_start(wf[0:F, 0:C], w_att).then_inc(w_in, 16)
            act.dma_start(wf[0:F, C:2 * C], w_msg).then_inc(w_in, 16)
            act.dma_start(wf[F:F + 1, 0:C], b_att.rearrange("(a c) -> a c", a=1)).then_inc(w_in, 16)
            act.dma_start(wf[F:F + 1, C:2 * C], b_msg.rearrange("(a c) -> a c", a=1)).then_inc(w_in, 16)
            full = E // P
            for k, a in enumerate((src, dst)):
                act.dma_start(er[:, k, 0:6, :], a[0:6 * P * P].rearrange("(c r p) -> r c p", p=P, r=P)).then_inc(er_in, 16)
                act.dma_start(er[0:full - 6 * P, k, 6, :], a[6 * P * P:full * P].rearrange("(r p) -> r p", p=P)).then_inc(er_in, 16)
                act.dma_start(er[full - 6 * P:full - 6 * P + 1, k, 6, 0:E - full * P],
                              a[full * P:E].rearrange("(a p) -> a p", a=1)).then_inc(er_in, 16)
            for c in range(5, PREP):
                raise_rows(c)
            act.wait_ge(w_split, 1)
            for k, part in enumerate((0, 1, 2, 0, 1, 0)):
                act.dma_start(wst[k * F:(k + 1) * F, :], wh[0:F, part, :]).then_inc(w_out, 16)
            for part in range(3):
                act.dma_start(wst[6 * F + part:6 * F + part + 1, :], wh[F:F + 1, part, :]).then_inc(w_out, 16)
            act.dma_start(wst[KROWS - 1:KROWS, :], wflag[0:1, :]).then_inc(w_out, 16)
            act.wait_ge(tables_ready, 1)

            def flags(t, b, i):
                act.wait_ge(blk_in[b], 16 * (i + 1))
                act.nop(nofuse=True)
                act.activation(blk[:, b, :, KROWS - 1], empty[:, bass.ds(t * G, G)], ACT.Copy).then_inc(flag_done, 1)

            def keep_turned(t, b):
                act.wait_ge(rows_turned, t + 1)
                ge(act, slot_product, G * (t - 2))
                act.activation(eft[:, b, :, :].rearrange("p g e -> p (g e)"), turned[0:KROWS, :], ACT.Copy).then_inc(eft_done, 1)

            def exps(t, b):
                for q in range(2):
                    act.wait_ge(shifted, 2 * t + q + 1)
                    act.activation(em[:, b, 4 * q:4 * q + 4, 0, :], em[:, b, 4 * q:4 * q + 4, 0, :], ACT.Exp).then_inc(exp_done, 1)

            def keep_max(t, b):
                act.wait_ge(max_turned, t + 1)
                act.nop(nofuse=True)
                act.activation(mt[:, :, bass.ds(t * P, P)], bank[6][:, 0:2 * P].rearrange("p (h g) -> p h g", h=2),
                               ACT.Copy).then_inc(max_kept, 1)

            def keep_sums(t, b, i):
                act.wait_ge(sum_done, t + 1)
                ge(act, spill_out[b], 16 * i)
                act.activation(spb[:, b, C:3 * C], bank[5][:, :], ACT.Copy).then_inc(sums_kept, 1)

            def step(t, b, i, before=3, left=3):
                if left >= 2:
                    keep_turned(t + 2, (b + 2) % 3)
                if before >= 1:
                    keep_max(t - 1, (b + 2) % 3)
                if before >= 2:
                    keep_sums(t - 2, (b + 1) % 3, i - 1 if b < 2 else i)
                exps(t, b)
                if left >= 3:
                    flags(t + 3, b, i + 1)

            for t in range(3):
                flags(t, t, 0)
                if t < 2:
                    keep_turned(t, t)
            for t in range(6):
                step(t, t % 3, t // 3, t)
            n3 = loops(act)
            n4 = joins(act)
            with act.Fori(2, n3 - 1) as i:
                for b in range(3):
                    step(3 * i + b, b, i)
            for b in range(3):
                step(3 * n3 - 3 + b, b, n3 - 1, 3, 2 - b)
            keep_max(3 * n3 - 1, 2)
            keep_sums(3 * n3 - 2, 1, n3 - 1)
            keep_sums(3 * n3 - 1, 2, n3 - 1)

            act.wait_ge(scans_ready, 1)

            def maxima(k, b):
                ge(act, node_max_turned, k - 3)
                act.nop(nofuse=True)
                tile = act.value_load(step_tile[0:1, bass.ds(k, 1)], min_val=0, max_val=T - 1)
                act.nop(nofuse=True)
                act.activation(mc[:, b, :, :], mt[:, :, bass.ds(tile * P, P)], ACT.Copy).then_inc(mc_done, 1)

            def factors(k, b):
                act.wait_ge(sub_done, k + 1)
                act.activation(md[:, b, 0:C], md[:, b, 0:C], ACT.Exp).then_inc(wexp_done, 1)

            for k in range(3):
                maxima(k, k)
            for k in range(4):
                maxima(k + 3, (k + 3) % 4)
                factors(k, k)
            with act.Fori(1, n4 - 1) as i:
                for b in range(4):
                    maxima(4 * i + b + 3, (b + 3) % 4)
                    factors(4 * i + b, b)
            maxima(4 * n4 - 1, 3)
            for b in range(4):
                factors(4 * n4 - 4 + b, b)
            act.wait_ge(ln_var, 1)
            act.activation(st2[:, :], st1[:, :], ACT.Sqrt).then_inc(ln_sd, 1)

            act.wait_ge(zero_ready, 1)
            act.sem_inc(lo_ready, 1)

            def keep_counts(w, b):
                act.wait_ge(win_ps, w + 1)
                act.nop(nofuse=True)
                act.activation(cnt[:, :, bass.ds(w * WIN, WIN)],
                               bank[b][:, 0:CW].rearrange("p (n h) -> p h n", h=NT), ACT.Copy).then_inc(win_ev, 1)

            def windows(v, first=False):
                units = window_units(mybir.EngineType.Activation, v)
                for b in range(WG):
                    w = WG * v + b
                    with act.Fori(units[b], units[b + 1] + 1) as i:
                        act.wait_ge(lo_ready, i + w + 1)
                        act.nop(nofuse=True)
                        for q in range(1, EU):
                            act.activation(hot_sq[:, q - 1, :], iota_lo[:, :], ACT.Square,
                                           bias=minus_lo[:, bass.ds(EU * i + q, 1)]).then_inc(sq_done, 1)
                        act.wait_ge(sq_done, (EU - 1) * (i + w + 1))
                        act.wait_ge(hot_used, EU * (i + w + 1))
                        act.activation(hot_lo[:, 1:EU, :], hot_sq[:, :, :], ACT.Relu, bias=one_col[:, :], scale=-1.0).then_inc(lo_ready, 1)
                    if b >= 1 or not first:
                        keep_counts(w - 1, (b + 3) % 4)

            windows(0, True)
            with act.Fori(1, NW // WG) as v:
                windows(v)
            keep_counts(NW - 1, 3)

            for c in range(2):
                for q in range(NB + 1):
                    if q < NB:
                        k, n = c * NB + q, BLOCKS[q][1]
                        act.wait_ge(xt_ps, k + 1)
                        ge(act, hid_ps, k - 1)
                        act.activation(xt[:, k % 2, 0:n], bank[k % 2][0:F, 0:n], ACT.Copy).then_inc(xt_ev, 1)
                        act.wait_ge(conv_ps, k + 1)
                        act.activation(agg[:, k % 2, 0:n], bank[2 + k % 2][0:3 * F, 0:n], ACT.Copy).then_inc(conv_ev, 1)
                    if q >= 1:
                        k, n = c * NB + q - 1, BLOCKS[q - 1][1]
                        act.wait_ge(hid_ps, k + 1)
                        ge(act, map2, k - 1)
                        act.activation(ut[0:F, k % 2, 0:n], bank[4 + k % 2][0:F, 0:n], ACT.Relu, bias=gba[:, c:c + 1]).then_inc(hid_ev, 1)
            act.wait_ge(lsm_e, 1)
            act.activation(hn[:, :, :], hn2[:, :, :], ACT.Exp).then_inc(lsm_s, 1)
            act.wait_ge(lsm_e, 2)
            act.activation(st2[:, :], st1[:, :], ACT.Ln).then_inc(lsm_l, 1)
            act.wait_ge(ln_var, 2)
            act.activation(st2[:, :], st1[:, :], ACT.Sqrt).then_inc(ln_sd, 1)

        @block.vector
        def _(dve):
            done = [0]

            def link(ins):
                done[0] += 1
                ins.then_inc(dve_step, 1)
                dve.wait_ge(dve_step, done[0])

            dve.wait_ge(const_ready, 4)
            dve.wait_ge(in_last, 16)
            dve.tensor_copy(rl_f[:, 0:SROWS], rl_i[:, :]).then_inc(last_ready, 1)
            dve.wait_ge(last_bcast, 1)
            link(dve.tensor_copy(rl_b[:, :], bank[0][:, 0:SROWS]))
            link(dve.tensor_tensor(less[:, :, :], rl_b[:, :].unsqueeze(1).to_broadcast([P, NT, SROWS]),
                                   node_id[:, :].unsqueeze(2).to_broadcast([P, NT, SROWS]), ALU.is_lt))
            fold = SROWS // 4
            link(dve.tensor_tensor(less[:, :, 0:2 * fold], less[:, :, 0:2 * fold], less[:, :, 2 * fold:4 * fold], ALU.add))
            link(dve.tensor_tensor(less[:, :, 3 * fold:4 * fold], less[:, :, 0:fold], less[:, :, fold:2 * fold], ALU.add))
            link(dve.tensor_reduce(found_r[:, :], less[:, :, 3 * fold:SROWS], AX.X, ALU.add))
            dve.tensor_copy(found_i[:, :], found_r[:, :]).then_inc(rows_found, 1)
            dve.wait_ge(in_src, 16)

            def split_rows(c):
                b = c % 2
                dve.wait_ge(rows_high, c + 1)
                ge(dve, rows_mid, c)
                ge(dve, rows_done, 2 * c)
                dve.tensor_tensor(resid[:, :, :], ef_in[:, b, :, :], rows[:, b, :, 0:F], ALU.subtract).then_inc(rows_resid, 1)
                dve.tensor_copy(rows[:, b, :, :].rearrange("p e r -> p (e r)").bitcast(I32)
                                .rearrange("p (e r) -> p e r", e=PC)[:, :, KROWS // 2], src_i[:, c, :]).then_inc(rows_done, 1)
                dve.wait_ge(rows_mid, c + 1)
                dve.tensor_tensor(rows[:, b, :, 5 * F:6 * F], resid[:, :, :], rows[:, b, :, 3 * F:4 * F],
                                  ALU.subtract).then_inc(rows_done, 1)

            for c in range(3):
                split_rows(c)
            dve.wait_ge(search_in, 16 * NT)
            link(dve.tensor_tensor(less[:, :, 0:SR], srow[:, :, :],
                                   node_id[:, :].unsqueeze(2).to_broadcast([P, NT, SR]), ALU.is_lt))
            for fold in (SR // 2, SR // 4):
                link(dve.tensor_tensor(less[:, :, 0:fold], less[:, :, 0:fold], less[:, :, fold:2 * fold], ALU.add))
            link(dve.tensor_reduce(start_nm[:, :], less[:, :, 0:SR // 4], AX.X, ALU.add))
            dve.scalar_tensor_tensor(out=start_nm[:, :], in0=found_r[:, :], scalar=float(SR), in1=start_nm[:, :],
                                     op0=ALU.mult, op1=ALU.add).then_inc(start_ready, 1)
            dve.wait_ge(start_turned, 1)
            dve.tensor_copy(start_t[:, :], bank[1][0:NT, 0:P]).then_inc(start_kept, 1)
            split_rows(3)
            dve.wait_ge(row_in, 32)
            link(dve.tensor_tensor(r_c[:, :], r_b[:, :], r_a[:, 0:NP], ALU.subtract))
            wmax = rl_f[:, 0:NW]
            link(dve.tensor_reduce(wmax, r_c[:, :].rearrange("a (w n) -> a w n", n=WIN), AX.X, ALU.max))
            link(dve.scalar_tensor_tensor(out=wmax, in0=wmax, scalar=float(EXACT), in1=w500[0:1, :], op0=ALU.is_gt, op1=ALU.mult))
            link(dve.tensor_reduce(rl_f[:, NW:NW + 1], wmax, AX.X, ALU.max))
            link(dve.tensor_scalar(counts[:, 2:3], rl_f[:, NW:NW + 1], 1.0 / CW, None, ALU.mult))
            link(dve.tensor_scalar(r_i[:, :], r_c[:, :], float(G - 1), None, ALU.add))
            link(dve.tensor_scalar(r_i[:, :], r_i[:, :], 3, None, ALU.arith_shift_right))
            link(dve.tensor_copy(r_b[:, :], r_i[:, :]))
            link(dve.tensor_scalar(r_c[:, :], r_c[:, :], 0.0, float(2 * S), ALU.is_equal, ALU.mult))
            link(dve.tensor_tensor_scan(r_g[:, :], r_b[:, :], r_b[:, :], 0.0, ALU.add, ALU.max))
            link(dve.tensor_copy(r_i[0:1, 0:NT], r_g[0:1, P - 1:NP:P]))
            link(dve.tensor_scalar(r_i[0:1, 0:NT], r_i[0:1, 0:NT], 7, None, ALU.arith_shift_right))
            cq, ct = rl_f[:, 3 * (NW + 1):3 * (NW + 1) + 1], rl_f[:, 3 * (NW + 1) + 1:3 * (NW + 1) + 2]
            link(dve.tensor_scalar(counts[:, 0:1], r_g[:, NP - 1:NP], 1.0 / (3 * P), None, ALU.mult))
            link(dve.tensor_copy(cq, counts[:, 0:1]))
            link(dve.scalar_tensor_tensor(out=ct, in0=cq, scalar=float(3 * P), in1=r_g[:, NP - 1:NP], op0=ALU.mult, op1=ALU.is_gt))
            link(dve.tensor_tensor(cq, cq, ct, ALU.subtract))
            link(dve.tensor_scalar(counts[:, 0:1], cq, 2.0, None, ALU.subtract))
            link(dve.tensor_scalar(counts[:, 1:2], r_i[0:1, NT - 1:NT], float(NT + 3 - 12), None, ALU.add))
            link(dve.tensor_scalar(counts[:, 1:2], counts[:, 1:2], 2, None, ALU.arith_shift_right))
            wstart, wq, wt = (rl_f[:, k * (NW + 1):(k + 1) * (NW + 1)] for k in range(3))
            link(dve.tensor_copy(wstart, r_a[0:1, 0:NP + 1:WIN]))
            link(dve.tensor_scalar(win_unit[:, :], wstart, 1.0 / (EU * P), None, ALU.mult))
            link(dve.tensor_copy(wq, win_unit[:, :]))
            link(dve.scalar_tensor_tensor(out=wt, in0=wq, scalar=float(EU * P), in1=wstart, op0=ALU.mult, op1=ALU.is_gt))
            link(dve.tensor_tensor(win_unit[:, :], wq, wt, ALU.subtract))
            link(dve.tensor_tensor(r_g[:, :], r_g[:, :], r_b[:, :], ALU.subtract))
            dve.tensor_tensor(r_c[:, :], r_c[:, :], r_g[:, :], ALU.add).then_inc(row_ready, 1)
            split_rows(4)
            dve.wait_ge(fill_ready, 3)
            link(dve.tensor_copy(kt_f[:, :], r_i[0:1, 0:NT]))
            link(dve.tensor_copy(last_tile[:, :], kt_f[:, NT - 1:NT]))
            link(dve.tensor_tensor(kt_f[:, :], kt_f[:, :], kst[:, 0:NT], ALU.add))
            link(dve.tensor_tensor(kcmp[:, :, :], kt_f[:, :].unsqueeze(1).to_broadcast([1, STEPS, NT]),
                                   kst[:, :].unsqueeze(2).to_broadcast([1, STEPS, NT]), ALU.is_lt))
            link(dve.tensor_reduce(kwin[:, :], kcmp[:, :, :], AX.X, ALU.add))
            link(dve.tensor_copy(step_win[:, :], kwin[:, :]))
            link(dve.tensor_tensor(kst[:, :], kst[:, :], kwin[:, :], ALU.subtract))
            link(dve.tensor_scalar(kst[:, :], kst[:, :], last_tile[:, 0:1], None, ALU.min))
            link(dve.tensor_copy(step_tile[:, :], kst[:, :]))
            dve.tensor_scalar(kwin[:, :], kwin[:, :], float(P), None, ALU.mult).then_inc(wk_ready, 1)
            dve.wait_ge(nm_turned, 1)
            nmv = bank[2][:, 0:4 * NT].rearrange("p (k t) -> p k t", k=4)
            link(dve.tensor_copy(pay[:, :, 0], node_id[:, :]))
            link(dve.tensor_copy(pay[:, :, 1], nmv[:, 3, :]))
            link(dve.tensor_copy(pay[:, :, 2], nmv[:, 2, :]))
            link(dve.tensor_copy(pay[:, :, 3], nmv[:, 0, :]))
            dve.tensor_copy(slot_i[:, :], nmv[:, 1, :]).then_inc(scatter_ready, 1)
            dve.wait_ge(w_in, 64)
            link(dve.tensor_copy(wh[:, 0, :], wf[:, :]))
            link(dve.tensor_tensor(wf[:, :], wf[:, :], wh[:, 0, :], ALU.subtract))
            link(dve.tensor_copy(wh[:, 1, :], wf[:, :]))
            dve.tensor_tensor(wh[:, 2, :], wf[:, :], wh[:, 1, :], ALU.subtract).then_inc(w_split, 1)
            dve.wait_ge(er_in, 96)
            link(dve.tensor_scalar(eh[:, :, :], er[:, 0, :, :], 7, None, ALU.arith_shift_right))
            link(dve.tensor_scalar(erf[:, 0, :, :], er[:, 1, :, :], float(NT), None, ALU.mult))
            link(dve.tensor_tensor(erf[:, 0, :, :], erf[:, 0, :, :], eh[:, :, :], ALU.add))
            link(dve.tensor_scalar(eh[:, :, :], er[:, 0, :, :], P - 1, None, ALU.bitwise_and))
            dve.tensor_copy(erf[:, 1, :, :], eh[:, :, :]).then_inc(er_ready, 1)
            for c in range(5, PREP):
                split_rows(c)
            dve.wait_ge(wk_bcast, 1)
            dve.tensor_scalar(tile_hot[:, :], bank[6][0:T, STEPS:2 * STEPS], node_id[0:T, 0:1], None,
                              ALU.is_equal).then_inc(tile_hot_ready, 1)
            dve.wait_ge(table_in, 16)
            for k in range(4):
                link(dve.tensor_tensor_scan(gs[:, k, :], gt[:, :, k], gt[:, :, k], 0.0, ALU.max, ALU.max))
            dve.tensor_copy(carry[:, :], gs[:, :, P - 1]).then_inc(carry_ready, 1)
            link(dve.memset(carry_r[:, 0:1], 0.0))
            dve.wait_ge(carry_turned, 1)
            link(dve.tensor_copy(carry_r[:, 1:T + 1], bank[3][0:4, 0:T]))
            dve.tensor_tensor_scan(carry_r[:, :], carry_r[:, :], carry_r[:, :], 0.0, ALU.max, ALU.max).then_inc(carry_scanned, 1)
            dve.wait_ge(carry_back, 1)
            link(dve.tensor_copy(carry_b[:, :], bank[4][0:T, 0:4]))
            for k in range(3):
                link(dve.tensor_scalar(gs[:, k, :], gs[:, k, :], carry_b[:, k:k + 1], None, ALU.max))
            dve.tensor_scalar(gs[:, 3, :], gs[:, 3, :], carry_b[:, 3:4], None, ALU.max).then_inc(owner_ready, 1)
            dve.wait_ge(owner_in, 16)
            link(dve.tensor_tensor(own_p[:, :], own_p[:, :], gs[:, 0, :], ALU.not_equal))
            dve.tensor_scalar(fence_r[:, :], own_p[:, :], -FAR, None, ALU.mult).then_inc(fence_ready, 1)
            dve.wait_ge(owners_turned, 1)
            link(dve.tensor_copy(gm[:, :, :], bank[5][:, 0:4 * T].rearrange("p (k t) -> p k t", k=4)))
            link(dve.tensor_tensor(gid[:, :], gid[:, :], gm[:, 3, :], ALU.subtract))
            link(dve.scalar_tensor_tensor(out=estf[:, :], in0=gid[:, :], scalar=float(G), in1=gm[:, 1, :], op0=ALU.mult, op1=ALU.add))
            link(dve.memset(est_i[:, T:T + 1], 0))
            link(dve.tensor_scalar(est_i[:, 0:T], estf[:, :], float(E), None, ALU.min))
            link(dve.tensor_tensor(eslot[:, :, :], eslot[:, :, :], estf[:, :].unsqueeze(2).to_broadcast([P, T, G]), ALU.add))
            link(dve.tensor_tensor(eslot[:, :, :], eslot[:, :, :], gm[:, 2, :].unsqueeze(2).to_broadcast([P, T, G]), ALU.is_ge))
            link(dve.tensor_scalar(empty[:, :], eslot[:, :, :].rearrange("p t g -> p (t g)"), float(FLAG), None, ALU.mult))
            dve.wait_ge(step_owners, 1)
            link(dve.tensor_copy(step_own[:, :], bank[6][:, 0:STEPS]))
            link(dve.tensor_tensor(step_own[:, :], bank[6][:, 2 * STEPS:3 * STEPS], step_own[:, :], ALU.subtract))
            dve.wait_ge(er_turned, 1)
            link(dve.tensor_copy(kb[:, 0:512], bank[0][:, :]))
            link(dve.tensor_copy(kb[:, 512:ET], bank[1][:, 0:ET - 512]))
            link(dve.tensor_copy(lo[:, 0:512], bank[7][:, :]))
            link(dve.tensor_copy(lo[:, 512:ET], bank[3][:, 0:ET - 512]))
            dve.wait_ge(w_out, 16 * 10)
            dve.wait_ge(fence_out, 32)
            for c in range(2):
                dve.wait_ge(rows_out[c], 16 * PREP // 2)
            dve.sem_inc(tables_ready, 1)

            n3 = loops(dve)
            n4 = joins(dve)
            with dve.Fori(n3, T // 3 + 1) as i:
                for h in range(2):
                    dve.tensor_scalar(mt[:, h, bass.ds((i - 1) * CH, CH)], w500[:, 0:1].to_broadcast([P, CH]), 0.0, -BIG,
                                      ALU.mult, ALU.add)

            def score(t, b, j):
                dve.wait_ge(slot_product, G * t + j + 1)
                dve.tensor_tensor(em[:, b, j, :, :].rearrange("p a (i o) -> p a i o", i=F),
                                  bank[j % 4][:, :].rearrange("p (a i o) -> p a i o", a=2, i=F),
                                  hb[:, b, j, :].unsqueeze(1).unsqueeze(3).to_broadcast([P, 2, F, F]),
                                  ALU.mult).then_inc(slot_scored, 1)

            def weigh(t, b, q):
                dve.wait_ge(exp_done, 2 * t + q + 1)
                dve.tensor_tensor(em[:, b, 4 * q:4 * q + 4, 1, :], em[:, b, 4 * q:4 * q + 4, 1, :],
                                  em[:, b, 4 * q:4 * q + 4, 0, :], ALU.mult).then_inc(weighed, 1)

            def step(t, b, i, before=3):
                dve.wait_ge(h_in[b], 16 * G * (i + 1))
                ge(dve, sum_done, t - 2)
                for j in range(5):
                    score(t, b, j)
                dve.wait_ge(slot_scored, G * t + 4)
                dve.tensor_tensor(mx[:, :, :], em[:, b, 0:2, 0, :], em[:, b, 2:4, 0, :], ALU.max).then_inc(max_taken, 1)
                for q in range(2):
                    for j in ((5, 6), (7,))[q]:
                        score(t, b, j)
                    if q == 1 and before >= 1:
                        weigh(t - 1, (b + 2) % 3, 0)
                    dve.wait_ge(slot_scored, G * t + 6 + 2 * q)
                    dve.wait_ge(max_taken, 4 * t + q + 1)
                    dve.tensor_tensor(mx[:, :, :], mx[:, :, :], em[:, b, 4 + 2 * q:6 + 2 * q, 0, :], ALU.max).then_inc(max_taken, 1)
                if before >= 1:
                    weigh(t - 1, (b + 2) % 3, 1)
                dve.wait_ge(max_taken, 4 * t + 3)
                ge(dve, max_turned, t - 2)
                ge(dve, spill_out[b], 16 * i)
                dve.tensor_tensor(spb[:, b, 0:C], mx[:, 0, :], mx[:, 1, :], ALU.max).then_inc(max_taken, 1)
                dve.wait_ge(max_taken, 4 * t + 4)
                for q in range(2):
                    dve.tensor_tensor(em[:, b, 4 * q:4 * q + 4, 0, :], em[:, b, 4 * q:4 * q + 4, 0, :],
                                      spb[:, b, 0:C].unsqueeze(1).to_broadcast([P, 4, C]), ALU.subtract).then_inc(shifted, 1)

            for t in range(3):
                step(t, t, 0, t)
            with dve.Fori(1, n3) as i:
                for b in range(3):
                    step(3 * i + b, b, i)
            for q in range(2):
                weigh(3 * n3 - 1, 2, q)

            dve.wait_ge(fence_in, 16)
            dve.wait_ge(max_kept, 3 * n3)
            for h in range(2):
                dve.tensor_tensor_scan(mt[:, h, 0:CH], fence[:, 0:CH], mt[:, h, 0:CH], 0.0, ALU.add, ALU.max).then_inc(scan_done, 1)
            with dve.Fori(1, n3) as i:
                for h in range(2):
                    dve.wait_ge(scan_done, 2 * i + h - 1)
                    dve.nop(nofuse=True)
                    part = mt[:, h, bass.ds(i * CH, CH)]
                    dve.tensor_tensor_scan(part, fence[:, bass.ds(i * CH, CH)], part, mt[:, h, bass.ds(i * CH - 1, 1)],
                                           ALU.add, ALU.max).then_inc(scan_done, 1)
            dve.wait_ge(scan_done, 2 * n3)
            dve.nop(nofuse=True)
            for h in range(2):
                dve.tensor_tensor_scan(mt[:, h, ::-1], fence[:, S:0:-1], mt[:, h, ::-1], 0.0, ALU.add, ALU.max).then_inc(back_done, 1)
            dve.wait_ge(back_done, 2)
            dve.sem_inc(scans_ready, 1)
            dve.memset(acc[:, 0:2, :], 0.0).then_inc(acc_zero, 1)

            def tile_factors(k, b, i):
                ge(dve, node_ps, k - 3)
                dve.nop(nofuse=True)
                dve.tensor_scalar(own_hot[:, b, :], iotaf[:, :], step_own[:, bass.ds(k, 1)], None,
                                  ALU.is_equal).then_inc(own_done, 1)
                dve.wait_ge(md_in[b], 16 * (i + 1))
                dve.wait_ge(node_max_turned, k + 1)
                dve.tensor_tensor(md[:, b, 0:C], md[:, b, 0:C], bank[b][:, 0:C], ALU.subtract).then_inc(sub_done, 1)

            def scale(k, b):
                dve.wait_ge(wexp_done, k + 1)
                dve.wait_ge(own_done, k + 1)
                sums = md[:, b, C:3 * C].rearrange("p (a c) -> p a c", a=2)
                dve.tensor_tensor(sums, sums, md[:, b, 0:C].unsqueeze(1).to_broadcast([P, 2, C]), ALU.mult).then_inc(wmul_done, 1)

            def add_nodes(k, b):
                if isinstance(k, int) and k == 0:
                    dve.wait_ge(acc_zero, 3)
                win = dve.value_load(step_win[0:1, bass.ds(k, 1)], min_val=0, max_val=NT)
                dve.wait_ge(node_ps, k + 1)
                ge(dve, node_add, k)
                dve.nop(nofuse=True)
                node = acc[:, bass.ds(win, 1), :].rearrange("p a c -> p (a c)")
                dve.tensor_tensor(node, node, bank[4 + b][:, :], ALU.add).then_inc(node_add, 1)

            def join(k, b, i):
                tile_factors(k, b, i)
                if not isinstance(k, int) or k >= 1:
                    scale(k - 1, (b + 3) % 4)
                if not isinstance(k, int) or k >= 2:
                    add_nodes(k - 2, (b + 2) % 4)

            for k in range(4):
                join(k, k, 0)
            with dve.Fori(1, n4) as i:
                for b in range(4):
                    join(4 * i + b, b, i)
            scale(4 * n4 - 1, 3)
            for b in (2, 3):
                add_nodes(4 * n4 - 4 + b, b)
            dve.wait_ge(node_add, 4 * n4)
            den = acc[:, 0:NT, 0:C]
            num = acc[:, 0:NT, C:2 * C]
            link(dve.tensor_scalar(den, den, 0.5, None, ALU.max))
            part = C
            for _ in range(2):
                part //= 2
                (n1, n2), (d1, d2) = ((v[:, :, 0:part], v[:, :, part:2 * part]) for v in (num, den))
                link(dve.tensor_tensor(n1, n1, d2, ALU.mult))
                link(dve.tensor_tensor(n2, n2, d1, ALU.mult))
                link(dve.tensor_tensor(n1, n1, n2, ALU.add))
                link(dve.tensor_tensor(d1, d1, d2, ALU.mult))
            num, den = num[:, :, 0:part], den[:, :, 0:part]
            link(dve.reciprocal(den, den))
            link(dve.tensor_tensor(num, num, den, ALU.mult))
            link(dve.tensor_reduce(sum0[:, :, :], num.rearrange("p t (i o) -> p t o i", o=F), AX.X, ALU.add))
            dve.wait_ge(in_x, 32)
            link(dve.tensor_tensor(sum0[:, :, :], sum0[:, :, :], x_sb[:, :, :], ALU.add))

            def layernorm(result, v, square, n, ready):
                link(dve.tensor_reduce(st1[:, :], v[:, :, :], AX.X, ALU.add))
                link(dve.tensor_scalar(st1[:, :], st1[:, :], 1.0 / F, None, ALU.mult))
                link(dve.tensor_tensor(v[:, :, :], v[:, :, :], st1[:, :].unsqueeze(2).to_broadcast([P, NT, F]), ALU.subtract))
                link(dve.tensor_tensor(square[:, :, :], v[:, :, :], v[:, :, :], ALU.mult))
                link(dve.tensor_reduce(st1[:, :], square[:, :, :], AX.X, ALU.add))
                link(dve.tensor_scalar(st1[:, :], st1[:, :], 1.0 / F, EPS, ALU.mult, ALU.add))
                dve.sem_inc(ln_var, 1)
                dve.wait_ge(ln_sd, n)
                link(dve.reciprocal(st2[:, :], st2[:, :]))
                link(dve.tensor_tensor(result[:, :, :], v[:, :, :], st2[:, :].unsqueeze(2).to_broadcast([P, NT, F]), ALU.mult))
                dve.sem_inc(ready, 1)

            layernorm(x1, sum0, square0, 1, x1_ready)

            link(dve.memset(one_col[:, :], 1.0))
            link(dve.memset(ut[:, :, :], 1.0))
            link(dve.tensor_scalar(minus_lo[:, :], lo[:, :], -1.0, None, ALU.mult))
            link(dve.memset(left_any[:, :], 0.0))
            dve.memset(zero_b[:, :], 0.0).then_inc(zero_ready, 1)
            dve.sem_inc(hot_used, EU)
            dve.sem_inc(left_out, 16)
            dve.sem_inc(left_or, 1)
            hw = dense_windows(dve)

            def keep_left(w, b):
                with dve.If(w < hw):
                    dve.wait_ge(win_ev, w + 1)
                    dve.wait_ge(left_out, w * 16 + 16)
                    dve.wait_ge(left_or, w + 1)
                    dve.nop(nofuse=True)
                    dve.tensor_tensor(left[:, :].rearrange("p (n h) -> p n h", h=NT),
                                      bank[b][:, 0:CW].rearrange("p (n h) -> p n h", h=NT),
                                      cnt[:, :, bass.ds(w * WIN, WIN)].rearrange("p h n -> p n h"), ALU.subtract).then_inc(left_ready, 1)
                    dve.wait_ge(left_ready, w + 1)
                    dve.scalar_tensor_tensor(out=left_any[:, :], in0=left[:, :], scalar=0.0, in1=left_any[:, :],
                                             op0=ALU.not_equal, op1=ALU.max).then_inc(left_or, 1)
                dve.sem_inc(left_past, 1)

            def windows(v, units, dense, first=False):
                for b in range(WG):
                    w = WG * v + b
                    with dve.Fori(units[b], units[b + 1] + 1) as i:
                        for q in range(EU):
                            dve.wait_ge(hot_used, EU * (i + w) + q + 1)
                            dve.nop(nofuse=True)
                            if q == 0:
                                dve.tensor_scalar(hot_lo[:, 0, :], iota_lo[:, :], minus_lo[:, bass.ds(EU * i, 1)], 0.0,
                                                  ALU.add, ALU.is_equal)
                            dve.tensor_scalar(hot_key[:, q, :], iota_key[:, :], w500[:, bass.ds(w, 1)],
                                              kb[:, bass.ds(EU * i + q, 1)], ALU.add, ALU.is_equal).then_inc(hot_ready, 1)
                    if b == 0 and not first or b > 0 and dense:
                        keep_left(w - 1, (b + 3) % 4)
                    if b == 0 and not dense:
                        dve.sem_inc(left_past, WG - 1)

            windows(0, window_units(mybir.EngineType.DVE, 0), True, True)
            with dve.Fori(1, NW // WG) as v:
                units = window_units(mybir.EngineType.DVE, v)
                with dve.If(WG * v >= hw):
                    windows(v, units, False)
                with dve.If(WG * v < hw):
                    windows(v, units, True)
            keep_left(NW - 1, 3)
            dve.wait_ge(left_or, hw + 1)
            dve.tensor_reduce(left_p[:, :], left_any[:, :], AX.X, ALU.max).then_inc(any_ready, 1)
            dve.wait_ge(any_turned, 1)
            link(dve.tensor_reduce(left_1[:, :], bank[6][0:1, 0:P], AX.X, ALU.max))
            dve.tensor_copy(flag[:, :], left_1[:, :]).then_inc(flag_ready, 1)
            dve.wait_ge(flag_ready, 1)
            some = dve.value_load(flag[0:1, 0:1], min_val=0, max_val=1)

            def add_left(c):
                with dve.If(some == 1):
                    with dve.Fori(0, hw) as w:
                        dve.wait_ge(left_ps, hw * c + w + 1)
                        dve.tensor_copy(left_sums[:, :], bank[6][0:3 * F, 0:WIN]).then_inc(left_kept, 1)
                    for q, (n0, n) in enumerate(BLOCKS):
                        k = c * NB + q
                        dve.wait_ge(conv_ev, k + 1)
                        dve.wait_ge(extra_in, 16 * (k + 1))
                        dve.tensor_tensor(agg[:, k % 2, 0:n], agg[:, k % 2, 0:n], extra[:, 0:n], ALU.add).then_inc(agg_ready, 1)
                with dve.If(some == 0):
                    dve.sem_inc(agg_ready, NB)

            dve.wait_ge(win_ev, NW)
            dve.wait_ge(gin_in, 16 * 16)
            link(dve.tensor_scalar(geps[:, :], geps[:, :], 1.0, None, ALU.add))
            for c in range(2):
                link(dve.tensor_scalar(gwe[:, c, :], gwe[:, c, :], geps[:, c:c + 1], None, ALU.mult))
            hps = bank[7][:, 0:NT * F].rearrange("p (t f) -> p t f", f=F)
            for c, feat in enumerate((x1, hn)):
                link(dve.tensor_copy(xs[:, :, 0, :], feat[:, :, :]))
                link(dve.tensor_tensor(xr[:, :, :], feat[:, :, :], xs[:, :, 0, :], ALU.subtract))
                link(dve.tensor_copy(xs[:, :, 1, :], xr[:, :, :]))
                dve.tensor_tensor(xs[:, :, 2, :], xr[:, :, :], xs[:, :, 1, :], ALU.subtract).then_inc(xs_ready, 1)
                add_left(c)
                dve.wait_ge(map2, (c + 1) * NB)
                if c == 0:
                    link(dve.tensor_scalar(hn[:, :, :], hps, 0.0, None, ALU.max))
            link(dve.tensor_copy(hn2[:, :, :], hps))
            link(dve.tensor_reduce(st1[:, :], hn2[:, :, :], AX.X, ALU.max))
            dve.tensor_tensor(hn2[:, :, :], hn2[:, :, :], st1[:, :].unsqueeze(2).to_broadcast([P, NT, F]),
                              ALU.subtract).then_inc(lsm_e, 1)
            dve.wait_ge(lsm_s, 1)
            dve.tensor_reduce(st1[:, :], hn[:, :, :], AX.X, ALU.add).then_inc(lsm_e, 1)
            dve.wait_ge(lsm_l, 1)
            link(dve.tensor_tensor(hn2[:, :, :], hn2[:, :, :], st2[:, :].unsqueeze(2).to_broadcast([P, NT, F]), ALU.subtract))
            link(dve.tensor_tensor(hn2[:, :, :], hn2[:, :, :], x1[:, :, :], ALU.add))
            layernorm(hn, hn2, hn, 2, y_ready)


def kernel(**inputs):
    import numpy as np
    import concourse.bacc as bacc
    from concourse.bass_utils import run_bass_kernel_spmd

    nc = bacc.Bacc("TRN2", target_bir_lowering=False, num_devices=1)
    arrays, a = {}, {}
    for name, value in inputs.items():
        v = np.ascontiguousarray(value)
        if v.ndim == 0:
            v = v.reshape(1)
        arrays[f"in_{name}"] = v
        a[name] = nc.dram_tensor(f"in_{name}", v.shape, mybir.dt.from_np(v.dtype), kind="ExternalInput").ap()
    out = nc.dram_tensor("out_0", (N, F), F32, kind="ExternalOutput").ap()
    gin = [tuple(a[f"L1_gnn_{k}"] for k in (f"w{c}a", f"b{c}a", f"w{c}b", f"b{c}b", f"eps{c}")) for c in (1, 2)]
    program(nc, a["x"], a["src"], a["dst"], a["edge_attr_16"], a["L0_gnn_W_msg"], a["L0_gnn_b_msg"],
            a["L0_gnn_W_attn"], a["L0_gnn_b_attn"], gin, out)
    r = run_bass_kernel_spmd(nc, [arrays], core_ids=[0])
    return r.results[0]["out_0"]
```
